# Optimizing a Trainium2 kernel written in Bass

```python
import numpy as np
import jax
import jax.numpy as jnp

def _softmax(x, axis=-1):
    return jax.nn.softmax(x, axis=axis)

def _gelu(x):
    return jax.nn.gelu(x, approximate=True)

def _silu(x):
    return jax.nn.silu(x)

def _sigmoid(x):
    return jax.nn.sigmoid(x)

def _layernorm(x, axis=-1, eps=1e-05):
    m = jnp.mean(x, axis=axis, keepdims=True)
    v = jnp.var(x, axis=axis, keepdims=True)
    return (x - m) / jnp.sqrt(v + eps)

def _scatter_add(tgt, idx, src, axis=0):
    return tgt.at[idx].add(src)

def _segment_sum(src, seg, n):
    return jax.ops.segment_sum(src, seg, n)
kernel_name = 'mk_hybrid_d2_jaxref_r8_b9fbe5'

def setup_inputs(seed: int=0):
    np.random.seed(seed)
    _w = jnp.asarray

    def _L0_attn_a_setup():
        import jax, jax.numpy as jnp
        import numpy as np
        COSINE_SIM_SCALE = 8.0
        LN_EPS = 1e-05
        HEADS = 8

        def _l2norm(t, eps=1e-12):
            return t * jax.lax.rsqrt(jnp.sum(t * t, axis=-1, keepdims=True) + eps)
        key = jax.random.key(seed)
        k1, k2, k3 = jax.random.split(key, 3)
        b, n, dim = (2, 256, 128)
        inner = 64
        return {'x': jax.random.normal(k1, (b, n, dim), dtype=jnp.float32), 'ln_w': jnp.ones((dim,), dtype=jnp.float32), 'ln_b': jnp.zeros((dim,), dtype=jnp.float32), 'w_qkv': jax.random.normal(k2, (dim, 3 * inner), dtype=jnp.float32) * 0.02, 'w_out': jax.random.normal(k3, (inner, dim), dtype=jnp.float32) * 0.02}
    _L0_attn_a_in = _L0_attn_a_setup()

    def _L0_attn_b_setup():
        import jax, jax.numpy as jnp
        import numpy as np
        EPS = 1e-06

        def rmsnorm(x, w):
            x32 = x.astype(jnp.float32)
            y = x32 * jax.lax.rsqrt(jnp.mean(x32 * x32, axis=-1, keepdims=True) + EPS)
            return y.astype(x.dtype) * w

        def _scan_combine(c1, c2):
            a1, x1 = c1
            a2, x2 = c2
            return (a1 * a2, a2 * x1 + x2)

        def _reference_tuple_inner(inp, Wg, Wc, w1, w2, w3, ln_w, ffn_w):
            norm_inp = rmsnorm(inp, ln_w)
            beta = jax.nn.sigmoid(jnp.einsum('bld,ed->ble', norm_inp, Wg))
            hx_hat = jnp.einsum('bld,ed->ble', norm_inp, Wc)
            a = 1.0 - beta
            x = beta * hx_hat
            _, hx_next = jax.lax.associative_scan(_scan_combine, (a, x), axis=1)
            h_norm = rmsnorm(hx_next, ffn_w)
            ff = jnp.einsum('blh,dh->bld', jax.nn.silu(jnp.einsum('bld,hd->blh', h_norm, w1)) * jnp.einsum('bld,hd->blh', h_norm, w3), w2)
            out = hx_next + ff
            return (out, hx_next)
        B, L, D = (4, 1024, 128)
        key = jax.random.key(seed)
        ks = jax.random.split(key, 6)
        s = 1.0 / np.sqrt(D)
        inp = jax.random.normal(ks[0], (B, L, D), dtype=jnp.float32)
        Wg = jax.random.uniform(ks[1], (D, D), jnp.float32, -s, s)
        Wc = jax.random.uniform(ks[2], (D, D), jnp.float32, -s, s)
        w1 = jax.random.uniform(ks[3], (D, D), jnp.float32, -s, s)
        w2 = jax.random.uniform(ks[4], (D, D), jnp.float32, -s, s)
        w3 = jax.random.uniform(ks[5], (D, D), jnp.float32, -s, s)
        ln_w = jnp.ones((D,), jnp.float32)
        ffn_w = jnp.ones((D,), jnp.float32)
        return {'inp': inp, 'Wg': Wg, 'Wc': Wc, 'w1': w1, 'w2': w2, 'w3': w3, 'ln_w': ln_w, 'ffn_w': ffn_w}
    _L0_attn_b_in = _L0_attn_b_setup()

    def _L0_ffn_setup():
        import jax, jax.numpy as jnp
        import numpy as np
        NUM_EXPERTS = 160
        TOP_K = 8
        ROUTED_SCALE = 2.5
        HIDDEN = 128
        INTER = 64
        key = jax.random.key(seed)
        ks = jax.random.split(key, 7)
        B, S = (1, 256)
        return {'hidden_states': jax.random.normal(ks[0], (B, S, HIDDEN), dtype=jnp.float32), 'router_w': jax.random.normal(ks[1], (NUM_EXPERTS, HIDDEN), dtype=jnp.float32) * 0.02, 'expert_bias': jnp.zeros((NUM_EXPERTS,), dtype=jnp.float32), 'w_gate': jax.random.normal(ks[2], (NUM_EXPERTS, INTER, HIDDEN), dtype=jnp.float32) * 0.02, 'w_down': jax.random.normal(ks[3], (NUM_EXPERTS, HIDDEN, INTER), dtype=jnp.float32) * 0.02, 'w_gate_shared': jax.random.normal(ks[4], (INTER, HIDDEN), dtype=jnp.float32) * 0.02, 'w_down_shared': jax.random.normal(ks[5], (HIDDEN, INTER), dtype=jnp.float32) * 0.02}
    _L0_ffn_in = _L0_ffn_setup()

    def _L1_attn_a_setup():
        import jax, jax.numpy as jnp
        import numpy as np
        D_MODEL = 128
        D_STATE = 16
        D_CONV = 4
        EXPAND = 2
        E = EXPAND * D_MODEL
        B, L = (4, 512)
        key = jax.random.key(seed)
        ks = jax.random.split(key, 8)
        x = jax.random.normal(ks[0], (B, L, D_MODEL), dtype=jnp.float32)
        W_in = jax.random.normal(ks[1], (D_MODEL, 2 * E), dtype=jnp.float32) * 0.02
        b_in = jnp.zeros((2 * E,), dtype=jnp.float32)
        conv_w = jax.random.normal(ks[2], (E, 1, D_CONV), dtype=jnp.float32) * 0.1
        conv_b = jnp.zeros((E,), dtype=jnp.float32)
        A = jax.random.normal(ks[3], (E, D_STATE), dtype=jnp.float32) * 0.01
        C = jax.random.normal(ks[4], (E, D_STATE), dtype=jnp.float32) * 0.01
        Dp = jnp.ones((E,), dtype=jnp.float32) * 0.01
        W_out = jax.random.normal(ks[5], (E, D_MODEL), dtype=jnp.float32) * 0.02
        b_out = jnp.zeros((D_MODEL,), dtype=jnp.float32)
        return {'x': x, 'W_in': W_in, 'b_in': b_in, 'conv_w': conv_w, 'conv_b': conv_b, 'A': A, 'C': C, 'Dp': Dp, 'W_out': W_out, 'b_out': b_out}
    _L1_attn_a_in = _L1_attn_a_setup()

    def _L1_attn_b_setup():
        import jax, jax.numpy as jnp
        import numpy as np
        import math
        D_MODEL = 128
        NUM_HEADS = 16
        THETA = 10000.0

        def _rope(x, theta):
            n, d_k = (x.shape[-2], x.shape[-1])
            powers = jnp.arange(0, d_k, 2, dtype=jnp.float32) / d_k
            freqs = 1.0 / theta ** powers
            t = jnp.arange(n, dtype=jnp.float32)
            angles = jnp.outer(t, freqs)
            cos = jnp.cos(angles).astype(x.dtype)
            sin = jnp.sin(angles).astype(x.dtype)
            x_even = x[..., 0::2]
            x_odd = x[..., 1::2]
            rot_even = x_even * cos - x_odd * sin
            rot_odd = x_even * sin + x_odd * cos
            return jnp.stack([rot_even, rot_odd], axis=-1).reshape(x.shape)
        key = jax.random.key(seed)
        ks = jax.random.split(key, 5)
        B, N, D = (2, 256, D_MODEL)
        std = math.sqrt(2.0 / (D + D))
        x = jax.random.normal(ks[0], (B, N, D), dtype=jnp.float32)
        wq = jax.random.normal(ks[1], (D, D), dtype=jnp.float32) * std
        wk = jax.random.normal(ks[2], (D, D), dtype=jnp.float32) * std
        wv = jax.random.normal(ks[3], (D, D), dtype=jnp.float32) * std
        wo = jax.random.normal(ks[4], (D, D), dtype=jnp.float32) * std
        return {'x': x, 'wq': wq, 'wk': wk, 'wv': wv, 'wo': wo}
    _L1_attn_b_in = _L1_attn_b_setup()

    def _L1_ffn_setup():
        import jax, jax.numpy as jnp
        import numpy as np
        DIM = 128

        def _reference_tuple_inner(x, W_r, W_k, W_v, mu_r, mu_k):
            B, T, C = x.shape
            x_prev = jnp.concatenate([jnp.zeros((B, 1, C), x.dtype), x[:, :-1, :]], axis=1)
            xr = mu_r * x + (1.0 - mu_r) * x_prev
            xk = mu_k * x + (1.0 - mu_k) * x_prev
            r = jax.nn.sigmoid(jnp.einsum('btc,dc->btd', xr, W_r))
            k = jnp.einsum('btc,dc->btd', xk, W_k)
            k_act = jnp.square(jax.nn.relu(k))
            out = r * jnp.einsum('btc,dc->btd', k_act, W_v)
            new_state = x[:, -1, :]
            return (out, new_state)
        key = jax.random.key(seed)
        ks = jax.random.split(key, 6)
        B, T, C = (8, 256, DIM)
        x = jax.random.normal(ks[0], (B, T, C), dtype=jnp.float32)
        s = 1.0 / np.sqrt(C)
        W_r = jax.random.uniform(ks[1], (C, C), jnp.float32, -s, s)
        W_k = jax.random.uniform(ks[2], (C, C), jnp.float32, -s, s)
        W_v = jax.random.uniform(ks[3], (C, C), jnp.float32, -s, s)
        mu_r = jax.random.uniform(ks[4], (C,), jnp.float32)
        mu_k = jax.random.uniform(ks[5], (C,), jnp.float32)
        return {'x': x, 'W_r': W_r, 'W_k': W_k, 'W_v': W_v, 'mu_r': mu_r, 'mu_k': mu_k}
    _L1_ffn_in = _L1_ffn_setup()
    _d = {'L0_attn_a_x': _L0_attn_a_in['x'], 'L0_attn_a_ln_w': _L0_attn_a_in['ln_w'], 'L0_attn_a_ln_b': _L0_attn_a_in['ln_b'], 'L0_attn_a_w_qkv': _L0_attn_a_in['w_qkv'], 'L0_attn_a_w_out': _L0_attn_a_in['w_out'], 'L0_attn_b_Wg': _L0_attn_b_in['Wg'], 'L0_attn_b_Wc': _L0_attn_b_in['Wc'], 'L0_attn_b_w1': _L0_attn_b_in['w1'], 'L0_attn_b_w2': _L0_attn_b_in['w2'], 'L0_attn_b_w3': _L0_attn_b_in['w3'], 'L0_attn_b_ln_w': _L0_attn_b_in['ln_w'], 'L0_attn_b_ffn_w': _L0_attn_b_in['ffn_w'], 'L0_ffn_router_w': _L0_ffn_in['router_w'], 'L0_ffn_expert_bias': _L0_ffn_in['expert_bias'], 'L0_ffn_w_gate': _L0_ffn_in['w_gate'], 'L0_ffn_w_down': _L0_ffn_in['w_down'], 'L0_ffn_w_gate_shared': _L0_ffn_in['w_gate_shared'], 'L0_ffn_w_down_shared': _L0_ffn_in['w_down_shared'], 'L1_attn_a_W_in': _L1_attn_a_in['W_in'], 'L1_attn_a_b_in': _L1_attn_a_in['b_in'], 'L1_attn_a_conv_w': _L1_attn_a_in['conv_w'], 'L1_attn_a_conv_b': _L1_attn_a_in['conv_b'], 'L1_attn_a_A': _L1_attn_a_in['A'], 'L1_attn_a_C': _L1_attn_a_in['C'], 'L1_attn_a_Dp': _L1_attn_a_in['Dp'], 'L1_attn_a_W_out': _L1_attn_a_in['W_out'], 'L1_attn_a_b_out': _L1_attn_a_in['b_out'], 'L1_attn_b_wq': _L1_attn_b_in['wq'], 'L1_attn_b_wk': _L1_attn_b_in['wk'], 'L1_attn_b_wv': _L1_attn_b_in['wv'], 'L1_attn_b_wo': _L1_attn_b_in['wo'], 'L1_ffn_W_r': _L1_ffn_in['W_r'], 'L1_ffn_W_k': _L1_ffn_in['W_k'], 'L1_ffn_W_v': _L1_ffn_in['W_v'], 'L1_ffn_mu_r': _L1_ffn_in['mu_r'], 'L1_ffn_mu_k': _L1_ffn_in['mu_k']}
    _x0 = _d['L0_attn_a_x']
    _d['L0_attn_a_x'] = jax.random.normal(jax.random.fold_in(jax.random.key(seed), 1), (16, 256, 128), dtype=_x0.dtype)
    del _x0
    return _d

def reference(L0_attn_a_x, L0_attn_a_ln_w, L0_attn_a_ln_b, L0_attn_a_w_qkv, L0_attn_a_w_out, L0_attn_b_Wg, L0_attn_b_Wc, L0_attn_b_w1, L0_attn_b_w2, L0_attn_b_w3, L0_attn_b_ln_w, L0_attn_b_ffn_w, L0_ffn_router_w, L0_ffn_expert_bias, L0_ffn_w_gate, L0_ffn_w_down, L0_ffn_w_gate_shared, L0_ffn_w_down_shared, L1_attn_a_W_in, L1_attn_a_b_in, L1_attn_a_conv_w, L1_attn_a_conv_b, L1_attn_a_A, L1_attn_a_C, L1_attn_a_Dp, L1_attn_a_W_out, L1_attn_a_b_out, L1_attn_b_wq, L1_attn_b_wk, L1_attn_b_wv, L1_attn_b_wo, L1_ffn_W_r, L1_ffn_W_k, L1_ffn_W_v, L1_ffn_mu_r, L1_ffn_mu_k):

    def _L0_attn_a_ref(x, ln_w, ln_b, w_qkv, w_out):
        import jax, jax.numpy as jnp
        import numpy as np
        COSINE_SIM_SCALE = 8.0
        LN_EPS = 1e-05
        HEADS = 8

        def _l2norm(t, eps=1e-12):
            return t * jax.lax.rsqrt(jnp.sum(t * t, axis=-1, keepdims=True) + eps)
        b, n, dim = x.shape
        h = HEADS
        mu = jnp.mean(x, axis=-1, keepdims=True)
        var = jnp.mean(jnp.square(x - mu), axis=-1, keepdims=True)
        xn = (x - mu) * jax.lax.rsqrt(var + LN_EPS) * ln_w + ln_b
        qkv = xn @ w_qkv
        q, k, v = jnp.split(qkv, 3, axis=-1)

        def to_heads(t):
            return t.reshape(b, n, h, -1).transpose(0, 2, 1, 3)
        q, k, v = map(to_heads, (q, k, v))
        q = _l2norm(q)
        k = _l2norm(k)
        sim = jnp.einsum('bhid,bhjd->bhij', q, k) * COSINE_SIM_SCALE
        causal_mask = jnp.tril(jnp.ones((n, n), dtype=bool))
        sim = jnp.where(causal_mask, sim, jnp.finfo(sim.dtype).min)
        attn = jax.nn.softmax(sim, axis=-1)
        o = jnp.einsum('bhij,bhjd->bhid', attn, v)
        o = o.transpose(0, 2, 1, 3).reshape(b, n, -1)
        return o @ w_out

    def _L0_attn_b_ref(inp, Wg, Wc, w1, w2, w3, ln_w, ffn_w):
        import jax, jax.numpy as jnp
        import numpy as np
        EPS = 1e-06

        def rmsnorm(x, w):
            x32 = x.astype(jnp.float32)
            y = x32 * jax.lax.rsqrt(jnp.mean(x32 * x32, axis=-1, keepdims=True) + EPS)
            return y.astype(x.dtype) * w

        def _scan_combine(c1, c2):
            a1, x1 = c1
            a2, x2 = c2
            return (a1 * a2, a2 * x1 + x2)

        def _reference_tuple_inner(inp, Wg, Wc, w1, w2, w3, ln_w, ffn_w):
            norm_inp = rmsnorm(inp, ln_w)
            beta = jax.nn.sigmoid(jnp.einsum('bld,ed->ble', norm_inp, Wg))
            hx_hat = jnp.einsum('bld,ed->ble', norm_inp, Wc)
            a = 1.0 - beta
            x = beta * hx_hat
            _, hx_next = jax.lax.associative_scan(_scan_combine, (a, x), axis=1)
            h_norm = rmsnorm(hx_next, ffn_w)
            ff = jnp.einsum('blh,dh->bld', jax.nn.silu(jnp.einsum('bld,hd->blh', h_norm, w1)) * jnp.einsum('bld,hd->blh', h_norm, w3), w2)
            out = hx_next + ff
            return (out, hx_next)
        return _reference_tuple_inner(inp, Wg, Wc, w1, w2, w3, ln_w, ffn_w)[0]

    def _L0_ffn_ref(hidden_states, router_w, expert_bias, w_gate, w_down, w_gate_shared, w_down_shared):
        import jax, jax.numpy as jnp
        import numpy as np
        NUM_EXPERTS = 160
        TOP_K = 8
        ROUTED_SCALE = 2.5
        HIDDEN = 128
        INTER = 64
        B, S, H = hidden_states.shape
        x = hidden_states.reshape(-1, H)
        T = x.shape[0]
        logits = x @ router_w.T + expert_bias[None, :]
        probs = jax.nn.sigmoid(logits)
        top_w, top_idx = jax.lax.top_k(probs, TOP_K)
        top_w = top_w / (jnp.sum(top_w, axis=-1, keepdims=True) + 1e-09)
        top_w = top_w * ROUTED_SCALE
        combine = jnp.zeros((T, NUM_EXPERTS), dtype=x.dtype)
        combine = combine.at[jnp.arange(T)[:, None], top_idx].set(top_w)
        h1 = jax.nn.silu(jnp.einsum('th,eih->eti', x, w_gate))
        h1w = h1 * combine.T[:, :, None]
        routed = jnp.einsum('eti,ehi->th', h1w, w_down)
        shared = jax.nn.silu(x @ w_gate_shared.T) @ w_down_shared.T
        return (routed + shared).reshape(B, S, H)

    def _L1_attn_a_ref(x, W_in, b_in, conv_w, conv_b, A, C, Dp, W_out, b_out):
        import jax, jax.numpy as jnp
        import numpy as np
        D_MODEL = 128
        D_STATE = 16
        D_CONV = 4
        EXPAND = 2
        E = EXPAND * D_MODEL
        B, L = (4, 512)
        Bb, Ll, _ = x.shape
        x_and_z = x @ W_in + b_in
        x_proj, z = jnp.split(x_and_z, 2, axis=-1)
        xc = jnp.transpose(x_proj, (0, 2, 1))
        xc = jax.lax.conv_general_dilated(xc, conv_w, window_strides=(1,), padding=[(D_CONV - 1, 0)], dimension_numbers=('NCH', 'OIH', 'NCH'), feature_group_count=E)
        x_conv = jnp.transpose(xc + conv_b[None, :, None], (0, 2, 1))

        def step(h, xt):
            h = jnp.tanh(xt @ A + h)
            yt = h @ C.T + Dp * xt
            return (h, yt)
        h0 = jnp.zeros((Bb, D_STATE), dtype=x.dtype)
        _, ys = jax.lax.scan(step, h0, jnp.transpose(x_conv, (1, 0, 2)))
        x_s4 = jnp.transpose(ys, (1, 0, 2))
        y = jax.nn.sigmoid(z) * x_s4
        return y @ W_out + b_out

    def _L1_attn_b_ref(x, wq, wk, wv, wo):
        import jax, jax.numpy as jnp
        import numpy as np
        import math
        D_MODEL = 128
        NUM_HEADS = 16
        THETA = 10000.0

        def _rope(x, theta):
            n, d_k = (x.shape[-2], x.shape[-1])
            powers = jnp.arange(0, d_k, 2, dtype=jnp.float32) / d_k
            freqs = 1.0 / theta ** powers
            t = jnp.arange(n, dtype=jnp.float32)
            angles = jnp.outer(t, freqs)
            cos = jnp.cos(angles).astype(x.dtype)
            sin = jnp.sin(angles).astype(x.dtype)
            x_even = x[..., 0::2]
            x_odd = x[..., 1::2]
            rot_even = x_even * cos - x_odd * sin
            rot_odd = x_even * sin + x_odd * cos
            return jnp.stack([rot_even, rot_odd], axis=-1).reshape(x.shape)
        B, N, D = x.shape
        H = NUM_HEADS
        d_k = D // H

        def split_heads(t):
            return t.reshape(B, N, H, d_k).transpose(0, 2, 1, 3)
        Q = split_heads(x @ wq.T)
        K = split_heads(x @ wk.T)
        V = split_heads(x @ wv.T)
        Q = _rope(Q, THETA)
        K = _rope(K, THETA)
        scale = 1.0 / math.sqrt(d_k)
        scores = jnp.einsum('bhqd,bhkd->bhqk', Q, K) * scale
        causal_mask = jnp.triu(jnp.ones((N, N), dtype=bool), k=1)
        scores = jnp.where(causal_mask, -jnp.inf, scores)
        attn = jax.nn.softmax(scores, axis=-1)
        out = jnp.einsum('bhqk,bhkd->bhqd', attn, V)
        out = out.transpose(0, 2, 1, 3).reshape(B, N, D)
        return out @ wo.T

    def _L1_ffn_ref(x, W_r, W_k, W_v, mu_r, mu_k):
        import jax, jax.numpy as jnp
        import numpy as np
        DIM = 128

        def _reference_tuple_inner(x, W_r, W_k, W_v, mu_r, mu_k):
            B, T, C = x.shape
            x_prev = jnp.concatenate([jnp.zeros((B, 1, C), x.dtype), x[:, :-1, :]], axis=1)
            xr = mu_r * x + (1.0 - mu_r) * x_prev
            xk = mu_k * x + (1.0 - mu_k) * x_prev
            r = jax.nn.sigmoid(jnp.einsum('btc,dc->btd', xr, W_r))
            k = jnp.einsum('btc,dc->btd', xk, W_k)
            k_act = jnp.square(jax.nn.relu(k))
            out = r * jnp.einsum('btc,dc->btd', k_act, W_v)
            new_state = x[:, -1, :]
            return (out, new_state)
        return _reference_tuple_inner(x, W_r, W_k, W_v, mu_r, mu_k)[0]
    x = L0_attn_a_x
    x = x + _L0_attn_a_ref(_layernorm(x, axis=-1), L0_attn_a_ln_w, L0_attn_a_ln_b, L0_attn_a_w_qkv, L0_attn_a_w_out)
    x = x + _L0_ffn_ref(_layernorm(x, axis=-1), L0_ffn_router_w, L0_ffn_expert_bias, L0_ffn_w_gate, L0_ffn_w_down, L0_ffn_w_gate_shared, L0_ffn_w_down_shared)
    x = x + _L0_attn_b_ref(_layernorm(x, axis=-1), L0_attn_b_Wg, L0_attn_b_Wc, L0_attn_b_w1, L0_attn_b_w2, L0_attn_b_w3, L0_attn_b_ln_w, L0_attn_b_ffn_w)
    x = x + _L0_ffn_ref(_layernorm(x, axis=-1), L0_ffn_router_w, L0_ffn_expert_bias, L0_ffn_w_gate, L0_ffn_w_down, L0_ffn_w_gate_shared, L0_ffn_w_down_shared)
    x = x + _L1_attn_a_ref(_layernorm(x, axis=-1), L1_attn_a_W_in, L1_attn_a_b_in, L1_attn_a_conv_w, L1_attn_a_conv_b, L1_attn_a_A, L1_attn_a_C, L1_attn_a_Dp, L1_attn_a_W_out, L1_attn_a_b_out)
    x = x + _L1_ffn_ref(_layernorm(x, axis=-1), L1_ffn_W_r, L1_ffn_W_k, L1_ffn_W_v, L1_ffn_mu_r, L1_ffn_mu_k)
    x = x + _L1_attn_b_ref(_layernorm(x, axis=-1), L1_attn_b_wq, L1_attn_b_wk, L1_attn_b_wv, L1_attn_b_wo)
    x = x + _L1_ffn_ref(_layernorm(x, axis=-1), L1_ffn_W_r, L1_ffn_W_k, L1_ffn_W_v, L1_ffn_mu_r, L1_ffn_mu_k)
    return x

_drawn_inputs = setup_inputs


def setup_inputs(seed=0):
    import zlib

    import numpy as np

    out = dict(_drawn_inputs(seed))
    spreads = {'L0_attn_a_ln_w': (1.0, 0.6),
     'L0_attn_a_ln_b': (0.0, 0.8),
     'L0_attn_b_ln_w': (1.0, 0.2),
     'L0_attn_b_ffn_w': (1.0, 0.2),
     'L0_ffn_expert_bias': (0.0, 0.344),
     'L1_attn_a_b_in': (0.0, 0.8),
     'L1_attn_a_conv_b': (0.0, 0.8),
     'L1_attn_a_Dp': (0.009999999776482582, 0.6),
     'L1_attn_a_b_out': (0.0, 0.1)}
    factors = {'L0_attn_a_w_out': 2.749,
     'L1_attn_a_W_in': 8.0,
     'L1_attn_a_conv_w': 8.0,
     'L1_attn_a_A': 8.0,
     'L1_attn_a_C': 8.0,
     'L1_attn_a_W_out': 8.0,
     'L1_ffn_mu_r': 3.521}
    for name, (base, spread) in spreads.items():
        noise = np.random.default_rng([zlib.crc32(name.encode()), seed]).standard_normal(out[name].shape)
        drawn = base * np.exp(spread * noise) if base else spread * noise
        out[name] = jnp.asarray(drawn.astype(out[name].dtype))
    for name, factor in factors.items():
        out[name] = (out[name] * factor).astype(out[name].dtype)
    return out
```

```python
from contextlib import ExitStack

import concourse.bass as bass
from concourse import mybir

F32 = mybir.dt.float32
BF16 = mybir.dt.bfloat16
I32 = mybir.dt.int32
ACT = mybir.ActivationFunctionType
ALU = mybir.AluOpType
AX = mybir.AxisListType

P = 128
D = 128
SEQ = 256
NSEQ = 16
TOK = NSEQ * SEQ
TILES = TOK // P
TPI = 4
STEPS = TILES // TPI
W = TPI * P
EPS = 1e-5
DH = 8
SPLIT = 6 * DH
HROWS = 64
NEG = -1.0e30


START = 2


class Signal:

    def __init__(self, nc, ctx, name, per=1, steps=STEPS):
        self.sem = ctx.enter_context(nc.semaphore(name))
        self.per, self.steps = per, steps

    def at(self, run, i, c=None):
        return i * self.per + (START + run * self.steps * self.per + (self.per if c is None else c))

    def before(self, run, i):
        return self.at(run, i, 0)

    def end(self, run):
        return START + (run + 1) * self.steps * self.per


LAYERS = ("cos", "moe", "glru", "moe", "mamba", "ffn", "rope", "ffn")


def program(nc, a):
    ctx = ExitStack()
    with ctx:
        def sb(name, shape, dt=F32):
            return ctx.enter_context(nc.sbuf_tensor(name, shape, dt))

        signals = []

        def signal(name, per=1, steps=STEPS):
            s = Signal(nc, ctx, name, per, steps)
            signals.append(s)
            return s

        def semaphore(name):
            return ctx.enter_context(nc.semaphore(name))

        psum = ctx.enter_context(nc.psum_tensor("psum", [P, 8, 512], F32))

        X = sb("X", [P, TILES, D])
        ident = sb("ident", [P, P])
        identb = sb("identb", [P, P], BF16)
        mask_kq = sb("mask_kq", [P, P], BF16)
        mask_qk = sb("mask_qk", [P, P], BF16)
        ones4 = sb("ones4", [P, 4, 32])
        tiny = sb("tiny", [P, 1])
        rms_eps = sb("rms_eps", [P, 1])
        ones = sb("ones", [P, P])
        minus_half = sb("minus_half", [P, 64])
        ARENA = 40704
        arena = sb("arena", [P, ARENA])
        used = [0]

        def view(shape, dt=F32, at=None):
            n = 1
            for k in shape[1:]:
                n *= k
            words = n if dt in (F32, I32) else (n + 1) // 2
            o = used[0] if at is None else at
            used[0] = o + words
            assert used[0] <= ARENA, used[0]
            v = arena[0:shape[0], o:o + words]
            if dt != F32:
                v = v.bitcast(dt)
            if len(shape) > 2:
                names = [f"d{k}" for k in range(len(shape) - 1)]
                v = v.rearrange("p (" + " ".join(names) + ") -> p " + " ".join(names),
                                **{m: k for m, k in zip(names[1:], shape[2:])})
            return v

        stats = sb("stats", [P, TPI, 6])
        mv = sb("mv", [P, TPI, 2])
        rstd = sb("rstd", [P, TPI])
        rstd2 = sb("rstd2", [P, TPI])
        XN = sb("XN", [P, TPI, D])
        XT = sb("XT", [P, W])

        loaded = semaphore("loaded")
        stored = semaphore("stored")
        constants = semaphore("constants")
        primed = semaphore("primed")
        stood = semaphore("stood")
        phase_done = semaphore("phase_done")

        weights = []

        def weight(name, shape, dt=F32, src=None):
            t = sb("w_" + name, shape, dt)
            weights.append((t, a[name] if src is None else src))
            return t

        w_qkv = weight("w_qkv", [D, 192])
        ln_w = weight("ln_w", [D, 1])
        ln_b = weight("ln_b", [D, 1])
        w_out = weight("w_out", [P, 2, D])
        for t, n in ((ident, "ident"), (identb, "identb"), (mask_kq, "mask_kq"), (mask_qk, "mask_qk")):
            weights.append((t, a[n]))

        class Order:

            def __init__(self, sig, run, i):
                self.sem, self.sig, self.run, self.i, self.c = sig.sem, sig, run, i, 0

            def one(self):
                self.c += 1
                return 1

            def so_far(self):
                return self.sig.at(self.run, self.i, self.c)

            def close(self):
                assert self.c == self.sig.per, (self.c, self.sig.per)

        def stand(eng):
            eng.sem_inc(stood, 1)

        def layernorm(dve, link, i, ready, run, have_mv, have_rstd, second=None, rr=None):
            for j in range(TPI):
                dve.bn_stats(stats[:, j, :], X[:, bass.ds(i * TPI + j, 1), :].rearrange("p a d -> p (a d)")).then_inc(link.sem, link.one())
            dve.wait_ge(link.sem, link.so_far())
            stand(dve)
            for j in range(TPI):
                ins = dve.bn_aggr(mv[:, j, :], stats[:, j, :])
                if j < TPI - 1:
                    ins.then_inc(link.sem, link.one())
            ins.then_inc(have_mv.sem, 1)
            dve.wait_ge(have_rstd.sem, have_rstd.at(run if rr is None else rr, i))
            scale = rstd if second is None else rstd2
            for j in range(TPI):
                dve.tensor_scalar(XN[:, j, :], X[:, bass.ds(i * TPI + j, 1), :].rearrange("p a d -> p (a d)"),
                                  mv[:, j, 0:1], scale[:, j:j + 1],
                                  ALU.subtract, ALU.mult).then_inc(ready.sem, 1)

        def inverse_deviations(pool, i, run, have_mv, have_rstd, second=None, rr=None):
            rr = run if rr is None else rr
            half = minus_half[:, 0:TPI]

            def done(k):
                pool.wait_ge(have_rstd.sem, have_rstd.at(rr, i, k))
                stand(pool)

            pool.wait_ge(have_mv.sem, have_mv.at(run, i))
            stand(pool)
            pool.tensor_scalar(rstd[:], mv[:, :, 1], EPS, None, ALU.add).then_inc(have_rstd.sem, 1)
            done(1)
            pool.tensor_tensor(rstd[:], rstd[:], half, ALU.pow).then_inc(have_rstd.sem, 1)
            if second is not None:
                done(2)
                pool.tensor_tensor(rstd2[:], rstd[:], rstd[:], ALU.mult).then_inc(have_rstd.sem, 1)
                done(3)
                pool.tensor_tensor(rstd2[:], rstd2[:], mv[:, :, 1], ALU.mult).then_inc(have_rstd.sem, 1)
                done(4)
                pool.tensor_scalar(rstd2[:], rstd2[:], second, None, ALU.add).then_inc(have_rstd.sem, 1)
                done(5)
                pool.tensor_tensor(rstd2[:], rstd2[:], half, ALU.pow).then_inc(have_rstd.sem, 1)
                done(6)
                pool.tensor_tensor(rstd2[:], rstd2[:], rstd[:], ALU.mult).then_inc(have_rstd.sem, 1)

        used[0] = 0
        QKV = view([P, TPI, 192])
        SQ = view([P, TPI, 128])
        SS = view([P, TPI, 16])
        RN = view([P, TPI, 16])
        QN = view([P, 2, TPI, 8, DH])
        R1 = view([P, 64, DH])
        HML = view([P, 64, 3, DH], BF16)
        Qs = view([P, 32, HROWS], BF16)
        Ks = view([P, 32, HROWS], BF16)
        QT = view([P, 2, 4, SEQ], BF16)
        KT = view([P, 2, 4, SEQ], BF16)
        VP = view([P, TPI, 8, 32])
        PR = view([P, 2, 4, 384])
        REC = view([P, SEQ])
        OT = view([P, SEQ])
        a_link = signal("a_link", 14)
        a_mv = signal("a_mv")
        a_rstd = signal("a_rstd", 7)
        a_ss = signal("a_ss")
        a_xn = signal("a_xn", TPI)
        a_xt_ps = signal("a_xt_ps")
        a_xt = signal("a_xt")
        a_qkv_ps = signal("a_qkv_ps")
        a_qkv = signal("a_qkv", 2)
        a_split = signal("a_split")
        a_vp = signal("a_vp", 4)
        a_qrows = signal("a_qrows", 3)
        a_krows = signal("a_krows", 3)
        a_sqrt = signal("a_sqrt")
        a_tr = signal("a_tr", 4)
        a_qt = signal("a_qt", 4)
        a_sc = signal("a_sc", 4)
        a_exp = signal("a_exp", 4)
        a_av = signal("a_av", 4)
        a_rec = signal("a_rec")
        a_ot = signal("a_ot")
        a_y = signal("a_y")
        a_x = signal("a_x")

        def cos_vector(dve, layer):
            with dve.Fori(0, STEPS) as i:
                link = Order(a_link, 0, i)
                dve.wait_ge(a_xt_ps.sem, a_xt_ps.before(0, i))
                layernorm(dve, link, i, a_xn, 0, a_mv, a_rstd, second=EPS)
                dve.wait_ge(a_qkv.sem, a_qkv.at(0, i))
                dve.tensor_tensor(SQ, QKV[:, :, 0:128], QKV[:, :, 0:128], ALU.mult).then_inc(link.sem, link.one())
                dve.wait_ge(link.sem, link.so_far())
                dve.tensor_reduce(SS, SQ.rearrange("p t (h d) -> p t h d", d=DH), AX.X, ALU.add).then_inc(a_ss.sem, 1)
                dve.wait_ge(a_sqrt.sem, a_sqrt.at(0, i))
                dve.reciprocal(RN, RN).then_inc(link.sem, link.one())
                dve.wait_ge(link.sem, link.so_far())
                for s in range(2):
                    dve.tensor_tensor(
                        QN[:, s], QKV[:, :, 64 * s:64 * s + 64].rearrange("p t (h d) -> p t h d", d=DH),
                        RN[:, :, 8 * s:8 * s + 8].unsqueeze(3).broadcast_to([P, TPI, 8, DH]), ALU.mult).then_inc(link.sem, link.one())
                dve.wait_ge(link.sem, link.so_far())
                split3(dve, link, QN.rearrange("p s t h d -> p (s t h) d"), R1, HML, a_split, a_krows, 0, i)
                dve.wait_ge(a_split.sem, a_split.at(0, i))
                dve.wait_ge(a_tr.sem, a_tr.before(0, i))
                query_rows(dve, HML[:, 0:32], Qs, 32, a_qrows)

                def keys(b):
                    dve.wait_ge(a_tr.sem, a_tr.at(0, i, 2 * b + 2))
                    dve.tensor_copy(KT[:, b], psum_b16(2)).then_inc(a_qt.sem, 1)

                keys(0)
                keys(1)
                normalise(dve, 0, i, a_av, a_rec, a_ot)
                dve.wait_ge(a_y.sem, a_y.at(0, i))
                xs = X[:, bass.ds(i * TPI, TPI), :].rearrange("p t d -> p (t d)")
                dve.tensor_tensor(xs, psum[:, 0, :], xs, ALU.add).then_inc(a_x.sem, 1)
                dve.wait_ge(a_x.sem, a_x.at(0, i))
                link.close()

        def normalise(dve, run, n, av, rec, ot):
            dve.wait_ge(av.sem, av.at(run, n))
            dve.reciprocal(REC, psum[:, 3, 256:512]).then_inc(rec.sem, 1)
            dve.wait_ge(rec.sem, rec.at(run, n))
            dve.tensor_tensor(OT, psum[:, 3, 0:256], REC, ALU.mult).then_inc(ot.sem, 1)

        def psum_b16(bank):
            return psum[:, bank, :].bitcast(BF16).rearrange("p (c q) -> p c q", q=SEQ)

        def split3(dve, link, src, rest, parts, done, copied, run, i):
            dve.wait_ge(copied.sem, copied.before(run, i))
            dve.tensor_copy(parts[:, :, 0, :], src).then_inc(link.sem, link.one())
            dve.wait_ge(link.sem, link.so_far())
            dve.tensor_tensor(rest, src, parts[:, :, 0, :], ALU.subtract).then_inc(link.sem, link.one())
            dve.wait_ge(link.sem, link.so_far())
            dve.tensor_copy(parts[:, :, 1, :], rest).then_inc(link.sem, link.one())
            dve.wait_ge(link.sem, link.so_far())
            dve.tensor_tensor(parts[:, :, 2, :], rest, parts[:, :, 1, :], ALU.subtract).then_inc(done.sem, 1)

        def cos_scalar(act, layer):
            with act.Fori(0, STEPS) as i:
                act.wait_ge(a_xt_ps.sem, a_xt_ps.at(0, i))
                act.wait_ge(a_qkv_ps.sem, a_qkv_ps.before(0, i))
                act.activation(XT[:], psum[:, 0, :], ACT.Identity, scale=ln_w[:, 0:1], bias=ln_b[:, 0:1]).then_inc(a_xt.sem, 1)
                act.wait_ge(a_qkv_ps.sem, a_qkv_ps.at(0, i))
                act.wait_ge(a_split.sem, a_split.before(0, i))
                act.wait_ge(a_vp.sem, a_vp.before(0, i))
                for k in range(2):
                    act.activation(QKV[:, 2 * k:2 * k + 2, :], psum[:, 1 + k, 0:384].rearrange("p (t c) -> p t c", t=2),
                                   ACT.Copy).then_inc(a_qkv.sem, 1)
                act.wait_ge(a_ss.sem, a_ss.at(0, i))
                act.activation(RN, SS, ACT.Sqrt, bias=tiny[:, 0:1]).then_inc(a_sqrt.sem, 1)
                act.wait_ge(a_split.sem, a_split.at(0, i))
                act.wait_ge(a_tr.sem, a_tr.before(0, i))
                key_rows(act, HML[:, 32:64], Ks, a_krows)
                for b in range(2):
                    act.wait_ge(a_tr.sem, a_tr.at(0, i, 2 * b + 1))
                    act.activation(QT[:, b], psum_b16(1), ACT.Copy).then_inc(a_qt.sem, 1)
                for n in range(4):
                    if True:
                        act.wait_ge(a_sc.sem, a_sc.at(0, i, n + 1))
                        act.wait_ge(a_av.sem, a_av.at(0, i, n - 1))
                        act.activation(PR[:, n % 2], psum[:, 4:8, 0:384], ACT.Exp, scale=8.0).then_inc(a_exp.sem, 1)

        def cos_gpsimd(pool, layer):
            pool.memset(VP, 0.0).then_inc(constants, 1)
            pool.memset(Qs, 0.0).then_inc(constants, 1)
            pool.memset(Ks, 0.0).then_inc(constants, 1)
            pool.wait_ge(constants, 12)
            with pool.Fori(0, STEPS) as i:
                inverse_deviations(pool, i, 0, a_mv, a_rstd, second=EPS)
                pool.wait_ge(a_qkv.sem, a_qkv.at(0, i))
                pool.wait_ge(a_av.sem, a_av.before(0, i))
                stand(pool)
                for n in range(4):
                    pool.tensor_copy(VP[:, :, n:8:4, DH * n:DH * n + DH],
                                     QKV[:, :, 128:192].rearrange("p t (h d) -> p t h d", d=DH)[:, :, n:8:4, :]).then_inc(a_vp.sem, 1)
        def rows_of(x, u, k):
            return x[:, :, DH * u:DH * (u + k)].rearrange("p n (k d) -> p n k d", d=DH)

        def query_rows(dve, parts, rows, n, done):
            for part, u, k in ((0, 0, 3), (1, 3, 2), (2, 5, 1)):
                dve.tensor_copy(rows_of(rows, u, k), parts[:, :, part, :].unsqueeze(2).broadcast_to([P, n, k, DH])).then_inc(done.sem, 1)

        def key_rows(act, parts, rows, done):
            for u, k in ((0, 3), (3, 2), (5, 1)):
                act.activation(rows_of(rows, u, k), parts[:, :, 0:k, :], ACT.Copy).then_inc(done.sem, 1)

        def head_scores(pe, bank, kt, qt, k):
            pe.matmul(psum[:, bank, 0:256], kt[0:k, 0:128], qt[0:k, :], start=True, stop=False, skip_group_check=True)
            pe.matmul(psum[:, bank, 256:384], kt[0:k, 128:256], qt[0:k, 128:256], start=False, stop=False, skip_group_check=True)

        def mask_scores(pe, bank):
            v = psum[:, bank, :].rearrange("p (a q) -> p a q", q=256)[:, :, 0:128]
            return pe.matmul(v, identb[:], mask_kq[:].unsqueeze(1).broadcast_to([P, 2, P]), start=False, stop=True, skip_group_check=True)

        def weigh_values(pe, n, vp, pr):
            for half in range(2):
                for kt in range(2):
                    for r in range(4):
                        lo, hi = (0, 256) if kt == 0 else (128, 256)
                        mm = pe.matmul(psum[32 * r:32 * r + 32, 3, 256 * half + lo:256 * half + hi],
                                       ones4[:, n, :] if half else vp(kt, 4 * r + n),
                                       pr[:, r, 0:256] if kt == 0 else pr[:, r, 256:384],
                                       start=(n == half == kt == 0), stop=(n == 3 and half == kt == 1),
                                       skip_group_check=True, tile_position=(0, 32 * r))
            return mm

        def cos_tensor(pe, layer):
            pe.wait_ge(constants, 12)
            with pe.Fori(0, STEPS) as i:
                pe.wait_ge(a_xn.sem, a_xn.at(0, i))
                pe.wait_ge(a_x.sem, a_x.before(0, i))
                for j in range(TPI):
                    mm = pe.transpose(psum[:, 0, P * j:P * j + P], XN[:, j, :], ident[:])
                mm.then_inc(a_xt_ps.sem, 1)
                pe.wait_ge(a_xt.sem, a_xt.at(0, i))
                pe.wait_ge(a_qt.sem, a_qt.before(0, i))
                for j in range(TPI):
                    mm = pe.matmul(psum[:, 1 + j // 2, 192 * (j % 2):192 * (j % 2) + 192], XT[:, P * j:P * j + P],
                                   w_qkv[:], start=True, stop=True)
                mm.then_inc(a_qkv_ps.sem, 1)
                pe.wait_ge(a_qrows.sem, a_qrows.at(0, i))
                pe.wait_ge(a_krows.sem, a_krows.at(0, i))
                pe.wait_ge(a_qkv.sem, a_qkv.at(0, i))

                def transposes(b):
                    for s, rows_ in ((0, Qs), (1, Ks)):
                        if b:
                            pe.wait_ge(a_qt.sem, a_qt.at(0, i, 2))
                        for c in range(4):
                            for t in range(2):
                                mm = pe.transpose(psum_b16(1 + s)[:, c, P * t:P * t + P],
                                                  rows_[:, (2 * b + t) * 8 + 2 * c:(2 * b + t) * 8 + 2 * c + 2, :].rearrange("p h k -> p (h k)"),
                                                  identb[:])
                        mm.then_inc(a_tr.sem, 1)

                def scores(n):
                    pe.wait_ge(a_qt.sem, a_qt.at(0, i))
                    pe.wait_ge(a_exp.sem, a_exp.at(0, i, n))
                    for r in range(4):
                        b, h = r // 2, n + 4 * (r % 2)
                        c, lo = h // 2, HROWS * (h % 2)
                        head_scores(pe, 4 + r, KT[lo:lo + HROWS, b, c], QT[lo:lo + HROWS, b, c], SPLIT)
                    for r in range(4):
                        mm = mask_scores(pe, 4 + r)
                    mm.then_inc(a_sc.sem, 1)

                def values(n):
                    pe.wait_ge(a_exp.sem, a_exp.at(0, i, n + 1))
                    if n == 0:
                        pe.wait_ge(a_vp.sem, a_vp.at(0, i))
                        pe.wait_ge(a_ot.sem, a_ot.before(0, i))
                    weigh_values(pe, n, lambda kt, h: VP[:, 2 * (h // 8) + kt, h % 8, :], PR[:, n % 2]).then_inc(a_av.sem, 1)

                transposes(0)
                transposes(1)
                scores(0)
                for n in range(4):
                    if n < 3:
                        scores(n + 1)
                    values(n)
                pe.wait_ge(a_ot.sem, a_ot.at(0, i))
                for b in range(2):
                    for t in range(2):
                        mm = pe.matmul(psum[:, 0, P * (2 * b + t):P * (2 * b + t) + P], OT[:, P * t:P * t + P],
                                       w_out[:, b, :], start=True, stop=True, skip_group_check=True)
                mm.then_inc(a_y.sem, 1)

        def earlier(layer):
            return LAYERS[:layer].count(LAYERS[layer])

        def front_run(layer):
            return sum(k != "cos" for k in LAYERS[:layer])

        def rstd_run(r):
            return sum(k != "glru" for k in [k for k in LAYERS if k != "cos"][:r])

        f_link = signal("f_link", 7)
        f_mv = signal("f_mv")
        f_rstd = signal("f_rstd", 2)
        f_rstd2 = signal("f_rstd2", 7)
        f_xn = signal("f_xn", TPI)
        f_xt_ps = signal("f_xt_ps")
        f_xt = signal("f_xt")

        def front_vector(dve, i, r, have_rstd=None, second=None, rr=None):
            rr = rr if rr is not None else rstd_run(r)
            link = Order(f_link, r, i)
            dve.wait_ge(f_xt_ps.sem, f_xt_ps.before(r, i))
            layernorm(dve, link, i, f_xn, r, f_mv, f_rstd if have_rstd is None else have_rstd, second, rr)
            link.close()

        def front_tensor(pe, i, r):
            pe.wait_ge(f_xn.sem, f_xn.at(r, i))
            pe.wait_ge(f_xt.sem, f_xt.before(r, i))
            for j in range(TPI):
                mm = pe.transpose(psum[:, 0, P * j:P * j + P], XN[:, j, :], ident[:])
            mm.then_inc(f_xt_ps.sem, 1)

        used[0] = 0
        wg_t = weight("wg_t", [D, D])
        wc_t = weight("wc_t", [D, D])
        w1_t = weight("w1_t", [D, D])
        w2_t = weight("w2_t", [D, D])
        w3_t = weight("w3_t", [D, D])
        rms_w = weight("rms_w", [D, 1])
        ffn_w = weight("ffn_w", [D, 1])
        BETA = view([P, W])
        KEEP = view([P, W])
        HX = view([P, W])
        HSQ = view([P, W])
        RMS = view([P, W])
        HN = view([P, W])
        GATE = view([P, W])
        g_proj = signal("g_proj")
        g_beta = signal("g_beta", 2)
        g_link = signal("g_link", 4)
        g_hx = signal("g_hx", 2)
        g_sq = signal("g_sq")
        g_ms = signal("g_ms")
        g_rms = signal("g_rms")
        g_hn = signal("g_hn")
        g_up = signal("g_up")
        g_sig = signal("g_sig")
        g_gate = signal("g_gate")
        g_y = signal("g_y")
        g_x = signal("g_x")

        def glru_vector(dve, layer):
            r = front_run(layer)
            rr = 0
            with dve.Fori(0, STEPS) as i:
                front_vector(dve, i, r, f_rstd2, 1e-6, rr)
                link = Order(g_link, 0, i)
                dve.wait_ge(g_beta.sem, g_beta.at(0, i))
                dve.tensor_tensor(BETA, psum[:, 2, :], BETA, ALU.mult).then_inc(link.sem, link.one())
                dve.wait_ge(link.sem, link.so_far())
                dve.wait_ge(g_y.sem, g_y.before(0, i))
                stand(dve)
                for b in range(2):
                    s = slice(SEQ * b, SEQ * b + SEQ)
                    dve.tensor_tensor_scan(HX[:, s], KEEP[:, s], BETA[:, s], 0.0, ALU.mult, ALU.add).then_inc(g_hx.sem, 1)
                dve.wait_ge(g_rms.sem, g_rms.at(0, i))
                dve.reciprocal(RMS, RMS).then_inc(link.sem, link.one())
                dve.wait_ge(link.sem, link.so_far())
                dve.scalar_tensor_tensor(HN, HX, ffn_w[:, 0:1], RMS, ALU.mult, ALU.mult).then_inc(g_hn.sem, 1)
                dve.wait_ge(g_sig.sem, g_sig.at(0, i))
                dve.tensor_tensor(GATE, psum[:, 4, :], GATE, ALU.mult).then_inc(link.sem, link.one())
                dve.wait_ge(link.sem, link.so_far())
                dve.tensor_tensor(GATE, psum[:, 5, :], GATE, ALU.mult).then_inc(g_gate.sem, 1)
                dve.wait_ge(g_y.sem, g_y.at(0, i))
                xs = X[:, bass.ds(i * TPI, TPI), :].rearrange("p t d -> p (t d)")
                dve.tensor_tensor(xs, psum[:, 6, :], xs, ALU.add).then_inc(link.sem, link.one())
                dve.wait_ge(link.sem, link.so_far())
                link.close()

        def glru_scalar(act, layer):
            r = front_run(layer)
            with act.Fori(0, STEPS) as i:
                act.wait_ge(f_xt_ps.sem, f_xt_ps.at(r, i))
                act.wait_ge(g_proj.sem, g_proj.before(0, i))
                act.activation(XT[:], psum[:, 0, :], ACT.Copy, scale=rms_w[:, 0:1]).then_inc(f_xt.sem, 1)
                act.wait_ge(g_proj.sem, g_proj.at(0, i))
                act.wait_ge(g_hx.sem, g_hx.before(0, i))
                act.activation(BETA, psum[:, 1, :], ACT.Sigmoid).then_inc(g_beta.sem, 1)
                act.activation(KEEP, psum[:, 1, :], ACT.Sigmoid, scale=-1.0).then_inc(g_beta.sem, 1)
                act.wait_ge(g_hx.sem, g_hx.at(0, i))
                act.activation(HSQ, HX, ACT.Square).then_inc(g_sq.sem, 1)
                act.wait_ge(g_ms.sem, g_ms.at(0, i))
                act.wait_ge(g_hn.sem, g_hn.before(0, i))
                act.activation(RMS, psum[:, 3, :], ACT.Sqrt, bias=rms_eps[:, 0:1], scale=1.0 / D).then_inc(g_rms.sem, 1)
                act.wait_ge(g_up.sem, g_up.at(0, i))
                act.wait_ge(g_y.sem, g_y.before(0, i))
                act.activation(GATE, psum[:, 4, :], ACT.Sigmoid).then_inc(g_sig.sem, 1)

        def glru_gpsimd(pool, layer):
            r = front_run(layer)
            rr = 0
            with pool.Fori(0, STEPS) as i:
                inverse_deviations(pool, i, r, f_mv, f_rstd2, second=1e-6, rr=rr)

        def glru_tensor(pe, layer):
            r = front_run(layer)
            with pe.Fori(0, STEPS) as i:
                front_tensor(pe, i, r)
                pe.wait_ge(f_xt.sem, f_xt.at(r, i))
                pe.wait_ge(g_hx.sem, g_hx.before(0, i))
                pe.matmul(psum[:, 1, :], wg_t[:], XT[:], start=True, stop=True)
                pe.matmul(psum[:, 2, :], wc_t[:], XT[:], start=True, stop=True).then_inc(g_proj.sem, 1)
                pe.wait_ge(g_sq.sem, g_sq.at(0, i))
                pe.matmul(psum[:, 3, :], ones[:], HSQ, start=True, stop=True).then_inc(g_ms.sem, 1)
                pe.wait_ge(g_hn.sem, g_hn.at(0, i))
                pe.matmul(psum[:, 4, :], w1_t[:], HN, start=True, stop=True)
                pe.matmul(psum[:, 5, :], w3_t[:], HN, start=True, stop=True).then_inc(g_up.sem, 1)
                pe.wait_ge(g_gate.sem, g_gate.at(0, i))
                for j in range(TPI):
                    s = slice(P * j, P * j + P)
                    pe.matmul(psum[:, 6, s], HX[:, s], ident[:], start=True, stop=False, skip_group_check=True)
                    mm = pe.matmul(psum[:, 6, s], GATE[:, s], w2_t[:], start=False, stop=True, skip_group_check=True)
                mm.then_inc(g_y.sem, 1)

        used[0] = 0
        wr_t = weight("wr_t", [D, D])
        wk_t = weight("wk_t", [D, D])
        wv_t = weight("wv_t", [D, D])
        mu = weight("mu", [D, 2])
        one_minus_mu = sb("one_minus_mu", [D, 2])
        XS = view([P, 2, SEQ + 1])
        MIX = view([P, 2, 2, SEQ])
        R_ = view([P, W])
        KK = view([P, W])
        h_zero = semaphore("h_zero")
        h_prev = signal("h_prev", 2)
        h_mix = signal("h_mix", 2)
        h_rk = signal("h_rk")
        h_r = signal("h_r")
        h_k = signal("h_k")
        h_v = signal("h_v")
        h_link = signal("h_link", 2)

        def ffn_vector(dve, layer):
            r, run = front_run(layer), earlier(layer)
            dve.memset(XS[:, :, 0:1], 0.0).then_inc(h_zero, 1)
            dve.tensor_scalar(one_minus_mu[:], mu[:], -1.0, 1.0, ALU.mult, ALU.add).then_inc(h_zero, 1)
            with dve.Fori(0, STEPS) as i:
                front_vector(dve, i, r)
                link = Order(h_link, run, i)
                for m in range(2):
                    dve.wait_ge(h_prev.sem, h_prev.at(run, i, m + 1))
                    dve.scalar_tensor_tensor(MIX[:, m], XS[:, :, 1:SEQ + 1], mu[:, m:m + 1], MIX[:, m],
                                             ALU.mult, ALU.add).then_inc(h_mix.sem, 1)
                dve.wait_ge(h_rk.sem, h_rk.at(run, i))
                dve.tensor_scalar(KK, psum[:, 2, :], 0.0, None, ALU.max).then_inc(link.sem, link.one())
                dve.wait_ge(link.sem, link.so_far())
                dve.tensor_tensor(KK, KK, KK, ALU.mult).then_inc(h_k.sem, 1)
                dve.wait_ge(h_v.sem, h_v.at(run, i))
                dve.wait_ge(h_r.sem, h_r.at(run, i))
                dve.tensor_tensor(R_, psum[:, 3, :], R_, ALU.mult).then_inc(h_mul.sem, 1)
                dve.wait_ge(h_mul.sem, h_mul.at(run, i))
                xs = X[:, bass.ds(i * TPI, TPI), :].rearrange("p t d -> p (t d)")
                dve.tensor_tensor(xs, R_, xs, ALU.add).then_inc(link.sem, link.one())
                dve.wait_ge(link.sem, link.so_far())
                link.close()

        h_mul = signal("h_mul")

        def ffn_scalar(act, layer):
            r, run = front_run(layer), earlier(layer)
            act.wait_ge(h_zero, 2 * run + 2)
            with act.Fori(0, STEPS) as i:
                act.wait_ge(f_xt_ps.sem, f_xt_ps.at(r, i))
                act.wait_ge(h_mix.sem, h_mix.before(run, i))
                act.activation(XS[:, :, 1:SEQ + 1], psum[:, 0, :].rearrange("p (b q) -> p b q", b=2), ACT.Copy).then_inc(f_xt.sem, 1)
                act.wait_ge(f_xt.sem, f_xt.at(r, i))
                act.wait_ge(h_rk.sem, h_rk.before(run, i))
                for m in range(2):
                    act.activation(MIX[:, m], XS[:, :, 0:SEQ], ACT.Copy, scale=one_minus_mu[:, m:m + 1]).then_inc(h_prev.sem, 1)
                act.wait_ge(h_rk.sem, h_rk.at(run, i))
                act.wait_ge(h_mul.sem, h_mul.before(run, i))
                act.wait_ge(h_link.sem, h_link.before(run, i))
                act.activation(R_, psum[:, 1, :], ACT.Sigmoid).then_inc(h_r.sem, 1)

        def ffn_gpsimd(pool, layer):
            r, run = front_run(layer), earlier(layer)
            with pool.Fori(0, STEPS) as i:
                inverse_deviations(pool, i, r, f_mv, f_rstd, rr=rstd_run(r))

        def ffn_tensor(pe, layer):
            r, run = front_run(layer), earlier(layer)
            with pe.Fori(0, STEPS) as i:
                front_tensor(pe, i, r)
                pe.wait_ge(h_mix.sem, h_mix.at(run, i))
                pe.wait_ge(h_r.sem, h_r.before(run, i))
                pe.wait_ge(h_k.sem, h_k.before(run, i))
                for j in range(TPI):
                    s = slice(P * j % SEQ, P * j % SEQ + P)
                    pe.matmul(psum[:, 1, P * j:P * j + P], MIX[:, 0, j // 2, s], wr_t[:], start=True, stop=True)
                pe.matmul(psum[:, 2, :], wk_t[:], MIX[:, 1].rearrange("p b q -> p (b q)"), start=True, stop=True).then_inc(h_rk.sem, 1)
                pe.wait_ge(h_k.sem, h_k.at(run, i))
                pe.wait_ge(h_mul.sem, h_mul.before(run, i))
                for j in range(TPI):
                    mm = pe.matmul(psum[:, 3, P * j:P * j + P], KK[:, P * j:P * j + P], wv_t[:], start=True, stop=True)
                mm.then_inc(h_v.sem, 1)

        used[0] = 0
        E2 = 2
        STATE = 16
        TAPS = 4
        w_in = weight("w_in", [D, 2 * E2, P])
        b_in = weight("b_in", [P, 2 * E2])
        conv_w = weight("conv_w", [P, E2, TAPS])
        conv_b = weight("conv_b", [P, E2])
        m_a = weight("m_a", [P, E2, STATE])
        m_ct = weight("m_ct", [STATE, E2, P])
        m_d = weight("m_d", [P, E2])
        m_wo = weight("m_wo", [P, E2, D])
        m_bo = weight("m_bo", [1, D])
        XP = view([P, E2, 2, TAPS - 1 + SEQ])
        XCS = view([P, E2, 2, SEQ])
        XC = view([P, E2, TOK])
        Z = view([P, E2, TOK])
        U16 = view([STATE, NSEQ, SEQ])
        U = view([P, 2, SEQ])
        H = view([P, 2, SEQ])
        H16 = view([STATE, NSEQ, SEQ])
        YM = view([P, E2, W])
        HALF = NSEQ // 2
        m_zero = semaphore("m_zero")
        m_in = signal("m_in")
        m_xp = signal("m_xp", 4)
        m_conv = signal("m_conv", 8)
        m_u_ps = signal("m_u_ps")
        m_u = signal("m_u")
        m_spread = semaphore("m_spread")
        m_h = semaphore("m_h")
        m_gather = semaphore("m_gather")
        m_y_ps = signal("m_y_ps")
        m_ym = signal("m_ym", 4)
        m_out = signal("m_out")
        m_x = signal("m_x")
        UNROLL = 16

        def mamba_vector(dve, layer):
            r = front_run(layer)
            dve.memset(XP[:, :, :, 0:TAPS - 1], 0.0).then_inc(m_zero, 1)
            with dve.Fori(0, STEPS) as i:
                front_vector(dve, i, r)
                dve.wait_ge(m_u_ps.sem, m_u_ps.before(0, i))
                dve.wait_ge(m_xc.sem, m_xc.before(0, i))
                dve.wait_ge(m_xp.sem, m_xp.at(0, i, 2))
                for k in range(TAPS):
                    if k:
                        dve.wait_ge(m_conv.sem, m_conv.at(0, i, 2 * k))
                    for e in range(E2):
                        if k == 0:
                            ins = dve.tensor_scalar(XCS[:, e], XP[:, e, :, 0:SEQ], conv_w[:, e, 0:1], conv_b[:, e:e + 1], ALU.mult, ALU.add)
                        else:
                            ins = dve.scalar_tensor_tensor(XCS[:, e], XP[:, e, :, k:k + SEQ], conv_w[:, e, k:k + 1], XCS[:, e], ALU.mult, ALU.add)
                        ins.then_inc(m_conv.sem, 1)
            with dve.Fori(0, STEPS) as i:
                dve.wait_ge(m_y_ps.sem, m_y_ps.at(0, i))
                dve.wait_ge(m_out.sem, m_out.before(0, i))
                ym = lambda e: YM[:, e, :]
                for e in range(E2):
                    dve.scalar_tensor_tensor(ym(e), XC[:, e, bass.ds(i * W, W)], m_d[:, e:e + 1], psum[:, 1 + e, :], ALU.mult, ALU.add).then_inc(m_ym.sem, 1)
                for e in range(E2):
                    dve.wait_ge(m_ym.sem, m_ym.at(0, i, e + 1))
                    dve.tensor_tensor(ym(e), ym(e), Z[:, e, bass.ds(i * W, W)], ALU.mult).then_inc(m_ym.sem, 1)
                dve.wait_ge(m_out.sem, m_out.at(0, i))
                xs = X[:, bass.ds(i * TPI, TPI), :].rearrange("p t d -> p (t d)")
                dve.tensor_tensor(xs, psum[:, 3, :], xs, ALU.add).then_inc(m_x.sem, 1)

        m_xc = signal("m_xc")

        def mamba_scalar(act, layer):
            r = front_run(layer)
            act.wait_ge(m_zero, 1)
            with act.Fori(0, STEPS) as i:
                act.wait_ge(f_xt_ps.sem, f_xt_ps.at(r, i))
                act.wait_ge(m_in.sem, m_in.before(0, i))
                act.activation(XT[:], psum[:, 0, :], ACT.Copy).then_inc(f_xt.sem, 1)
                act.wait_ge(m_in.sem, m_in.at(0, i))
                act.wait_ge(m_conv.sem, m_conv.before(0, i))
                for e in range(E2):
                    act.activation(XP[:, e, :, TAPS - 1:], psum[:, 1 + e, :].rearrange("p (b q) -> p b q", b=2),
                                   ACT.Identity, bias=b_in[:, e:e + 1]).then_inc(m_xp.sem, 1)
                for e in range(E2):
                    act.activation(Z[:, e, bass.ds(i * W, W)], psum[:, 1 + E2 + e, :], ACT.Sigmoid, bias=b_in[:, E2 + e:E2 + e + 1]).then_inc(m_xp.sem, 1)
                act.wait_ge(m_conv.sem, m_conv.at(0, i))
                act.activation(XC[:, :, bass.ds(i * W, W)], XCS.rearrange("p e b q -> p e (b q)"), ACT.Copy).then_inc(m_xc.sem, 1)
                act.wait_ge(m_u_ps.sem, m_u_ps.at(0, i))
                act.activation(U16[:, bass.ds(i * 2, 2), :], psum[0:STATE, 5, :].rearrange("p (b q) -> p b q", b=2), ACT.Copy).then_inc(m_u.sem, 1)
            act.wait_ge(m_spread, 16 * NSEQ)
            for g in range(2):
                act.activation(H[:, g, 0:1], U[:, g, 0:1], ACT.Tanh).then_inc(m_h, 1)
            for t in range(1, SEQ):
                for g in range(2):
                    act.wait_ge(m_h, 2 * t + g - 1)
                    act.activation(H[:, g, t:t + 1], U[:, g, t:t + 1], ACT.Tanh, bias=H[:, g, t - 1:t]).then_inc(m_h, 1)

        def mamba_gpsimd(pool, layer):
            r = front_run(layer)
            with pool.Fori(0, STEPS) as i:
                inverse_deviations(pool, i, r, f_mv, f_rstd, rr=rstd_run(r))
            pool.wait_ge(m_u.sem, m_u.end(0))
            for s in range(NSEQ):
                pool.dma_start(U[STATE * (s % HALF):STATE * (s % HALF) + STATE, s // HALF, :], U16[:, s, :]).then_inc(m_spread, 16)
            pool.wait_ge(m_h, 2 * SEQ)
            for s in range(NSEQ):
                pool.dma_start(H16[:, s, :], H[STATE * (s % HALF):STATE * (s % HALF) + STATE, s // HALF, :]).then_inc(m_gather, 16)

        def mamba_tensor(pe, layer):
            r = front_run(layer)
            with pe.Fori(0, STEPS) as i:
                front_tensor(pe, i, r)
                pe.wait_ge(f_xt.sem, f_xt.at(r, i))
                pe.wait_ge(m_xp.sem, m_xp.before(0, i))
                for e in range(2 * E2):
                    mm = pe.matmul(psum[:, 1 + e, :], w_in[:, e, :], XT[:], start=True, stop=True)
                mm.then_inc(m_in.sem, 1)
                pe.wait_ge(m_conv.sem, m_conv.at(0, i))
                pe.wait_ge(m_u.sem, m_u.before(0, i))
                for e in range(E2):
                    mm = pe.matmul(psum[0:STATE, 5, :], m_a[:, e, :], XCS[:, e].rearrange("p b q -> p (b q)"), start=(e == 0), stop=(e == E2 - 1))
                mm.then_inc(m_u_ps.sem, 1)
            pe.wait_ge(m_gather, 16 * NSEQ)
            with pe.Fori(0, STEPS) as i:
                pe.wait_ge(m_ym.sem, m_ym.before(0, i))
                for e in range(E2):
                    mm = pe.matmul(psum[:, 1 + e, :], m_ct[:, e, :], H16[:, bass.ds(i * 2, 2), :].rearrange("p b q -> p (b q)"), start=True, stop=True)
                mm.then_inc(m_y_ps.sem, 1)
                pe.wait_ge(m_ym.sem, m_ym.at(0, i))
                pe.wait_ge(m_x.sem, m_x.before(0, i))
                for j in range(TPI):
                    s = slice(P * j, P * j + P)
                    for e in range(E2):
                        pe.matmul(psum[:, 3, s], YM[:, e, s], m_wo[:, e, :], start=(e == 0), stop=False, skip_group_check=True)
                    mm = pe.matmul(psum[:, 3, s], ones[0:1, :], m_bo[:], start=False, stop=True, skip_group_check=True)
                mm.then_inc(m_out.sem, 1)

        used[0] = 0
        NH = 16
        w_qkvt = weight("w_qkvt", [D, 3 * D])
        w_ot = weight("w_ot", [D, D])
        cos = weight("cos", [P, TPI, DH // 2])
        sin = weight("sin", [P, 2, TPI, DH // 2])
        MROW = SPLIT
        SCORE_K = SPLIT + 3
        QKV3 = view([P, 3, TPI, D])
        RT = view([P, 2, TPI, NH, DH])
        RU = view([P, 2, TPI, NH, DH])
        RL = view([P, 2 * TPI * NH, DH])
        RH = view([P, 2 * TPI * NH, 3, DH], BF16)
        QS2 = view([P, TPI * NH, HROWS], BF16)
        KS2 = view([P, TPI * NH, HROWS], BF16)
        QT2 = view([P, 2, NH // 2, SEQ], BF16)
        KT2 = view([P, 2, NH // 2, SEQ], BF16)
        VP2 = view([P, TPI, NH, 32])
        PR2 = view([P, 2, 4, 384])
        REC2 = view([P, SEQ])
        OT2 = view([P, 2, SEQ])
        MX = view([P, TPI, NH])
        ML = view([P, TPI * NH])
        r_zero = semaphore("r_zero")
        r_link = signal("r_link", 10)
        r_qkv_ps = signal("r_qkv_ps")
        r_qkv = signal("r_qkv", TPI)
        r_split = signal("r_split")
        r_vp = signal("r_vp", 4)
        r_qrows = signal("r_qrows", 3)
        r_krows = signal("r_krows", 3)
        r_tr = signal("r_tr", 12)
        r_qt = signal("r_qt", 12)
        r_s1 = signal("r_s1", 8)
        r_max = signal("r_max", 8)
        r_mrows = signal("r_mrows", 5)
        r_sc = signal("r_sc", 8)
        r_exp = signal("r_exp", 8)
        r_av = signal("r_av", 8)
        r_rec = signal("r_rec", 2)
        r_ot = signal("r_ot", 2)
        r_y = signal("r_y")
        r_x = signal("r_x")

        def rope_vector(dve, layer):
            r = front_run(layer)
            with dve.Fori(0, STEPS) as i:
                front_vector(dve, i, r)
                link = Order(r_link, 0, i)
                dve.wait_ge(r_qkv.sem, r_qkv.at(0, i))
                for s in range(2):
                    x = QKV3[:, s].rearrange("p t (h d) -> p t h d", d=DH // 2)
                    xh = QKV3[:, s].rearrange("p t (h u d) -> p t h u d", u=2, d=DH // 2)
                    c = cos[:].unsqueeze(2).broadcast_to([P, TPI, 2 * NH, DH // 2])
                    dve.tensor_tensor(RT[:, s].rearrange("p t h (u d) -> p t (h u) d", u=2), x, c, ALU.mult).then_inc(link.sem, link.one())
                    for u in range(2):
                        sn = sin[:, u].unsqueeze(2).broadcast_to([P, TPI, NH, DH // 2])
                        dve.tensor_tensor(RU[:, s, :, :, 4 * u:4 * u + 4], xh[:, :, :, 1 - u, :], sn, ALU.mult).then_inc(link.sem, link.one())
                dve.wait_ge(link.sem, link.so_far())
                dve.tensor_tensor(RT, RT, RU, ALU.add).then_inc(link.sem, link.one())
                dve.wait_ge(link.sem, link.so_far())
                split3(dve, link, RT.rearrange("p s t h d -> p (s t h) d"), RL, RH, r_split, r_krows, 0, i)
                dve.wait_ge(r_split.sem, r_split.at(0, i))
                dve.wait_ge(r_tr.sem, r_tr.before(0, i))
                query_rows(dve, RH[:, 0:TPI * NH], QS2, TPI * NH, r_qrows)
                for g in range(8):
                    b, n = g // 4, g % 4
                    dve.wait_ge(r_s1.sem, r_s1.at(0, i, g + 1))
                    dve.tensor_reduce(MX[:, 2 * b, n:NH:4], psum[:, 4:8, 0:128], AX.X, ALU.max, negate=True)
                    dve.tensor_reduce(MX[:, 2 * b + 1, n:NH:4], psum[:, 4:8, 128:384], AX.X, ALU.max, negate=True).then_inc(r_max.sem, 1)
                dve.drain()
                dve.wait_ge(r_max.sem, r_max.at(0, i))
                m = MX.rearrange("p t h -> p (t h)")
                row = lambda k: QS2[:, :, MROW + k]
                dve.wait_ge(r_tr.sem, r_tr.at(0, i, 8))
                dve.tensor_copy(row(0), m).then_inc(r_mrows.sem, 1)
                dve.wait_ge(r_mrows.sem, r_mrows.at(0, i, 1))
                dve.tensor_tensor(ML, m, row(0), ALU.subtract).then_inc(r_mrows.sem, 1)
                dve.wait_ge(r_mrows.sem, r_mrows.at(0, i, 2))
                dve.tensor_copy(row(1), ML).then_inc(r_mrows.sem, 1)
                dve.wait_ge(r_mrows.sem, r_mrows.at(0, i, 3))
                dve.tensor_tensor(ML, ML, row(1), ALU.subtract).then_inc(r_mrows.sem, 1)
                dve.wait_ge(r_mrows.sem, r_mrows.at(0, i, 4))
                dve.tensor_copy(row(2), ML).then_inc(r_mrows.sem, 1)
                for b in range(2):
                    dve.wait_ge(r_av.sem, r_av.at(0, i, 4 * b + 4))
                    dve.reciprocal(REC2, psum[:, 3, 256:512]).then_inc(r_rec.sem, 1)
                    dve.wait_ge(r_rec.sem, r_rec.at(0, i, b + 1))
                    dve.wait_ge(r_y.sem, r_y.before(0, i))
                    dve.tensor_tensor(OT2[:, b], psum[:, 3, 0:256], REC2, ALU.mult).then_inc(r_ot.sem, 1)
                    dve.wait_ge(r_ot.sem, r_ot.at(0, i, b + 1))
                dve.wait_ge(r_y.sem, r_y.at(0, i))
                xs = X[:, bass.ds(i * TPI, TPI), :].rearrange("p t d -> p (t d)")
                dve.tensor_tensor(xs, psum[:, 2, :], xs, ALU.add).then_inc(r_x.sem, 1)
                link.close()

        def rope_scalar(act, layer):
            r = front_run(layer)
            with act.Fori(0, STEPS) as i:
                act.wait_ge(f_xt_ps.sem, f_xt_ps.at(r, i))
                act.wait_ge(r_qkv_ps.sem, r_qkv_ps.before(0, i))
                act.activation(XT[:], psum[:, 0, :], ACT.Copy).then_inc(f_xt.sem, 1)
                act.wait_ge(r_qkv_ps.sem, r_qkv_ps.at(0, i))
                act.wait_ge(r_split.sem, r_split.before(0, i))
                act.wait_ge(r_vp.sem, r_vp.before(0, i))
                for j in range(TPI):
                    act.activation(QKV3[:, :, j, :], psum[:, 4 + j, 0:384].rearrange("p (s c) -> p s c", s=3), ACT.Copy).then_inc(r_qkv.sem, 1)
                act.wait_ge(r_split.sem, r_split.at(0, i))
                act.wait_ge(r_tr.sem, r_tr.before(0, i))
                key_rows(act, RH[:, TPI * NH:], KS2, r_krows)
                for k in range(12):
                    act.wait_ge(r_tr.sem, r_tr.at(0, i, k + 1))
                    if k < 8:
                        b, hh, t = k // 4, k // 2 % 2, (QT2, KT2)[k % 2]
                    else:
                        b, hh, t = (k - 8) // 2, k % 2, QT2
                        act.wait_ge(r_s1.sem, r_s1.at(0, i))
                    act.activation(t[:, b, 4 * hh:4 * hh + 4], psum_b16(1 + k % 2), ACT.Copy).then_inc(r_qt.sem, 1)
                for g in range(8):
                    act.wait_ge(r_sc.sem, r_sc.at(0, i, g + 1))
                    act.wait_ge(r_av.sem, r_av.at(0, i, g - 1))
                    act.activation(PR2[:, g % 2], psum[:, 4:8, 0:384], ACT.Exp, scale=DH ** -0.5).then_inc(r_exp.sem, 1)

        def rope_gpsimd(pool, layer):
            r = front_run(layer)
            pool.memset(VP2, 0.0).then_inc(r_zero, 1)
            pool.memset(QS2, 0.0).then_inc(r_zero, 1)
            pool.memset(KS2, 0.0).then_inc(r_zero, 1)
            pool.wait_ge(r_zero, 3)
            pool.memset(KS2[:, :, MROW:MROW + 3], 1.0).then_inc(r_zero, 1)
            pool.wait_ge(r_zero, 4)
            with pool.Fori(0, STEPS) as i:
                inverse_deviations(pool, i, r, f_mv, f_rstd, rr=rstd_run(r))
                pool.wait_ge(r_qkv.sem, r_qkv.at(0, i))
                pool.wait_ge(r_av.sem, r_av.before(0, i))
                stand(pool)
                for n in range(4):
                    pool.tensor_copy(VP2[:, :, n:NH:4, DH * n:DH * n + DH],
                                     QKV3[:, 2].rearrange("p t (h d) -> p t h d", d=DH)[:, :, n:NH:4, :]).then_inc(r_vp.sem, 1)

        def rope_tensor(pe, layer):
            r = front_run(layer)
            pe.wait_ge(r_zero, 4)
            with pe.Fori(0, STEPS) as i:
                front_tensor(pe, i, r)
                pe.wait_ge(f_xt.sem, f_xt.at(r, i))
                pe.wait_ge(r_exp.sem, r_exp.before(0, i))
                for j in range(TPI):
                    mm = pe.matmul(psum[:, 4 + j, 0:384], XT[:, P * j:P * j + P], w_qkvt[:], start=True, stop=True)
                mm.then_inc(r_qkv_ps.sem, 1)
                pe.wait_ge(r_qrows.sem, r_qrows.at(0, i))
                pe.wait_ge(r_krows.sem, r_krows.at(0, i))
                pe.wait_ge(r_x.sem, r_x.before(0, i))

                def transposes(k, b, hh, rows):
                    if k >= 2:
                        pe.wait_ge(r_qt.sem, r_qt.at(0, i, k - 1))
                    for c in range(4):
                        for t in range(2):
                            h = (2 * b + t) * NH + 8 * hh + 2 * c
                            mm = pe.transpose(psum_b16(1 + k % 2)[:, c, P * t:P * t + P],
                                              rows[:, h:h + 2, :].rearrange("p h k -> p (h k)"), identb[:])
                    mm.then_inc(r_tr.sem, 1)

                def head(t, b, h):
                    return t[HROWS * (h % 2):HROWS * (h % 2) + HROWS, b, h // 2]

                for k in range(8):
                    transposes(k, k // 4, k // 2 % 2, (QS2, KS2)[k % 2])
                pe.wait_ge(r_qkv.sem, r_qkv.at(0, i))
                for g in range(8):
                    b, n = g // 4, g % 4
                    if g % 4 == 0:
                        pe.wait_ge(r_qt.sem, r_qt.at(0, i, 4 * b + 4))
                    pe.wait_ge(r_max.sem, r_max.at(0, i, g))
                    for rr in range(4):
                        q, kk = head(QT2, b, n + 4 * rr), head(KT2, b, n + 4 * rr)
                        pe.matmul(psum[:, 4 + rr, 0:128], q[0:SPLIT, 0:128], kk[0:SPLIT, 0:128], start=True, stop=False, skip_group_check=True)
                        pe.matmul(psum[:, 4 + rr, 128:384], q[0:SPLIT, 128:256], kk[0:SPLIT, :], start=False, stop=False, skip_group_check=True)
                    for rr in range(4):
                        v = psum[:, 4 + rr, 0:384].rearrange("p (a q) -> p a q", q=P)[:, 0:3:2, :]
                        mm = pe.matmul(v, identb[:], mask_qk[:].unsqueeze(1).broadcast_to([P, 2, P]), start=False, stop=True, skip_group_check=True)
                    mm.then_inc(r_s1.sem, 1)
                pe.wait_ge(r_mrows.sem, r_mrows.at(0, i))
                for k in range(8, 12):
                    transposes(k, (k - 8) // 2, k % 2, QS2)

                def scores(g):
                    b, n = g // 4, g % 4
                    pe.wait_ge(r_qt.sem, r_qt.at(0, i, 10 + 2 * b))
                    pe.wait_ge(r_exp.sem, r_exp.at(0, i, g))
                    for rr in range(4):
                        head_scores(pe, 4 + rr, head(KT2, b, n + 4 * rr), head(QT2, b, n + 4 * rr), SCORE_K)
                    for rr in range(4):
                        mm = mask_scores(pe, 4 + rr)
                    mm.then_inc(r_sc.sem, 1)

                def values(g):
                    b, n = g // 4, g % 4
                    pe.wait_ge(r_exp.sem, r_exp.at(0, i, g + 1))
                    if g == 0:
                        pe.wait_ge(r_vp.sem, r_vp.at(0, i))
                    if n == 0:
                        pe.wait_ge(r_ot.sem, r_ot.at(0, i, b))
                    weigh_values(pe, n, lambda kt, h: VP2[:, 2 * b + kt, h, :], PR2[:, g % 2]).then_inc(r_av.sem, 1)

                scores(0)
                for g in range(8):
                    if g < 7:
                        scores(g + 1)
                    values(g)
                pe.wait_ge(r_ot.sem, r_ot.at(0, i))
                for j in range(TPI):
                    mm = pe.matmul(psum[:, 2, P * j:P * j + P], OT2[:, j // 2, P * (j % 2):P * (j % 2) + P], w_ot[:],
                                   start=True, stop=True, skip_group_check=True)
                mm.then_inc(r_y.sem, 1)

        used[0] = 0
        NE = 160
        TOPK = 8
        INTER = 64
        ROUTED_SCALE = 2.5
        CE = 8
        CHUNKS = NE // CE
        router_t = weight("router_t", [D, NE])
        e_bias = weight("e_bias", [1, NE])
        sh_gate = weight("sh_gate", [D, INTER])
        sh_down = weight("sh_down", [INTER, D])
        GT = view([D, NE * INTER])
        DT = view([P, NE // 2, D])
        PROB = view([P, TPI, NE])
        REST = view([P, TPI, NE])
        M8 = view([P, TPI, TOPK])
        SUM = view([P, TPI])
        COMB = view([P, TPI, NE])
        SG = view([P, 2, CE * INTER])
        HE = view([P, 2, CE * INTER])
        HT = view([P, 2, CE // 2, P])
        e_loaded = semaphore("e_loaded")
        e_lg = signal("e_lg")
        e_prob = signal("e_prob", 2)
        e_link = signal("e_link", 3 * TPI + 3)
        e_comb = signal("e_comb", TPI)
        e_x = signal("e_x")
        e_hsh = signal("e_hsh", TPI)
        e_h = signal("e_h", TPI, STEPS * (CHUNKS + 1))
        e_sg = signal("e_sg", TPI, STEPS * (CHUNKS + 1))
        e_mul = signal("e_mul", TPI, STEPS * (CHUNKS + 1))
        e_he = signal("e_he", TPI, STEPS * (CHUNKS + 1))
        e_tr = signal("e_tr", TPI, STEPS * (CHUNKS + 1))
        e_ht = signal("e_ht", TPI, STEPS * (CHUNKS + 1))
        e_y = signal("e_y", TPI, STEPS * (CHUNKS + 1))

        def moe_vector(dve, layer):
            r, run = front_run(layer), earlier(layer)
            with dve.Fori(0, STEPS) as i:
                front_vector(dve, i, r)
                link = Order(e_link, run, i)
                dve.wait_ge(e_prob.sem, e_prob.at(run, i))
                stand(dve)
                for j in range(TPI):
                    dve.max(M8[:, j], PROB[:, j]).then_inc(link.sem, link.one())
                dve.wait_ge(link.sem, link.so_far())
                stand(dve)
                for j in range(TPI):
                    dve.match_replace(REST[:, j], M8[:, j], PROB[:, j], -1.0).then_inc(link.sem, link.one())
                dve.tensor_reduce(SUM, M8, AX.X, ALU.add).then_inc(link.sem, link.one())
                dve.wait_ge(link.sem, link.so_far())
                dve.tensor_scalar(SUM, SUM, 1e-9, None, ALU.add).then_inc(link.sem, link.one())
                for j in range(TPI):
                    dve.scalar_tensor_tensor(REST[:, j], REST[:, j], 0.0, PROB[:, j], ALU.is_lt, ALU.mult).then_inc(link.sem, link.one())
                dve.wait_ge(link.sem, link.so_far())
                dve.reciprocal(SUM, SUM).then_inc(link.sem, link.one())
                dve.wait_ge(link.sem, link.so_far())
                for j in range(TPI):
                    dve.tensor_scalar(COMB[:, j], REST[:, j], SUM[:, j:j + 1], ROUTED_SCALE, ALU.mult, ALU.mult).then_inc(e_comb.sem, 1)
                dve.wait_ge(e_comb.sem, e_comb.at(run, i))

                def unit(c, j, n, weigh):
                    dve.wait_ge(e_sg.sem, e_sg.at(run, c, j + 1))
                    dve.wait_ge(e_tr.sem, e_tr.at(run, c, j - 1))
                    dve.tensor_tensor(HE[:, j % 2, 0:n], psum[:, 1 + j % 2, 0:n], SG[:, j % 2, 0:n], ALU.mult).then_inc((e_mul if weigh is not None else e_he).sem, 1)
                    if weigh is None:
                        return
                    dve.wait_ge(e_mul.sem, e_mul.at(run, c, j + 1))
                    he = HE[:, j % 2].rearrange("p (e k) -> p e k", k=INTER)
                    dve.tensor_tensor(he, he, weigh.unsqueeze(2).broadcast_to([P, CE, INTER]), ALU.mult).then_inc(e_he.sem, 1)

                for j in range(TPI):
                    unit(i * (CHUNKS + 1), j, INTER, None)
                dve.sem_inc(e_mul.sem, TPI)
                with dve.Fori(0, CHUNKS) as c:
                    for j in range(TPI):
                        unit(i * (CHUNKS + 1) + c + 1, j, CE * INTER, COMB[:, j, bass.ds(c * CE, CE)])
                dve.wait_ge(e_y.sem, e_y.at(run, i * (CHUNKS + 1) + CHUNKS))
                xs = X[:, bass.ds(i * TPI, TPI), :].rearrange("p t d -> p (t d)")
                dve.tensor_tensor(xs, psum[:, 5, :], xs, ALU.add).then_inc(e_x.sem, 1)
                link.close()

        def moe_scalar(act, layer):
            r, run = front_run(layer), earlier(layer)
            with act.Fori(0, STEPS) as i:
                act.wait_ge(f_xt_ps.sem, f_xt_ps.at(r, i))
                act.wait_ge(e_h.sem, e_h.before(run, i * (CHUNKS + 1)))
                act.activation(XT[:], psum[:, 0, :], ACT.Copy).then_inc(f_xt.sem, 1)
                act.wait_ge(e_lg.sem, e_lg.at(run, i))
                act.wait_ge(e_comb.sem, e_comb.before(run, i))
                for k in range(2):
                    act.activation(PROB[:, 2 * k:2 * k + 2, :], psum[:, 6 + k, 0:2 * NE].rearrange("p (t c) -> p t c", t=2), ACT.Sigmoid).then_inc(e_prob.sem, 1)

                def sigmoid(c, j, n):
                    act.wait_ge(e_h.sem, e_h.at(run, c, j + 1))
                    act.wait_ge(e_he.sem, e_he.at(run, c, j - 1))
                    act.activation(SG[:, j % 2, 0:n], psum[:, 1 + j % 2, 0:n], ACT.Sigmoid).then_inc(e_sg.sem, 1)

                def transposed(c, j, v):
                    act.wait_ge(e_tr.sem, e_tr.at(run, c, j + 1))
                    act.wait_ge(e_y.sem, e_y.at(run, c, j - 1))
                    act.activation(v(HT[:, j % 2].rearrange("p e t -> p (e t)")), v(psum[:, 3 + j % 2, :]), ACT.Copy).then_inc(e_ht.sem, 1)

                def units(c, n, v):
                    sigmoid(c, 0, n)
                    for j in range(TPI):
                        if j < TPI - 1:
                            sigmoid(c, j + 1, n)
                        transposed(c, j, v)

                units(i * (CHUNKS + 1), INTER, lambda t: t[0:INTER, 0:P])
                with act.Fori(0, CHUNKS) as c:
                    units(i * (CHUNKS + 1) + c + 1, CE * INTER, lambda t: t)

        def moe_gpsimd(pool, layer):
            r, run = front_run(layer), earlier(layer)
            pool.dma_start(GT, a["gate_t"]).then_inc(e_loaded, 16)
            pool.dma_start(DT, a["down_t"]).then_inc(e_loaded, 16)
            with pool.Fori(0, STEPS) as i:
                inverse_deviations(pool, i, r, f_mv, f_rstd, rr=rstd_run(r))

        def moe_tensor(pe, layer):
            r, run = front_run(layer), earlier(layer)
            pe.wait_ge(e_loaded, 32 * (run + 1))
            with pe.Fori(0, STEPS) as i:
                front_tensor(pe, i, r)
                pe.wait_ge(f_xt.sem, f_xt.at(r, i))
                pe.wait_ge(e_prob.sem, e_prob.before(run, i))
                for j in range(TPI):
                    o = psum[:, 6 + j // 2, NE * (j % 2):NE * (j % 2) + NE]
                    pe.matmul(o, XT[:, P * j:P * j + P], router_t[:], start=True, stop=False, skip_group_check=True)
                    mm = pe.matmul(o, ones[0:1, :], e_bias[:], start=False, stop=True, skip_group_check=True)
                mm.then_inc(e_lg.sem, 1)

                def hidden(c, j, n, gate):
                    pe.wait_ge(e_he.sem, e_he.at(run, c, j - 1))
                    pe.matmul(psum[:, 1 + j % 2, 0:n], XT[:, P * j:P * j + P], gate, start=True, stop=True, skip_group_check=True).then_inc(e_h.sem, 1)

                def transposes(c, j, n):
                    pe.wait_ge(e_he.sem, e_he.at(run, c, j + 1))
                    pe.wait_ge(e_ht.sem, e_ht.at(run, c, j - 1))
                    for k in range((n + P - 1) // P):
                        m = min(P, n)
                        if m < P:
                            stand(pe)
                        mm = pe.transpose(psum[0:m, 3 + j % 2, P * k:P * k + P], HE[:, j % 2, P * k:P * k + m], ident[:])
                    mm.then_inc(e_tr.sem, 1)

                def output(c, j, down, first):
                    pe.wait_ge(e_ht.sem, e_ht.at(run, c, j + 1))
                    for k, dn in enumerate(down):
                        m = INTER if first else P
                        mm = pe.matmul(psum[:, 5, P * j:P * j + P], HT[0:m, j % 2, k, :], dn, start=first and j == 0, stop=True, skip_group_check=True)
                    mm.then_inc(e_y.sem, 1)

                def units(c, n, gate, down, first):
                    hidden(c, 0, n, gate)
                    for j in range(TPI):
                        if j < TPI - 1:
                            hidden(c, j + 1, n, gate)
                        transposes(c, j, n)
                        if j:
                            output(c, j - 1, down, first)
                    output(c, TPI - 1, down, first)

                pe.wait_ge(e_x.sem, e_x.before(run, i))
                units(i * (CHUNKS + 1), INTER, sh_gate[:], [sh_down[:]], True)
                with pe.Fori(0, CHUNKS) as c:
                    units(i * (CHUNKS + 1) + c + 1, CE * INTER, GT[:, bass.ds(c * CE * INTER, CE * INTER)],
                          [DT[:, bass.ds(c * (CE // 2) + k, 1), :].rearrange("p a d -> p (a d)") for k in range(CE // 2)], False)

        ENGINES = 4

        def begin(eng):
            eng.wait_ge(primed, 1)
            eng.wait_ge(loaded, 16 * (len(weights) + 1))

        def finish(eng, layer):
            eng.drain().then_inc(phase_done, 1)
            eng.wait_ge(phase_done, ENGINES * (layer + 1))

        block = ctx.enter_context(nc.Block())

        @block.sync
        def _(sp):
            for s in signals:
                sp.sem_inc(s.sem, START)
            sp.sem_inc(primed, 1)
            sp.dma_start(X[:], a["x"].rearrange("(t p) d -> p t d", p=P)).then_inc(loaded, 16)
            for t, src in weights:
                sp.dma_start(t[:], src).then_inc(loaded, 16)
            sp.wait_ge(phase_done, ENGINES * len(LAYERS))
            sp.dma_start(a["out"].rearrange("(t p) d -> p t d", p=P), X[:]).then_inc(stored, 16)
            sp.wait_ge(stored, 16)

        @block.vector
        def _(dve):
            begin(dve)
            cos_vector(dve, 0)
            finish(dve, 0)
            moe_vector(dve, 1)
            finish(dve, 1)
            glru_vector(dve, 2)
            finish(dve, 2)
            moe_vector(dve, 3)
            finish(dve, 3)
            mamba_vector(dve, 4)
            finish(dve, 4)
            ffn_vector(dve, 5)
            finish(dve, 5)
            rope_vector(dve, 6)
            finish(dve, 6)
            ffn_vector(dve, 7)
            finish(dve, 7)

        @block.scalar
        def _(act):
            begin(act)
            cos_scalar(act, 0)
            finish(act, 0)
            moe_scalar(act, 1)
            finish(act, 1)
            glru_scalar(act, 2)
            finish(act, 2)
            moe_scalar(act, 3)
            finish(act, 3)
            mamba_scalar(act, 4)
            finish(act, 4)
            ffn_scalar(act, 5)
            finish(act, 5)
            rope_scalar(act, 6)
            finish(act, 6)
            ffn_scalar(act, 7)
            finish(act, 7)

        @block.gpsimd
        def _(pool):
            pool.memset(ones4[:], 0.0).then_inc(constants, 1)
            pool.memset(tiny[:], 1e-12).then_inc(constants, 1)
            pool.wait_ge(constants, 1)
            for n in range(4):
                pool.memset(ones4[:, n, DH * n:DH * n + DH], 1.0).then_inc(constants, 1)
            pool.memset(minus_half[:], -0.5).then_inc(constants, 1)
            pool.memset(rms_eps[:], 1e-6).then_inc(constants, 1)
            pool.memset(ones[:], 1.0).then_inc(constants, 1)
            begin(pool)
            cos_gpsimd(pool, 0)
            finish(pool, 0)
            moe_gpsimd(pool, 1)
            finish(pool, 1)
            glru_gpsimd(pool, 2)
            finish(pool, 2)
            moe_gpsimd(pool, 3)
            finish(pool, 3)
            mamba_gpsimd(pool, 4)
            finish(pool, 4)
            ffn_gpsimd(pool, 5)
            finish(pool, 5)
            rope_gpsimd(pool, 6)
            finish(pool, 6)
            ffn_gpsimd(pool, 7)
            finish(pool, 7)

        @block.tensor
        def _(pe):
            begin(pe)
            cos_tensor(pe, 0)
            finish(pe, 0)
            moe_tensor(pe, 1)
            finish(pe, 1)
            glru_tensor(pe, 2)
            finish(pe, 2)
            moe_tensor(pe, 3)
            finish(pe, 3)
            mamba_tensor(pe, 4)
            finish(pe, 4)
            ffn_tensor(pe, 5)
            finish(pe, 5)
            rope_tensor(pe, 6)
            finish(pe, 6)
            ffn_tensor(pe, 7)
            finish(pe, 7)


def layout(inputs):
    import numpy as np

    contiguous = np.ascontiguousarray

    def of(layer):
        return lambda name: np.asarray(inputs[layer + "_" + name])

    out = {}
    w = of("L0_attn_a")
    out["x"] = w("x").reshape(TOK, D)
    out["w_qkv"] = w("w_qkv")
    out["ln_w"], out["ln_b"] = w("ln_w").reshape(D, 1), w("ln_b").reshape(D, 1)
    inner = w("w_out").shape[0]
    w_out = np.zeros((P, 2, D), np.float32)
    w_out[:inner, 0] = w_out[inner:, 1] = w("w_out")
    out["w_out"] = w_out
    w = of("L0_attn_b")
    for name, source in (("wg_t", "Wg"), ("wc_t", "Wc"), ("w1_t", "w1"), ("w2_t", "w2"), ("w3_t", "w3")):
        out[name] = contiguous(w(source).T)
    out["rms_w"], out["ffn_w"] = w("ln_w").reshape(D, 1), w("ffn_w").reshape(D, 1)
    w = of("L0_ffn")
    experts, width = w("w_gate").shape[:2]
    out["router_t"] = contiguous(w("router_w").T)
    out["e_bias"] = w("expert_bias").reshape(1, experts)
    out["sh_gate"], out["sh_down"] = contiguous(w("w_gate_shared").T), contiguous(w("w_down_shared").T)
    out["gate_t"] = contiguous(w("w_gate").reshape(experts * width, D).T)
    out["down_t"] = contiguous(w("w_down").reshape(experts // 2, 2, D, width).transpose(1, 3, 0, 2).reshape(P, experts // 2, D))
    w = of("L1_attn_a")
    out["w_in"] = w("W_in").reshape(D, 4, P)
    out["b_in"] = contiguous(w("b_in").reshape(4, P).T)
    out["conv_w"] = contiguous(w("conv_w").reshape(2, P, -1).transpose(1, 0, 2))
    out["conv_b"] = contiguous(w("conv_b").reshape(2, P).T)
    out["m_a"] = contiguous(w("A").reshape(2, P, -1).transpose(1, 0, 2))
    out["m_ct"] = contiguous(w("C").T.reshape(-1, 2, P))
    out["m_d"] = contiguous(w("Dp").reshape(2, P).T)
    out["m_wo"] = contiguous(w("W_out").reshape(2, P, D).transpose(1, 0, 2))
    out["m_bo"] = w("b_out").reshape(1, D)
    w = of("L1_ffn")
    for name, source in (("wr_t", "W_r"), ("wk_t", "W_k"), ("wv_t", "W_v")):
        out[name] = contiguous(w(source).T)
    out["mu"] = np.stack([w("mu_r"), w("mu_k")], 1)
    w = of("L1_attn_b")
    order = np.concatenate([np.arange(0, DH, 2), np.arange(1, DH, 2)])
    rows = (np.arange(D // DH)[:, None] * DH + order[None]).reshape(-1)
    out["w_qkvt"] = contiguous(np.concatenate([w("wq")[rows], w("wk")[rows], w("wv")], 0).T)
    out["w_ot"] = contiguous(w("wo").T)
    powers = np.arange(0, DH, 2, dtype=np.float32) / np.float32(DH)
    angles = np.outer(np.arange(SEQ, dtype=np.float32), 1.0 / np.float32(10000.0) ** powers).astype(np.float32)
    tiles = lambda t: np.concatenate([t.reshape(2, P, -1).transpose(1, 0, 2)] * (TPI // 2), 1)
    out["cos"] = contiguous(tiles(np.cos(angles)))
    out["sin"] = contiguous(np.stack([-tiles(np.sin(angles)), tiles(np.sin(angles))], 1))
    out["ident"] = np.eye(P, dtype=np.float32)
    out["identb"] = np.eye(P, dtype=mybir.dt.np(BF16))
    later = np.arange(P)[:, None] > np.arange(P)[None, :]
    out["mask_kq"] = np.where(later, NEG, 0.0).astype(mybir.dt.np(BF16))
    out["mask_qk"] = np.where(later.T, NEG, 0.0).astype(mybir.dt.np(BF16))
    return out


def kernel(**inputs):
    import numpy as np
    import concourse.bacc as bacc
    from concourse.bass_utils import run_bass_kernel_spmd

    nc = bacc.Bacc("TRN2", target_bir_lowering=False, num_devices=1)
    arrays, a = {}, {}
    for name, array in layout(inputs).items():
        arrays[f"in_{name}"] = array
        a[name] = nc.dram_tensor(f"in_{name}", array.shape, mybir.dt.from_np(array.dtype), kind="ExternalInput").ap()
    a["out"] = nc.dram_tensor("out", (TOK, D), F32, kind="ExternalOutput").ap()
    program(nc, a)
    r = run_bass_kernel_spmd(nc, [arrays], core_ids=[0])
    return np.asarray(r.results[0]["out"]).reshape(NSEQ, SEQ, D)
```

```python
from contextlib import ExitStack

import concourse.bass as bass
from concourse import mybir

F32 = mybir.dt.float32
BF16 = mybir.dt.bfloat16
I32 = mybir.dt.int32
ACT = mybir.ActivationFunctionType
ALU = mybir.AluOpType
AX = mybir.AxisListType

P = 128
D = 128
SEQ = 256
NSEQ = 16
TOK = NSEQ * SEQ
TILES = TOK // P
TPI = 4
STEPS = TILES // TPI
W = TPI * P
EPS = 1e-5
DH = 8
SPLIT = 6 * DH
HROWS = 64
NEG = -1.0e30


START = 2


class Signal:

    def __init__(self, nc, ctx, name, per=1, steps=STEPS, start=START):
        self.sem = ctx.enter_context(nc.semaphore(name))
        self.per, self.steps, self.start = per, steps, start

    def at(self, run, i, c=None):
        return i * self.per + (self.start + run * self.steps * self.per + (self.per if c is None else c))

    def before(self, run, i):
        return self.at(run, i, 0)

    def end(self, run):
        return self.start + (run + 1) * self.steps * self.per


LAYERS = ("cos", "moe", "glru", "moe", "mamba", "ffn", "rope", "ffn")


def program(nc, a):
    ctx = ExitStack()
    with ctx:
        def sb(name, shape, dt=F32):
            return ctx.enter_context(nc.sbuf_tensor(name, shape, dt))

        signals = []

        def signal(name, per=1, steps=STEPS, start=START):
            s = Signal(nc, ctx, name, per, steps, start)
            signals.append(s)
            return s

        def semaphore(name):
            return ctx.enter_context(nc.semaphore(name))

        psum = ctx.enter_context(nc.psum_tensor("psum", [P, 8, 512], F32))

        X = sb("X", [P, TILES, D])
        ident = sb("ident", [P, P])
        identb = sb("identb", [P, P], BF16)
        mask_kq = sb("mask_kq", [P, P], BF16)
        mask_qk = sb("mask_qk", [P, P], BF16)
        ones4 = sb("ones4", [P, 4, 32])
        tiny = sb("tiny", [P, 1])
        rms_eps = sb("rms_eps", [P, 1])
        ones = sb("ones", [P, P])
        ones_row = sb("ones_row", [P, 160])
        minus_half = sb("minus_half", [P, 64])
        ARENA = 40704
        arena = sb("arena", [P, ARENA])
        used = [0]

        def view(shape, dt=F32, at=None):
            n = 1
            for k in shape[1:]:
                n *= k
            words = n if dt in (F32, I32) else (n + 1) // 2
            o = used[0] if at is None else at
            used[0] = o + words
            assert used[0] <= ARENA, used[0]
            v = arena[0:shape[0], o:o + words]
            if dt != F32:
                v = v.bitcast(dt)
            if len(shape) > 2:
                names = [f"d{k}" for k in range(len(shape) - 1)]
                v = v.rearrange("p (" + " ".join(names) + ") -> p " + " ".join(names),
                                **{m: k for m, k in zip(names[1:], shape[2:])})
            return v

        stats = sb("stats", [P, TPI, 6])
        mv = sb("mv", [P, TPI, 2])
        rstd = sb("rstd", [P, TPI])
        rstd2 = sb("rstd2", [P, TPI])
        XN = sb("XN", [P, TPI, D])
        XT = sb("XT", [P, W])

        loaded = semaphore("loaded")
        stored = semaphore("stored")
        constants = semaphore("constants")
        primed = semaphore("primed")
        stood = semaphore("stood")
        phase_done = semaphore("phase_done")

        weights = []

        def weight(name, shape, dt=F32, src=None):
            t = sb("w_" + name, shape, dt)
            weights.append((t, a[name] if src is None else src))
            return t

        w_qkv = weight("w_qkv", [D, 192])
        ln_w = weight("ln_w", [D, 1])
        ln_b = weight("ln_b", [D, 1])
        w_out = weight("w_out", [P, 2, D])
        for t, n in ((ident, "ident"), (identb, "identb"), (mask_kq, "mask_kq"), (mask_qk, "mask_qk")):
            weights.append((t, a[n]))

        class Order:

            def __init__(self, sig, run, i):
                self.sem, self.sig, self.run, self.i, self.c = sig.sem, sig, run, i, 0

            def one(self):
                self.c += 1
                return 1

            def so_far(self):
                return self.sig.at(self.run, self.i, self.c)

            def close(self):
                assert self.c == self.sig.per, (self.c, self.sig.per)

        def stand(eng):
            eng.sem_inc(stood, 1)

        def layernorm(dve, link, i, ready, run, have_mv, have_rstd, second=None, rr=None):
            for j in range(TPI):
                dve.bn_stats(stats[:, j, :], X[:, bass.ds(i * TPI + j, 1), :].rearrange("p a d -> p (a d)")).then_inc(link.sem, link.one())
            dve.wait_ge(link.sem, link.so_far())
            stand(dve)
            for j in range(TPI):
                ins = dve.bn_aggr(mv[:, j, :], stats[:, j, :])
                if j < TPI - 1:
                    ins.then_inc(link.sem, link.one())
            ins.then_inc(have_mv.sem, 1)
            dve.wait_ge(have_rstd.sem, have_rstd.at(run if rr is None else rr, i))
            scale = rstd if second is None else rstd2
            for j in range(TPI):
                dve.tensor_scalar(XN[:, j, :], X[:, bass.ds(i * TPI + j, 1), :].rearrange("p a d -> p (a d)"),
                                  mv[:, j, 0:1], scale[:, j:j + 1],
                                  ALU.subtract, ALU.mult).then_inc(ready.sem, 1)

        def inverse_deviations(pool, i, run, have_mv, have_rstd, second=None, rr=None):
            rr = run if rr is None else rr
            half = minus_half[:, 0:TPI]

            def done(k):
                pool.wait_ge(have_rstd.sem, have_rstd.at(rr, i, k))
                stand(pool)

            pool.wait_ge(have_mv.sem, have_mv.at(run, i))
            stand(pool)
            pool.tensor_scalar(rstd[:], mv[:, :, 1], EPS, None, ALU.add).then_inc(have_rstd.sem, 1)
            done(1)
            pool.tensor_tensor(rstd[:], rstd[:], half, ALU.pow).then_inc(have_rstd.sem, 1)
            if second is not None:
                done(2)
                pool.tensor_tensor(rstd2[:], rstd[:], rstd[:], ALU.mult).then_inc(have_rstd.sem, 1)
                done(3)
                pool.tensor_tensor(rstd2[:], rstd2[:], mv[:, :, 1], ALU.mult).then_inc(have_rstd.sem, 1)
                done(4)
                pool.tensor_scalar(rstd2[:], rstd2[:], second, None, ALU.add).then_inc(have_rstd.sem, 1)
                done(5)
                pool.tensor_tensor(rstd2[:], rstd2[:], half, ALU.pow).then_inc(have_rstd.sem, 1)
                done(6)
                pool.tensor_tensor(rstd2[:], rstd2[:], rstd[:], ALU.mult).then_inc(have_rstd.sem, 1)

        used[0] = 0
        QKV = view([P, TPI, 192])
        SQ = view([P, TPI, 128])
        SS = view([P, TPI, 16])
        RN = view([P, TPI, 16])
        QN = view([P, 2, TPI, 8, DH])
        R1 = view([P, 64, DH])
        HML = view([P, 64, 3, DH], BF16)
        Qs = view([P, 32, HROWS], BF16)
        Ks = view([P, 32, HROWS], BF16)
        QT = view([P, 2, 4, SEQ], BF16)
        KT = view([P, 2, 4, SEQ], BF16)
        VP = view([P, TPI, 8, 32])
        PR = view([P, 2, 4, 384])
        REC = view([P, SEQ])
        OT = view([P, SEQ])
        a_link = signal("a_link", 14)
        a_mv = signal("a_mv")
        a_rstd = signal("a_rstd", 7)
        a_ss = signal("a_ss")
        a_xn = signal("a_xn", TPI)
        a_xt_ps = signal("a_xt_ps")
        a_xt = signal("a_xt")
        a_qkv_ps = signal("a_qkv_ps")
        a_qkv = signal("a_qkv", 2)
        a_split = signal("a_split")
        a_vp = signal("a_vp", 4)
        a_qrows = signal("a_qrows", 3)
        a_krows = signal("a_krows", 3)
        a_sqrt = signal("a_sqrt")
        a_tr = signal("a_tr", 4)
        a_qt = signal("a_qt", 4)
        a_sc = signal("a_sc", 4)
        a_exp = signal("a_exp", 4)
        a_av = signal("a_av", 4)
        a_rec = signal("a_rec")
        a_ot = signal("a_ot")
        a_y = signal("a_y")
        a_x = signal("a_x")

        def cos_vector(dve, layer):
            with dve.Fori(0, STEPS) as i:
                link = Order(a_link, 0, i)
                dve.wait_ge(a_xt_ps.sem, a_xt_ps.before(0, i))
                layernorm(dve, link, i, a_xn, 0, a_mv, a_rstd, second=EPS)
                dve.wait_ge(a_qkv.sem, a_qkv.at(0, i))
                dve.tensor_tensor(SQ, QKV[:, :, 0:128], QKV[:, :, 0:128], ALU.mult).then_inc(link.sem, link.one())
                dve.wait_ge(link.sem, link.so_far())
                dve.tensor_reduce(SS, SQ.rearrange("p t (h d) -> p t h d", d=DH), AX.X, ALU.add).then_inc(a_ss.sem, 1)
                dve.wait_ge(a_sqrt.sem, a_sqrt.at(0, i))
                dve.reciprocal(RN, RN).then_inc(link.sem, link.one())
                dve.wait_ge(link.sem, link.so_far())
                for s in range(2):
                    dve.tensor_tensor(
                        QN[:, s], QKV[:, :, 64 * s:64 * s + 64].rearrange("p t (h d) -> p t h d", d=DH),
                        RN[:, :, 8 * s:8 * s + 8].unsqueeze(3).broadcast_to([P, TPI, 8, DH]), ALU.mult).then_inc(link.sem, link.one())
                dve.wait_ge(link.sem, link.so_far())
                split3(dve, link, QN.rearrange("p s t h d -> p (s t h) d"), R1, HML, a_split, a_krows, 0, i)
                dve.wait_ge(a_split.sem, a_split.at(0, i))
                dve.wait_ge(a_tr.sem, a_tr.before(0, i))
                query_rows(dve, HML[:, 0:32], Qs, 32, a_qrows)

                def keys(b):
                    dve.wait_ge(a_tr.sem, a_tr.at(0, i, 2 * b + 2))
                    dve.tensor_copy(KT[:, b], psum_b16(2)).then_inc(a_qt.sem, 1)

                keys(0)
                keys(1)
                normalise(dve, 0, i, a_av, a_rec, a_ot)
                dve.wait_ge(a_y.sem, a_y.at(0, i))
                xs = X[:, bass.ds(i * TPI, TPI), :].rearrange("p t d -> p (t d)")
                dve.tensor_tensor(xs, psum[:, 0, :], xs, ALU.add).then_inc(a_x.sem, 1)
                dve.wait_ge(a_x.sem, a_x.at(0, i))
                link.close()

        def normalise(dve, run, n, av, rec, ot):
            dve.wait_ge(av.sem, av.at(run, n))
            dve.reciprocal(REC, psum[:, 3, 256:512]).then_inc(rec.sem, 1)
            dve.wait_ge(rec.sem, rec.at(run, n))
            dve.tensor_tensor(OT, psum[:, 3, 0:256], REC, ALU.mult).then_inc(ot.sem, 1)

        def psum_b16(bank):
            return psum[:, bank, :].bitcast(BF16).rearrange("p (c q) -> p c q", q=SEQ)

        def split3(dve, link, src, rest, parts, done, copied, run, i):
            dve.wait_ge(copied.sem, copied.before(run, i))
            dve.tensor_copy(parts[:, :, 0, :], src).then_inc(link.sem, link.one())
            dve.wait_ge(link.sem, link.so_far())
            dve.tensor_tensor(rest, src, parts[:, :, 0, :], ALU.subtract).then_inc(link.sem, link.one())
            dve.wait_ge(link.sem, link.so_far())
            dve.tensor_copy(parts[:, :, 1, :], rest).then_inc(link.sem, link.one())
            dve.wait_ge(link.sem, link.so_far())
            dve.tensor_tensor(parts[:, :, 2, :], rest, parts[:, :, 1, :], ALU.subtract).then_inc(done.sem, 1)

        def cos_scalar(act, layer):
            with act.Fori(0, STEPS) as i:
                act.wait_ge(a_xt_ps.sem, a_xt_ps.at(0, i))
                act.wait_ge(a_qkv_ps.sem, a_qkv_ps.before(0, i))
                act.activation(XT[:], psum[:, 0, :], ACT.Identity, scale=ln_w[:, 0:1], bias=ln_b[:, 0:1]).then_inc(a_xt.sem, 1)
                act.wait_ge(a_qkv_ps.sem, a_qkv_ps.at(0, i))
                act.wait_ge(a_split.sem, a_split.before(0, i))
                act.wait_ge(a_vp.sem, a_vp.before(0, i))
                for k in range(2):
                    act.activation(QKV[:, 2 * k:2 * k + 2, :], psum[:, 1 + k, 0:384].rearrange("p (t c) -> p t c", t=2),
                                   ACT.Copy).then_inc(a_qkv.sem, 1)
                act.wait_ge(a_ss.sem, a_ss.at(0, i))
                act.activation(RN, SS, ACT.Sqrt, bias=tiny[:, 0:1]).then_inc(a_sqrt.sem, 1)
                act.wait_ge(a_split.sem, a_split.at(0, i))
                act.wait_ge(a_tr.sem, a_tr.before(0, i))
                key_rows(act, HML[:, 32:64], Ks, a_krows)
                for b in range(2):
                    act.wait_ge(a_tr.sem, a_tr.at(0, i, 2 * b + 1))
                    act.activation(QT[:, b], psum_b16(1), ACT.Copy).then_inc(a_qt.sem, 1)
                for n in range(4):
                    if True:
                        act.wait_ge(a_sc.sem, a_sc.at(0, i, n + 1))
                        act.wait_ge(a_av.sem, a_av.at(0, i, n - 1))
                        act.activation(PR[:, n % 2], psum[:, 4:8, 0:384], ACT.Exp, scale=8.0).then_inc(a_exp.sem, 1)

        def cos_gpsimd(pool, layer):
            pool.memset(VP, 0.0).then_inc(constants, 1)
            pool.memset(Qs, 0.0).then_inc(constants, 1)
            pool.memset(Ks, 0.0).then_inc(constants, 1)
            pool.wait_ge(constants, 12)
            with pool.Fori(0, STEPS) as i:
                inverse_deviations(pool, i, 0, a_mv, a_rstd, second=EPS)
                pool.wait_ge(a_qkv.sem, a_qkv.at(0, i))
                pool.wait_ge(a_av.sem, a_av.before(0, i))
                stand(pool)
                for n in range(4):
                    pool.tensor_copy(VP[:, :, n:8:4, DH * n:DH * n + DH],
                                     QKV[:, :, 128:192].rearrange("p t (h d) -> p t h d", d=DH)[:, :, n:8:4, :]).then_inc(a_vp.sem, 1)
        def rows_of(x, u, k):
            return x[:, :, DH * u:DH * (u + k)].rearrange("p n (k d) -> p n k d", d=DH)

        def query_rows(dve, parts, rows, n, done):
            for part, u, k in ((0, 0, 3), (1, 3, 2), (2, 5, 1)):
                dve.tensor_copy(rows_of(rows, u, k), parts[:, :, part, :].unsqueeze(2).broadcast_to([P, n, k, DH])).then_inc(done.sem, 1)

        def key_rows(act, parts, rows, done):
            for u, k in ((0, 3), (3, 2), (5, 1)):
                act.activation(rows_of(rows, u, k), parts[:, :, 0:k, :], ACT.Copy).then_inc(done.sem, 1)

        def head_scores(pe, bank, kt, qt, k):
            pe.matmul(psum[:, bank, 0:256], kt[0:k, 0:128], qt[0:k, :], start=True, stop=False, skip_group_check=True)
            pe.matmul(psum[:, bank, 256:384], kt[0:k, 128:256], qt[0:k, 128:256], start=False, stop=False, skip_group_check=True)

        def mask_scores(pe, bank):
            v = psum[:, bank, :].rearrange("p (a q) -> p a q", q=256)[:, :, 0:128]
            return pe.matmul(v, identb[:], mask_kq[:].unsqueeze(1).broadcast_to([P, 2, P]), start=False, stop=True, skip_group_check=True)

        def weigh_values(pe, n, vp, pr):
            for half in range(2):
                for kt in range(2):
                    for r in range(4):
                        lo, hi = (0, 256) if kt == 0 else (128, 256)
                        mm = pe.matmul(psum[32 * r:32 * r + 32, 3, 256 * half + lo:256 * half + hi],
                                       ones4[:, n, :] if half else vp(kt, 4 * r + n),
                                       pr[:, r, 0:256] if kt == 0 else pr[:, r, 256:384],
                                       start=(n == half == kt == 0), stop=(n == 3 and half == kt == 1),
                                       skip_group_check=True, tile_position=(0, 32 * r))
            return mm

        def cos_tensor(pe, layer):
            pe.wait_ge(constants, 12)
            with pe.Fori(0, STEPS) as i:
                pe.wait_ge(a_xn.sem, a_xn.at(0, i))
                pe.wait_ge(a_x.sem, a_x.before(0, i))
                for j in range(TPI):
                    mm = pe.transpose(psum[:, 0, P * j:P * j + P], XN[:, j, :], ident[:])
                mm.then_inc(a_xt_ps.sem, 1)
                pe.wait_ge(a_xt.sem, a_xt.at(0, i))
                pe.wait_ge(a_qt.sem, a_qt.before(0, i))
                for j in range(TPI):
                    mm = pe.matmul(psum[:, 1 + j // 2, 192 * (j % 2):192 * (j % 2) + 192], XT[:, P * j:P * j + P],
                                   w_qkv[:], start=True, stop=True)
                mm.then_inc(a_qkv_ps.sem, 1)
                pe.wait_ge(a_qrows.sem, a_qrows.at(0, i))
                pe.wait_ge(a_krows.sem, a_krows.at(0, i))
                pe.wait_ge(a_qkv.sem, a_qkv.at(0, i))

                def transposes(b):
                    for s, rows_ in ((0, Qs), (1, Ks)):
                        if b:
                            pe.wait_ge(a_qt.sem, a_qt.at(0, i, 2))
                        for c in range(4):
                            for t in range(2):
                                mm = pe.transpose(psum_b16(1 + s)[:, c, P * t:P * t + P],
                                                  rows_[:, (2 * b + t) * 8 + 2 * c:(2 * b + t) * 8 + 2 * c + 2, :].rearrange("p h k -> p (h k)"),
                                                  identb[:])
                        mm.then_inc(a_tr.sem, 1)

                def scores(n):
                    pe.wait_ge(a_qt.sem, a_qt.at(0, i))
                    pe.wait_ge(a_exp.sem, a_exp.at(0, i, n))
                    for r in range(4):
                        b, h = r // 2, n + 4 * (r % 2)
                        c, lo = h // 2, HROWS * (h % 2)
                        head_scores(pe, 4 + r, KT[lo:lo + HROWS, b, c], QT[lo:lo + HROWS, b, c], SPLIT)
                    for r in range(4):
                        mm = mask_scores(pe, 4 + r)
                    mm.then_inc(a_sc.sem, 1)

                def values(n):
                    pe.wait_ge(a_exp.sem, a_exp.at(0, i, n + 1))
                    if n == 0:
                        pe.wait_ge(a_vp.sem, a_vp.at(0, i))
                        pe.wait_ge(a_ot.sem, a_ot.before(0, i))
                    weigh_values(pe, n, lambda kt, h: VP[:, 2 * (h // 8) + kt, h % 8, :], PR[:, n % 2]).then_inc(a_av.sem, 1)

                transposes(0)
                transposes(1)
                scores(0)
                for n in range(4):
                    if n < 3:
                        scores(n + 1)
                    values(n)
                pe.wait_ge(a_ot.sem, a_ot.at(0, i))
                for b in range(2):
                    for t in range(2):
                        mm = pe.matmul(psum[:, 0, P * (2 * b + t):P * (2 * b + t) + P], OT[:, P * t:P * t + P],
                                       w_out[:, b, :], start=True, stop=True, skip_group_check=True)
                mm.then_inc(a_y.sem, 1)

        def earlier(layer):
            return LAYERS[:layer].count(LAYERS[layer])

        def front_run(layer):
            return sum(k != "cos" for k in LAYERS[:layer])

        def rstd_run(r):
            return sum(k != "glru" for k in [k for k in LAYERS if k != "cos"][:r])

        f_link = signal("f_link", 7)
        f_mv = signal("f_mv")
        f_rstd = signal("f_rstd", 2)
        f_rstd2 = signal("f_rstd2", 7)
        f_xn = signal("f_xn", TPI)
        f_xt_ps = signal("f_xt_ps")
        f_xt = signal("f_xt")

        def front_stats(dve, i, r):
            link = Order(f_link, r, i)
            for j in range(TPI):
                dve.bn_stats(stats[:, j, :], X[:, bass.ds(i * TPI + j, 1), :].rearrange("p a d -> p (a d)")).then_inc(link.sem, link.one())
            dve.wait_ge(link.sem, link.so_far())
            stand(dve)
            for j in range(TPI):
                ins = dve.bn_aggr(mv[:, j, :], stats[:, j, :])
                if j < TPI - 1:
                    ins.then_inc(link.sem, link.one())
            ins.then_inc(f_mv.sem, 1)
            link.close()

        def front_scale(dve, i, r, have_rstd, rr, saved=None, saved_run=0):
            dve.wait_ge(f_xt_ps.sem, f_xt_ps.before(r, i))
            if saved is not None:
                dve.wait_ge(saved.sem, saved.before(saved_run, i))
            dve.wait_ge(have_rstd.sem, have_rstd.at(rr, i))
            scale = rstd2 if have_rstd is f_rstd2 else rstd
            for j in range(TPI):
                dve.tensor_scalar(XN[:, j, :], X[:, bass.ds(i * TPI + j, 1), :].rearrange("p a d -> p (a d)"),
                                  mv[:, j, 0:1], scale[:, j:j + 1], ALU.subtract, ALU.mult).then_inc(f_xn.sem, 1)

        def front_vector(dve, i, r, have_rstd=None, rr=None):
            front_stats(dve, i, r)
            front_scale(dve, i, r, f_rstd if have_rstd is None else have_rstd, rstd_run(r) if rr is None else rr)

        def front_tensor(pe, i, r):
            pe.wait_ge(f_xn.sem, f_xn.at(r, i))
            pe.wait_ge(f_xt.sem, f_xt.before(r, i))
            for j in range(TPI):
                mm = pe.transpose(psum[:, 0, P * j:P * j + P], XN[:, j, :], ident[:])
            mm.then_inc(f_xt_ps.sem, 1)

        used[0] = 0
        wg_t = weight("wg_t", [D, D])
        wc_t = weight("wc_t", [D, D])
        w1_t = weight("w1_t", [D, D])
        w2_t = weight("w2_t", [D, D])
        w3_t = weight("w3_t", [D, D])
        rms_w = weight("rms_w", [D, 1])
        ffn_w = weight("ffn_w", [D, 1])
        BETA = view([P, W])
        KEEP = view([P, W])
        HX = view([P, W])
        HSQ = view([P, W])
        RMS = view([P, W])
        HN = view([P, W])
        GATE = view([P, W])
        g_proj = signal("g_proj")
        g_beta = signal("g_beta", 2)
        g_link = signal("g_link", 4)
        g_hx = signal("g_hx", 2)
        g_sq = signal("g_sq")
        g_ms = signal("g_ms")
        g_rms = signal("g_rms")
        g_hn = signal("g_hn")
        g_up = signal("g_up")
        g_sig = signal("g_sig")
        g_gate = signal("g_gate")
        g_y = signal("g_y")
        g_x = signal("g_x")

        def glru_vector(dve, layer):
            r = front_run(layer)
            rr = 0
            with dve.Fori(0, STEPS) as i:
                front_vector(dve, i, r, f_rstd2, rr)
                link = Order(g_link, 0, i)
                dve.wait_ge(g_beta.sem, g_beta.at(0, i))
                dve.tensor_tensor(BETA, psum[:, 2, :], BETA, ALU.mult).then_inc(link.sem, link.one())
                dve.wait_ge(link.sem, link.so_far())
                dve.wait_ge(g_y.sem, g_y.before(0, i))
                stand(dve)
                for b in range(2):
                    s = slice(SEQ * b, SEQ * b + SEQ)
                    dve.tensor_tensor_scan(HX[:, s], KEEP[:, s], BETA[:, s], 0.0, ALU.mult, ALU.add).then_inc(g_hx.sem, 1)
                dve.wait_ge(g_rms.sem, g_rms.at(0, i))
                dve.reciprocal(RMS, RMS).then_inc(link.sem, link.one())
                dve.wait_ge(link.sem, link.so_far())
                dve.scalar_tensor_tensor(HN, HX, ffn_w[:, 0:1], RMS, ALU.mult, ALU.mult).then_inc(g_hn.sem, 1)
                dve.wait_ge(g_sig.sem, g_sig.at(0, i))
                dve.tensor_tensor(GATE, psum[:, 4, :], GATE, ALU.mult).then_inc(link.sem, link.one())
                dve.wait_ge(link.sem, link.so_far())
                dve.tensor_tensor(GATE, psum[:, 5, :], GATE, ALU.mult).then_inc(g_gate.sem, 1)
                dve.wait_ge(g_y.sem, g_y.at(0, i))
                xs = X[:, bass.ds(i * TPI, TPI), :].rearrange("p t d -> p (t d)")
                dve.tensor_tensor(xs, psum[:, 6, :], xs, ALU.add).then_inc(link.sem, link.one())
                dve.wait_ge(link.sem, link.so_far())
                link.close()

        def glru_scalar(act, layer):
            r = front_run(layer)
            with act.Fori(0, STEPS) as i:
                act.wait_ge(f_xt_ps.sem, f_xt_ps.at(r, i))
                act.wait_ge(g_proj.sem, g_proj.before(0, i))
                act.activation(XT[:], psum[:, 0, :], ACT.Copy, scale=rms_w[:, 0:1]).then_inc(f_xt.sem, 1)
                act.wait_ge(g_proj.sem, g_proj.at(0, i))
                act.wait_ge(g_hx.sem, g_hx.before(0, i))
                act.activation(BETA, psum[:, 1, :], ACT.Sigmoid).then_inc(g_beta.sem, 1)
                act.activation(KEEP, psum[:, 1, :], ACT.Sigmoid, scale=-1.0).then_inc(g_beta.sem, 1)
                act.wait_ge(g_hx.sem, g_hx.at(0, i))
                act.activation(HSQ, HX, ACT.Square).then_inc(g_sq.sem, 1)
                act.wait_ge(g_ms.sem, g_ms.at(0, i))
                act.wait_ge(g_hn.sem, g_hn.before(0, i))
                act.activation(RMS, psum[:, 3, :], ACT.Sqrt, bias=rms_eps[:, 0:1], scale=1.0 / D).then_inc(g_rms.sem, 1)
                act.wait_ge(g_up.sem, g_up.at(0, i))
                act.wait_ge(g_y.sem, g_y.before(0, i))
                act.activation(GATE, psum[:, 4, :], ACT.Sigmoid).then_inc(g_sig.sem, 1)

        def glru_gpsimd(pool, layer):
            r = front_run(layer)
            rr = 0
            with pool.Fori(0, STEPS) as i:
                inverse_deviations(pool, i, r, f_mv, f_rstd2, second=1e-6, rr=rr)

        def glru_tensor(pe, layer):
            r = front_run(layer)
            with pe.Fori(0, STEPS) as i:
                front_tensor(pe, i, r)
                pe.wait_ge(f_xt.sem, f_xt.at(r, i))
                pe.wait_ge(g_hx.sem, g_hx.before(0, i))
                pe.matmul(psum[:, 1, :], wg_t[:], XT[:], start=True, stop=True)
                pe.matmul(psum[:, 2, :], wc_t[:], XT[:], start=True, stop=True).then_inc(g_proj.sem, 1)
                pe.wait_ge(g_sq.sem, g_sq.at(0, i))
                pe.matmul(psum[:, 3, :], ones[:], HSQ, start=True, stop=True).then_inc(g_ms.sem, 1)
                pe.wait_ge(g_hn.sem, g_hn.at(0, i))
                pe.matmul(psum[:, 4, :], w1_t[:], HN, start=True, stop=True)
                pe.matmul(psum[:, 5, :], w3_t[:], HN, start=True, stop=True).then_inc(g_up.sem, 1)
                pe.wait_ge(g_gate.sem, g_gate.at(0, i))
                for j in range(TPI):
                    s = slice(P * j, P * j + P)
                    pe.matmul(psum[:, 6, s], HX[:, s], ident[:], start=True, stop=False, skip_group_check=True)
                    mm = pe.matmul(psum[:, 6, s], GATE[:, s], w2_t[:], start=False, stop=True, skip_group_check=True)
                mm.then_inc(g_y.sem, 1)

        used[0] = 0
        wr_t = weight("wr_t", [D, D])
        wk_t = weight("wk_t", [D, D])
        wv_t = weight("wv_t", [D, D])
        mu = weight("mu", [D, 2])
        one_minus_mu = sb("one_minus_mu", [D, 2])
        XS = view([P, 2, SEQ + 1])
        MIX = view([P, 2, 2, SEQ])
        R_ = view([P, W])
        KK = view([P, W])
        h_zero = semaphore("h_zero")
        h_prev = signal("h_prev", 2)
        h_mix = signal("h_mix", 2)
        h_rk = signal("h_rk")
        h_r = signal("h_r")
        h_k = signal("h_k")
        h_v = signal("h_v")
        h_link = signal("h_link", 2)

        def ffn_vector(dve, layer):
            r, run = front_run(layer), earlier(layer)
            dve.memset(XS[:, :, 0:1], 0.0).then_inc(h_zero, 1)
            dve.tensor_scalar(one_minus_mu[:], mu[:], -1.0, 1.0, ALU.mult, ALU.add).then_inc(h_zero, 1)
            with dve.Fori(0, STEPS) as i:
                front_vector(dve, i, r)
                link = Order(h_link, run, i)
                for m in range(2):
                    dve.wait_ge(h_prev.sem, h_prev.at(run, i, m + 1))
                    dve.scalar_tensor_tensor(MIX[:, m], XS[:, :, 1:SEQ + 1], mu[:, m:m + 1], MIX[:, m],
                                             ALU.mult, ALU.add).then_inc(h_mix.sem, 1)
                dve.wait_ge(h_rk.sem, h_rk.at(run, i))
                dve.tensor_scalar(KK, psum[:, 2, :], 0.0, None, ALU.max).then_inc(link.sem, link.one())
                dve.wait_ge(link.sem, link.so_far())
                dve.tensor_tensor(KK, KK, KK, ALU.mult).then_inc(h_k.sem, 1)
                dve.wait_ge(h_v.sem, h_v.at(run, i))
                dve.wait_ge(h_r.sem, h_r.at(run, i))
                dve.tensor_tensor(R_, psum[:, 3, :], R_, ALU.mult).then_inc(h_mul.sem, 1)
                dve.wait_ge(h_mul.sem, h_mul.at(run, i))
                xs = X[:, bass.ds(i * TPI, TPI), :].rearrange("p t d -> p (t d)")
                dve.tensor_tensor(xs, R_, xs, ALU.add).then_inc(link.sem, link.one())
                dve.wait_ge(link.sem, link.so_far())
                link.close()

        h_mul = signal("h_mul")

        def ffn_scalar(act, layer):
            r, run = front_run(layer), earlier(layer)
            act.wait_ge(h_zero, 2 * run + 2)
            with act.Fori(0, STEPS) as i:
                act.wait_ge(f_xt_ps.sem, f_xt_ps.at(r, i))
                act.wait_ge(h_mix.sem, h_mix.before(run, i))
                act.activation(XS[:, :, 1:SEQ + 1], psum[:, 0, :].rearrange("p (b q) -> p b q", b=2), ACT.Copy).then_inc(f_xt.sem, 1)
                act.wait_ge(f_xt.sem, f_xt.at(r, i))
                act.wait_ge(h_rk.sem, h_rk.before(run, i))
                for m in range(2):
                    act.activation(MIX[:, m], XS[:, :, 0:SEQ], ACT.Copy, scale=one_minus_mu[:, m:m + 1]).then_inc(h_prev.sem, 1)
                act.wait_ge(h_rk.sem, h_rk.at(run, i))
                act.wait_ge(h_mul.sem, h_mul.before(run, i))
                act.wait_ge(h_link.sem, h_link.before(run, i))
                act.activation(R_, psum[:, 1, :], ACT.Sigmoid).then_inc(h_r.sem, 1)

        def ffn_gpsimd(pool, layer):
            r, run = front_run(layer), earlier(layer)
            with pool.Fori(0, STEPS) as i:
                inverse_deviations(pool, i, r, f_mv, f_rstd, rr=rstd_run(r))

        def ffn_tensor(pe, layer):
            r, run = front_run(layer), earlier(layer)
            with pe.Fori(0, STEPS) as i:
                front_tensor(pe, i, r)
                pe.wait_ge(h_mix.sem, h_mix.at(run, i))
                pe.wait_ge(h_r.sem, h_r.before(run, i))
                pe.wait_ge(h_k.sem, h_k.before(run, i))
                for j in range(TPI):
                    s = slice(P * j % SEQ, P * j % SEQ + P)
                    pe.matmul(psum[:, 1, P * j:P * j + P], MIX[:, 0, j // 2, s], wr_t[:], start=True, stop=True)
                pe.matmul(psum[:, 2, :], wk_t[:], MIX[:, 1].rearrange("p b q -> p (b q)"), start=True, stop=True).then_inc(h_rk.sem, 1)
                pe.wait_ge(h_k.sem, h_k.at(run, i))
                pe.wait_ge(h_mul.sem, h_mul.before(run, i))
                for j in range(TPI):
                    mm = pe.matmul(psum[:, 3, P * j:P * j + P], KK[:, P * j:P * j + P], wv_t[:], start=True, stop=True)
                mm.then_inc(h_v.sem, 1)

        used[0] = 0
        E2 = 2
        STATE = 16
        TAPS = 4
        w_in = weight("w_in", [D, 2 * E2, P])
        b_in = weight("b_in", [P, 2 * E2])
        conv_w = weight("conv_w", [P, E2, TAPS])
        conv_b = weight("conv_b", [P, E2])
        m_a = weight("m_a", [P, E2, STATE])
        m_ct = weight("m_ct", [STATE, E2, P])
        m_d = weight("m_d", [P, E2])
        m_wo = weight("m_wo", [P, E2, D])
        m_bo = weight("m_bo", [1, D])
        XP = view([P, E2, 2, TAPS - 1 + SEQ])
        XCS = view([P, E2, 2, SEQ])
        XC = view([P, E2, TOK])
        Z = view([P, E2, TOK])
        U16 = view([STATE, NSEQ, SEQ])
        U = view([P, 2, SEQ])
        H = view([P, 2, SEQ])
        H16 = view([STATE, NSEQ, SEQ])
        YM = view([P, E2, W])
        HALF = NSEQ // 2
        m_zero = semaphore("m_zero")
        m_in = signal("m_in")
        m_xp = signal("m_xp", 4)
        m_conv = signal("m_conv", 8)
        m_u_ps = signal("m_u_ps")
        m_u = signal("m_u")
        m_spread = semaphore("m_spread")
        m_h = semaphore("m_h")
        m_gather = semaphore("m_gather")
        m_y_ps = signal("m_y_ps")
        m_ym = signal("m_ym", 4)
        m_out = signal("m_out")
        m_x = signal("m_x")

        def mamba_vector(dve, layer):
            r = front_run(layer)
            dve.memset(XP[:, :, :, 0:TAPS - 1], 0.0).then_inc(m_zero, 1)
            with dve.Fori(0, STEPS) as i:
                front_vector(dve, i, r)
                dve.wait_ge(m_u_ps.sem, m_u_ps.before(0, i))
                dve.wait_ge(m_xc.sem, m_xc.before(0, i))
                dve.wait_ge(m_xp.sem, m_xp.at(0, i, 2))
                for k in range(TAPS):
                    if k:
                        dve.wait_ge(m_conv.sem, m_conv.at(0, i, 2 * k))
                    for e in range(E2):
                        if k == 0:
                            ins = dve.tensor_scalar(XCS[:, e], XP[:, e, :, 0:SEQ], conv_w[:, e, 0:1], conv_b[:, e:e + 1], ALU.mult, ALU.add)
                        else:
                            ins = dve.scalar_tensor_tensor(XCS[:, e], XP[:, e, :, k:k + SEQ], conv_w[:, e, k:k + 1], XCS[:, e], ALU.mult, ALU.add)
                        ins.then_inc(m_conv.sem, 1)
            with dve.Fori(0, STEPS) as i:
                dve.wait_ge(m_y_ps.sem, m_y_ps.at(0, i))
                dve.wait_ge(m_out.sem, m_out.before(0, i))
                ym = lambda e: YM[:, e, :]
                for e in range(E2):
                    dve.scalar_tensor_tensor(ym(e), XC[:, e, bass.ds(i * W, W)], m_d[:, e:e + 1], psum[:, 1 + e, :], ALU.mult, ALU.add).then_inc(m_ym.sem, 1)
                for e in range(E2):
                    dve.wait_ge(m_ym.sem, m_ym.at(0, i, e + 1))
                    dve.tensor_tensor(ym(e), ym(e), Z[:, e, bass.ds(i * W, W)], ALU.mult).then_inc(m_ym.sem, 1)
                dve.wait_ge(m_out.sem, m_out.at(0, i))
                xs = X[:, bass.ds(i * TPI, TPI), :].rearrange("p t d -> p (t d)")
                dve.tensor_tensor(xs, psum[:, 3, :], xs, ALU.add).then_inc(m_x.sem, 1)

        m_xc = signal("m_xc")

        def mamba_scalar(act, layer):
            r = front_run(layer)
            act.wait_ge(m_zero, 1)
            with act.Fori(0, STEPS) as i:
                act.wait_ge(f_xt_ps.sem, f_xt_ps.at(r, i))
                act.wait_ge(m_in.sem, m_in.before(0, i))
                act.activation(XT[:], psum[:, 0, :], ACT.Copy).then_inc(f_xt.sem, 1)
                act.wait_ge(m_in.sem, m_in.at(0, i))
                act.wait_ge(m_conv.sem, m_conv.before(0, i))
                for e in range(E2):
                    act.activation(XP[:, e, :, TAPS - 1:], psum[:, 1 + e, :].rearrange("p (b q) -> p b q", b=2),
                                   ACT.Identity, bias=b_in[:, e:e + 1]).then_inc(m_xp.sem, 1)
                for e in range(E2):
                    act.activation(Z[:, e, bass.ds(i * W, W)], psum[:, 1 + E2 + e, :], ACT.Sigmoid, bias=b_in[:, E2 + e:E2 + e + 1]).then_inc(m_xp.sem, 1)
                act.wait_ge(m_conv.sem, m_conv.at(0, i))
                act.activation(XC[:, :, bass.ds(i * W, W)], XCS.rearrange("p e b q -> p e (b q)"), ACT.Copy).then_inc(m_xc.sem, 1)
                act.wait_ge(m_u_ps.sem, m_u_ps.at(0, i))
                act.activation(U16[:, bass.ds(i * 2, 2), :], psum[0:STATE, 5, :].rearrange("p (b q) -> p b q", b=2), ACT.Copy).then_inc(m_u.sem, 1)
            act.wait_ge(m_spread, 16 * NSEQ)
            for g in range(2):
                act.activation(H[:, g, 0:1], U[:, g, 0:1], ACT.Tanh).then_inc(m_h, 1)
            for t in range(1, SEQ):
                for g in range(2):
                    act.wait_ge(m_h, 2 * t + g - 1)
                    act.activation(H[:, g, t:t + 1], U[:, g, t:t + 1], ACT.Tanh, bias=H[:, g, t - 1:t]).then_inc(m_h, 1)

        def mamba_gpsimd(pool, layer):
            r = front_run(layer)
            with pool.Fori(0, STEPS) as i:
                inverse_deviations(pool, i, r, f_mv, f_rstd, rr=rstd_run(r))
            pool.wait_ge(m_u.sem, m_u.end(0))
            for s in range(NSEQ):
                pool.dma_start(U[STATE * (s % HALF):STATE * (s % HALF) + STATE, s // HALF, :], U16[:, s, :]).then_inc(m_spread, 16)
            pool.wait_ge(m_h, 2 * SEQ)
            for s in range(NSEQ):
                pool.dma_start(H16[:, s, :], H[STATE * (s % HALF):STATE * (s % HALF) + STATE, s // HALF, :]).then_inc(m_gather, 16)

        def mamba_tensor(pe, layer):
            r = front_run(layer)
            with pe.Fori(0, STEPS) as i:
                front_tensor(pe, i, r)
                pe.wait_ge(f_xt.sem, f_xt.at(r, i))
                pe.wait_ge(m_xp.sem, m_xp.before(0, i))
                for e in range(2 * E2):
                    mm = pe.matmul(psum[:, 1 + e, :], w_in[:, e, :], XT[:], start=True, stop=True)
                mm.then_inc(m_in.sem, 1)
                pe.wait_ge(m_conv.sem, m_conv.at(0, i))
                pe.wait_ge(m_u.sem, m_u.before(0, i))
                for e in range(E2):
                    mm = pe.matmul(psum[0:STATE, 5, :], m_a[:, e, :], XCS[:, e].rearrange("p b q -> p (b q)"), start=(e == 0), stop=(e == E2 - 1))
                mm.then_inc(m_u_ps.sem, 1)
            pe.wait_ge(m_gather, 16 * NSEQ)
            with pe.Fori(0, STEPS) as i:
                pe.wait_ge(m_ym.sem, m_ym.before(0, i))
                for e in range(E2):
                    mm = pe.matmul(psum[:, 1 + e, :], m_ct[:, e, :], H16[:, bass.ds(i * 2, 2), :].rearrange("p b q -> p (b q)"), start=True, stop=True)
                mm.then_inc(m_y_ps.sem, 1)
                pe.wait_ge(m_ym.sem, m_ym.at(0, i))
                pe.wait_ge(m_x.sem, m_x.before(0, i))
                for j in range(TPI):
                    s = slice(P * j, P * j + P)
                    for e in range(E2):
                        pe.matmul(psum[:, 3, s], YM[:, e, s], m_wo[:, e, :], start=(e == 0), stop=False, skip_group_check=True)
                    mm = pe.matmul(psum[:, 3, s], ones[0:1, :], m_bo[:], start=False, stop=True, skip_group_check=True)
                mm.then_inc(m_out.sem, 1)

        used[0] = 0
        NH = 16
        w_qkvt = weight("w_qkvt", [D, 3 * D])
        w_ot = weight("w_ot", [D, D])
        cos = weight("cos", [P, TPI, DH // 2])
        sin = weight("sin", [P, 2, TPI, DH // 2])
        MROW = SPLIT
        SCORE_K = SPLIT + 3
        QKV3 = view([P, 3, TPI, D])
        RT = view([P, 2, TPI, NH, DH])
        RU = view([P, 2, TPI, NH, DH])
        RL = view([P, 2 * TPI * NH, DH])
        RH = view([P, 2 * TPI * NH, 3, DH], BF16)
        QS2 = view([P, TPI * NH, HROWS], BF16)
        KS2 = view([P, TPI * NH, HROWS], BF16)
        QT2 = view([P, 2, NH // 2, SEQ], BF16)
        KT2 = view([P, 2, NH // 2, SEQ], BF16)
        VP2 = view([P, TPI, NH, 32])
        PR2 = view([P, 2, 4, 384])
        REC2 = view([P, SEQ])
        OT2 = view([P, 2, SEQ])
        MX = view([P, TPI, NH])
        ML = view([P, TPI * NH])
        r_zero = semaphore("r_zero")
        r_link = signal("r_link", 10)
        r_qkv_ps = signal("r_qkv_ps")
        r_qkv = signal("r_qkv", TPI)
        r_split = signal("r_split")
        r_vp = signal("r_vp", 4)
        r_qrows = signal("r_qrows", 3)
        r_krows = signal("r_krows", 3)
        r_tr = signal("r_tr", 12)
        r_qt = signal("r_qt", 12)
        r_s1 = signal("r_s1", 8)
        r_max = signal("r_max", 8)
        r_mrows = signal("r_mrows", 5)
        r_sc = signal("r_sc", 8)
        r_exp = signal("r_exp", 8)
        r_av = signal("r_av", 8)
        r_rec = signal("r_rec", 2)
        r_ot = signal("r_ot", 2)
        r_y = signal("r_y")
        r_x = signal("r_x")

        def rope_vector(dve, layer):
            r = front_run(layer)
            with dve.Fori(0, STEPS) as i:
                front_vector(dve, i, r)
                link = Order(r_link, 0, i)
                dve.wait_ge(r_qkv.sem, r_qkv.at(0, i))
                for s in range(2):
                    x = QKV3[:, s].rearrange("p t (h d) -> p t h d", d=DH // 2)
                    xh = QKV3[:, s].rearrange("p t (h u d) -> p t h u d", u=2, d=DH // 2)
                    c = cos[:].unsqueeze(2).broadcast_to([P, TPI, 2 * NH, DH // 2])
                    dve.tensor_tensor(RT[:, s].rearrange("p t h (u d) -> p t (h u) d", u=2), x, c, ALU.mult).then_inc(link.sem, link.one())
                    for u in range(2):
                        sn = sin[:, u].unsqueeze(2).broadcast_to([P, TPI, NH, DH // 2])
                        dve.tensor_tensor(RU[:, s, :, :, 4 * u:4 * u + 4], xh[:, :, :, 1 - u, :], sn, ALU.mult).then_inc(link.sem, link.one())
                dve.wait_ge(link.sem, link.so_far())
                dve.tensor_tensor(RT, RT, RU, ALU.add).then_inc(link.sem, link.one())
                dve.wait_ge(link.sem, link.so_far())
                split3(dve, link, RT.rearrange("p s t h d -> p (s t h) d"), RL, RH, r_split, r_krows, 0, i)
                dve.wait_ge(r_split.sem, r_split.at(0, i))
                dve.wait_ge(r_tr.sem, r_tr.before(0, i))
                query_rows(dve, RH[:, 0:TPI * NH], QS2, TPI * NH, r_qrows)
                for g in range(8):
                    b, n = g // 4, g % 4
                    dve.wait_ge(r_s1.sem, r_s1.at(0, i, g + 1))
                    dve.tensor_reduce(MX[:, 2 * b, n:NH:4], psum[:, 4:8, 0:128], AX.X, ALU.max, negate=True)
                    dve.tensor_reduce(MX[:, 2 * b + 1, n:NH:4], psum[:, 4:8, 128:384], AX.X, ALU.max, negate=True).then_inc(r_max.sem, 1)
                dve.drain()
                dve.wait_ge(r_max.sem, r_max.at(0, i))
                m = MX.rearrange("p t h -> p (t h)")
                row = lambda k: QS2[:, :, MROW + k]
                dve.wait_ge(r_tr.sem, r_tr.at(0, i, 8))
                dve.tensor_copy(row(0), m).then_inc(r_mrows.sem, 1)
                dve.wait_ge(r_mrows.sem, r_mrows.at(0, i, 1))
                dve.tensor_tensor(ML, m, row(0), ALU.subtract).then_inc(r_mrows.sem, 1)
                dve.wait_ge(r_mrows.sem, r_mrows.at(0, i, 2))
                dve.tensor_copy(row(1), ML).then_inc(r_mrows.sem, 1)
                dve.wait_ge(r_mrows.sem, r_mrows.at(0, i, 3))
                dve.tensor_tensor(ML, ML, row(1), ALU.subtract).then_inc(r_mrows.sem, 1)
                dve.wait_ge(r_mrows.sem, r_mrows.at(0, i, 4))
                dve.tensor_copy(row(2), ML).then_inc(r_mrows.sem, 1)
                for b in range(2):
                    dve.wait_ge(r_av.sem, r_av.at(0, i, 4 * b + 4))
                    dve.reciprocal(REC2, psum[:, 3, 256:512]).then_inc(r_rec.sem, 1)
                    dve.wait_ge(r_rec.sem, r_rec.at(0, i, b + 1))
                    dve.wait_ge(r_y.sem, r_y.before(0, i))
                    dve.tensor_tensor(OT2[:, b], psum[:, 3, 0:256], REC2, ALU.mult).then_inc(r_ot.sem, 1)
                    dve.wait_ge(r_ot.sem, r_ot.at(0, i, b + 1))
                dve.wait_ge(r_y.sem, r_y.at(0, i))
                xs = X[:, bass.ds(i * TPI, TPI), :].rearrange("p t d -> p (t d)")
                dve.tensor_tensor(xs, psum[:, 2, :], xs, ALU.add).then_inc(r_x.sem, 1)
                link.close()

        def rope_scalar(act, layer):
            r = front_run(layer)
            with act.Fori(0, STEPS) as i:
                act.wait_ge(f_xt_ps.sem, f_xt_ps.at(r, i))
                act.wait_ge(r_qkv_ps.sem, r_qkv_ps.before(0, i))
                act.activation(XT[:], psum[:, 0, :], ACT.Copy).then_inc(f_xt.sem, 1)
                act.wait_ge(r_qkv_ps.sem, r_qkv_ps.at(0, i))
                act.wait_ge(r_split.sem, r_split.before(0, i))
                act.wait_ge(r_vp.sem, r_vp.before(0, i))
                for j in range(TPI):
                    act.activation(QKV3[:, :, j, :], psum[:, 4 + j, 0:384].rearrange("p (s c) -> p s c", s=3), ACT.Copy).then_inc(r_qkv.sem, 1)
                act.wait_ge(r_split.sem, r_split.at(0, i))
                act.wait_ge(r_tr.sem, r_tr.before(0, i))
                key_rows(act, RH[:, TPI * NH:], KS2, r_krows)
                for k in range(12):
                    act.wait_ge(r_tr.sem, r_tr.at(0, i, k + 1))
                    if k < 8:
                        b, hh, t = k // 4, k // 2 % 2, (QT2, KT2)[k % 2]
                    else:
                        b, hh, t = (k - 8) // 2, k % 2, QT2
                        act.wait_ge(r_s1.sem, r_s1.at(0, i))
                    act.activation(t[:, b, 4 * hh:4 * hh + 4], psum_b16(1 + k % 2), ACT.Copy).then_inc(r_qt.sem, 1)
                for g in range(8):
                    act.wait_ge(r_sc.sem, r_sc.at(0, i, g + 1))
                    act.wait_ge(r_av.sem, r_av.at(0, i, g - 1))
                    act.activation(PR2[:, g % 2], psum[:, 4:8, 0:384], ACT.Exp, scale=DH ** -0.5).then_inc(r_exp.sem, 1)

        def rope_gpsimd(pool, layer):
            r = front_run(layer)
            pool.memset(VP2, 0.0).then_inc(r_zero, 1)
            pool.memset(QS2, 0.0).then_inc(r_zero, 1)
            pool.memset(KS2, 0.0).then_inc(r_zero, 1)
            pool.wait_ge(r_zero, 3)
            pool.memset(KS2[:, :, MROW:MROW + 3], 1.0).then_inc(r_zero, 1)
            pool.wait_ge(r_zero, 4)
            with pool.Fori(0, STEPS) as i:
                inverse_deviations(pool, i, r, f_mv, f_rstd, rr=rstd_run(r))
                pool.wait_ge(r_qkv.sem, r_qkv.at(0, i))
                pool.wait_ge(r_av.sem, r_av.before(0, i))
                stand(pool)
                for n in range(4):
                    pool.tensor_copy(VP2[:, :, n:NH:4, DH * n:DH * n + DH],
                                     QKV3[:, 2].rearrange("p t (h d) -> p t h d", d=DH)[:, :, n:NH:4, :]).then_inc(r_vp.sem, 1)

        def rope_tensor(pe, layer):
            r = front_run(layer)
            pe.wait_ge(r_zero, 4)
            with pe.Fori(0, STEPS) as i:
                front_tensor(pe, i, r)
                pe.wait_ge(f_xt.sem, f_xt.at(r, i))
                pe.wait_ge(r_exp.sem, r_exp.before(0, i))
                for j in range(TPI):
                    mm = pe.matmul(psum[:, 4 + j, 0:384], XT[:, P * j:P * j + P], w_qkvt[:], start=True, stop=True)
                mm.then_inc(r_qkv_ps.sem, 1)
                pe.wait_ge(r_qrows.sem, r_qrows.at(0, i))
                pe.wait_ge(r_krows.sem, r_krows.at(0, i))
                pe.wait_ge(r_x.sem, r_x.before(0, i))

                def transposes(k, b, hh, rows):
                    if k >= 2:
                        pe.wait_ge(r_qt.sem, r_qt.at(0, i, k - 1))
                    for c in range(4):
                        for t in range(2):
                            h = (2 * b + t) * NH + 8 * hh + 2 * c
                            mm = pe.transpose(psum_b16(1 + k % 2)[:, c, P * t:P * t + P],
                                              rows[:, h:h + 2, :].rearrange("p h k -> p (h k)"), identb[:])
                    mm.then_inc(r_tr.sem, 1)

                def head(t, b, h):
                    return t[HROWS * (h % 2):HROWS * (h % 2) + HROWS, b, h // 2]

                for k in range(8):
                    transposes(k, k // 4, k // 2 % 2, (QS2, KS2)[k % 2])
                pe.wait_ge(r_qkv.sem, r_qkv.at(0, i))
                for g in range(8):
                    b, n = g // 4, g % 4
                    if g % 4 == 0:
                        pe.wait_ge(r_qt.sem, r_qt.at(0, i, 4 * b + 4))
                    pe.wait_ge(r_max.sem, r_max.at(0, i, g))
                    for rr in range(4):
                        q, kk = head(QT2, b, n + 4 * rr), head(KT2, b, n + 4 * rr)
                        pe.matmul(psum[:, 4 + rr, 0:128], q[0:SPLIT, 0:128], kk[0:SPLIT, 0:128], start=True, stop=False, skip_group_check=True)
                        pe.matmul(psum[:, 4 + rr, 128:384], q[0:SPLIT, 128:256], kk[0:SPLIT, :], start=False, stop=False, skip_group_check=True)
                    for rr in range(4):
                        v = psum[:, 4 + rr, 0:384].rearrange("p (a q) -> p a q", q=P)[:, 0:3:2, :]
                        mm = pe.matmul(v, identb[:], mask_qk[:].unsqueeze(1).broadcast_to([P, 2, P]), start=False, stop=True, skip_group_check=True)
                    mm.then_inc(r_s1.sem, 1)
                pe.wait_ge(r_mrows.sem, r_mrows.at(0, i))
                for k in range(8, 12):
                    transposes(k, (k - 8) // 2, k % 2, QS2)

                def scores(g):
                    b, n = g // 4, g % 4
                    pe.wait_ge(r_qt.sem, r_qt.at(0, i, 10 + 2 * b))
                    pe.wait_ge(r_exp.sem, r_exp.at(0, i, g))
                    for rr in range(4):
                        head_scores(pe, 4 + rr, head(KT2, b, n + 4 * rr), head(QT2, b, n + 4 * rr), SCORE_K)
                    for rr in range(4):
                        mm = mask_scores(pe, 4 + rr)
                    mm.then_inc(r_sc.sem, 1)

                def values(g):
                    b, n = g // 4, g % 4
                    pe.wait_ge(r_exp.sem, r_exp.at(0, i, g + 1))
                    if g == 0:
                        pe.wait_ge(r_vp.sem, r_vp.at(0, i))
                    if n == 0:
                        pe.wait_ge(r_ot.sem, r_ot.at(0, i, b))
                    weigh_values(pe, n, lambda kt, h: VP2[:, 2 * b + kt, h, :], PR2[:, g % 2]).then_inc(r_av.sem, 1)

                scores(0)
                for g in range(8):
                    if g < 7:
                        scores(g + 1)
                    values(g)
                pe.wait_ge(r_ot.sem, r_ot.at(0, i))
                for j in range(TPI):
                    mm = pe.matmul(psum[:, 2, P * j:P * j + P], OT2[:, j // 2, P * (j % 2):P * (j % 2) + P], w_ot[:],
                                   start=True, stop=True, skip_group_check=True)
                mm.then_inc(r_y.sem, 1)

        NE = 160
        TOPK = 8
        INTER = 64
        ROUTED_SCALE = 2.5
        SLOT_TILES = -(-(TOK * TOPK // P + NE) // 8) * 8
        GROUP = 4
        GROUPS = SLOT_TILES // GROUP
        UNROLL = 4
        GSTEPS = GROUPS // UNROLL
        assert GROUPS % UNROLL == 0 and GROUPS <= P
        EW = INTER + D
        router_t = weight("router_t", [D, NE])
        e_bias = weight("e_bias", [1, NE])
        sh_gate = weight("sh_gate", [D, INTER])
        sh_down = weight("sh_down", [INTER, D])
        earlier_tokens = weight("earlier_tokens", [P, P], BF16)
        other_tokens = weight("other_tokens", [P, P], BF16)
        slot_tile = weight("slot_tile", [P, GROUP])
        onesb = sb("onesb", [P, P], BF16)
        zeros = sb("zeros", [P, 512])
        slot_rows = nc.dram_tensor("slot_rows", (SLOT_TILES * P, D), F32).ap()
        slot_results = nc.dram_tensor("slot_results", (SLOT_TILES * P, D), F32).ap()
        normalised = nc.dram_tensor("normalised", (TOK, D), F32).ap()
        M8 = sb("M8", [P, TPI, TOPK])
        SUM = sb("SUM", [P, TPI])
        S8 = sb("S8", [P, TPI, TOPK])
        W8 = sb("W8", [P, TPI, TOPK])
        SLOTS = sb("SLOTS", [P, TILES, TOPK], I32)
        WEIGHTS = sb("WEIGHTS", [P, TILES, TOPK])
        SLOTS_NOW = sb("SLOTS_NOW", [P, TPI, TOPK], I32)
        EXPERT_COL = sb("EXPERT_COL", [P, GROUP])
        EXPERT = sb("EXPERT", [1, GROUP, P], I32)
        used[0] = 0
        MASK = view([P, TILES, NE], BF16)
        COMB = view([P, TILES, NE])
        step_part = used[0]
        PROB = view([P, TPI, NE])
        REST = view([P, TPI, NE])
        SG = view([P, TPI * INTER])
        HE = view([P, TPI * INTER])
        HT = view([INTER, W])
        used[0] = step_part
        XNS = view([P, TPI, D])
        SLOTM = view([P, TPI, NE])
        JUNK = view([P, TOPK, NE], BF16)
        used[0] = step_part
        COUNT = view([P, NE], I32)
        NTILES = view([P, NE])
        INCL = view([P, NE])
        FIRST = view([P, NE])
        JUNK2 = view([P, GROUP, NE], BF16)
        used[0] = max(used[0], step_part + 2 * TPI * NE + 2 * TPI * INTER + W)
        XSB = view([P, UNROLL, GROUP, D])
        EWB = view([P, UNROLL, GROUP, EW])
        XSBT = view([P, 2, GROUP * P])
        SGB = view([P, 2, GROUP * INTER])
        HEB = view([P, 2, GROUP * INTER])
        HTB = view([INTER, 2, GROUP * P])
        YSB = view([P, UNROLL, GROUP, D])
        GATHERED = view([P, TPI, TOPK, D])
        e_ready = semaphore("e_ready")
        cleared = semaphore("cleared")
        e_saved = signal("e_saved", 16)
        e_lg = signal("e_lg")
        e_prob = signal("e_prob", 2)
        e_link = signal("e_link", 2 * TPI + 5)
        e_comb = signal("e_comb")
        e_mask = signal("e_mask")
        e_x = signal("e_x")
        e_h = signal("e_h")
        e_sg = signal("e_sg")
        e_he = signal("e_he")
        e_tr = signal("e_tr")
        e_ht = signal("e_ht")
        e_y = signal("e_y")
        e_cnt = signal("e_cnt")
        o_link = signal("o_link", 9, 1)
        o_row = signal("o_row", 1, 1)
        o_expert = signal("o_expert", 1, 1)
        s_xn = [signal(f"s_xn{j}", 16) for j in range(TPI)]
        s_a = signal("s_a", TPI)
        s_slotm = signal("s_slotm", TPI)
        s_s8 = signal("s_s8", TPI)
        s_idx = signal("s_idx", TPI)
        s_keep = signal("s_keep", TPI)
        s_w = signal("s_w", TPI * TOPK)
        s_wk = signal("s_wk", TPI)
        s_scat = [signal(f"s_scat{j}", 16 * TOPK, start=0) for j in range(TPI)]
        c_ld = [signal(f"c_ld{p}", 16, GSTEPS, start=0) for p in range(UNROLL)]
        c_ew = [[signal(f"c_ew{h}{p}", 16 * GROUP // 2, GSTEPS) for p in range(UNROLL)] for h in range(2)]
        c_st = [signal(f"c_st{p}", 16, GSTEPS) for p in range(UNROLL)]
        c_tr = signal("c_tr", UNROLL, GSTEPS)
        c_xt = signal("c_xt", UNROLL, GSTEPS)
        c_h = signal("c_h", UNROLL, GSTEPS)
        c_sg = signal("c_sg", UNROLL, GSTEPS)
        c_he = signal("c_he", UNROLL, GSTEPS)
        c_htr = signal("c_htr", UNROLL, GSTEPS)
        c_ht = signal("c_ht", UNROLL, GSTEPS)
        c_y = signal("c_y", UNROLL, GSTEPS)
        c_ysb = signal("c_ysb", UNROLL, GSTEPS)
        g_idx = signal("g_idx", 2 * TPI)
        g_rows = [signal(f"g_rows{j}", 16 * TOPK, start=0) for j in range(TPI)]
        g_sum = signal("g_sum", TPI * TOPK, start=START + TPI * TOPK)

        def moe_vector(dve, layer):
            r, run = front_run(layer), earlier(layer)

            def route(i, last):
                front_scale(dve, i, r, f_rstd, rstd_run(r), e_saved, run)
                if not last:
                    front_stats(dve, i + 1, r)
                dve.wait_ge(e_sg.sem, e_sg.at(run, i))
                dve.wait_ge(e_tr.sem, e_tr.before(run, i))
                dve.tensor_tensor(HE, psum[:, 1, 0:TPI * INTER], SG, ALU.mult).then_inc(e_he.sem, 1)
                link = Order(e_link, run, i)
                dve.wait_ge(e_prob.sem, e_prob.at(run, i))
                stand(dve)
                for j in range(TPI):
                    dve.max(M8[:, j], PROB[:, j]).then_inc(link.sem, link.one())
                dve.wait_ge(link.sem, link.so_far())
                stand(dve)
                dve.tensor_reduce(SUM[:], M8[:], AX.X, ALU.add).then_inc(link.sem, link.one())
                for j in range(TPI):
                    dve.match_replace(REST[:, j], M8[:, j], PROB[:, j], -1.0).then_inc(link.sem, link.one())
                dve.wait_ge(link.sem, link.so_far())
                dve.tensor_scalar(SUM[:], SUM[:], 1e-9, None, ALU.add).then_inc(link.sem, link.one())
                dve.tensor_scalar(MASK[:, bass.ds(i * TPI, TPI), :], REST, 0.0, None, ALU.is_lt).then_inc(e_mask.sem, 1)
                dve.wait_ge(link.sem, link.so_far())
                dve.reciprocal(SUM[:], SUM[:]).then_inc(link.sem, link.one())
                dve.wait_ge(e_mask.sem, e_mask.at(run, i))
                dve.scalar_tensor_tensor(REST, REST, 0.0, PROB, ALU.is_lt, ALU.mult).then_inc(link.sem, link.one())
                dve.wait_ge(link.sem, link.so_far())
                dve.tensor_scalar(SUM[:], SUM[:], ROUTED_SCALE, None, ALU.mult).then_inc(link.sem, link.one())
                dve.wait_ge(link.sem, link.so_far())
                dve.tensor_tensor(COMB[:, bass.ds(i * TPI, TPI), :], REST, SUM[:].unsqueeze(2).broadcast_to([P, TPI, NE]), ALU.mult).then_inc(e_comb.sem, 1)
                dve.wait_ge(e_y.sem, e_y.at(run, i))
                xs = X[:, bass.ds(i * TPI, TPI), :].rearrange("p t d -> p (t d)")
                dve.tensor_tensor(xs, psum[:, 5, :], xs, ALU.add).then_inc(e_x.sem, 1)
                link.close()

            front_stats(dve, 0, r)
            with dve.Fori(0, STEPS - 1) as i:
                route(i, False)
            route(STEPS - 1, True)

            link = Order(o_link, run, 0)
            dve.wait_ge(e_cnt.sem, e_cnt.end(run))
            dve.wait_ge(e_comb.sem, e_comb.end(run))
            dve.tensor_copy(COUNT, psum[:, 2, 0:NE]).then_inc(link.sem, link.one())
            dve.wait_ge(link.sem, link.so_far())
            dve.tensor_scalar(COUNT, COUNT, P - 1, None, ALU.add).then_inc(link.sem, link.one())
            dve.wait_ge(link.sem, link.so_far())
            dve.tensor_scalar(COUNT, COUNT, 7, None, ALU.arith_shift_right).then_inc(link.sem, link.one())
            dve.wait_ge(link.sem, link.so_far())
            dve.tensor_copy(NTILES, COUNT).then_inc(link.sem, link.one())
            dve.wait_ge(link.sem, link.so_far())
            dve.tensor_tensor_scan(INCL, ones_row[:], NTILES, 0.0, ALU.mult, ALU.add).then_inc(link.sem, link.one())
            dve.wait_ge(link.sem, link.so_far())
            dve.tensor_tensor(FIRST, INCL, NTILES, ALU.subtract).then_inc(link.sem, link.one())
            for q in range(GROUP):
                ins = dve.scalar_tensor_tensor(JUNK2[:, q], INCL, slot_tile[:, q:q + 1], ones_row[:], ALU.is_le, ALU.mult, accum_out=EXPERT_COL[:, q:q + 1])
            ins.then_inc(link.sem, link.one())
            dve.drain()
            dve.wait_ge(link.sem, link.so_far())
            dve.tensor_scalar(FIRST, FIRST, float(P), None, ALU.mult).then_inc(link.sem, link.one())
            dve.tensor_scalar(EXPERT_COL[:], EXPERT_COL[:], NE - 1.0, None, ALU.min).then_inc(link.sem, link.one())
            dve.wait_ge(o_row.sem, o_row.at(run, 0))
            dve.tensor_copy(EXPERT[:], psum[0:1, 4, :].rearrange("p (q g) -> p q g", q=GROUP)).then_inc(o_expert.sem, 1)
            link.close()

            def place(i, first):
                for j in range(TPI):
                    t = bass.ds(i * TPI + j, 1)
                    dve.wait_ge(s_a.sem, s_a.at(run, i, j + 1))
                    dve.scalar_tensor_tensor(SLOTM[:, j], psum[:, 2, 0:NE], 1.0, MASK[:, t, :].rearrange("p a e -> p (a e)"),
                                             ALU.add, ALU.mult).then_inc(s_slotm.sem, 1)
                    dve.wait_ge(s_slotm.sem, s_slotm.at(run, i, j + 1))
                    stand(dve)
                    dve.max(S8[:, j], SLOTM[:, j]).then_inc(s_s8.sem, 1)
                    dve.wait_ge(s_s8.sem, s_s8.at(run, i, j + 1))
                    if not first:
                        dve.wait_ge(s_scat[j].sem, s_scat[j].before(run, i))
                    dve.tensor_scalar(SLOTS_NOW[:, j], S8[:, j], -1.0, None, ALU.add).then_inc(s_idx.sem, 1)
                    dve.tensor_scalar(SLOTS[:, t, :].rearrange("p a k -> p (a k)"), S8[:, j], -1.0, None, ALU.add).then_inc(s_keep.sem, 1)
                    dve.wait_ge(s_w.sem, s_w.at(run, i, TOPK * j))
                    for k in range(TOPK):
                        dve.scalar_tensor_tensor(JUNK[:, k], SLOTM[:, j], S8[:, j, k:k + 1], COMB[:, t, :].rearrange("p a e -> p (a e)"),
                                                 ALU.is_equal, ALU.mult, accum_out=W8[:, j, k:k + 1]).then_inc(s_w.sem, 1)
                    dve.wait_ge(s_w.sem, s_w.at(run, i, TOPK * j + TOPK))
                    dve.tensor_copy(WEIGHTS[:, t, :].rearrange("p a k -> p (a k)"), W8[:, j]).then_inc(s_wk.sem, 1)

            place(0, True)
            with dve.Fori(1, STEPS) as i:
                place(i, False)

            def silu(g, p):
                dve.wait_ge(c_sg.sem, c_sg.at(run, g, p + 1))
                dve.wait_ge(c_htr.sem, c_htr.at(run, g, p - 1))
                dve.tensor_tensor(HEB[:, p % 2], psum[:, 2, 256 * (p % 2):256 * (p % 2) + 256], SGB[:, p % 2], ALU.mult).then_inc(c_he.sem, 1)

            def evacuate(g, p):
                dve.wait_ge(c_htr.sem, c_htr.at(run, g, p + 1))
                dve.wait_ge(c_y.sem, c_y.at(run, g, p - 1))
                dve.tensor_copy(HTB[:, p % 2], psum[0:INTER, 3 + p % 2, :]).then_inc(c_ht.sem, 1)

            def results(g, p):
                dve.wait_ge(c_y.sem, c_y.at(run, g, p + 1))
                dve.wait_ge(c_st[p].sem, c_st[p].before(run, g))
                dve.tensor_copy(YSB[:, p], psum[:, 5 + p % 2, :].rearrange("p (q d) -> p q d", q=GROUP)).then_inc(c_ysb.sem, 1)

            silu(0, 0)
            with dve.Fori(0, GSTEPS - 1) as g:
                for p in range(UNROLL):
                    evacuate(g, p)
                    silu(g + (p + 1) // UNROLL, (p + 1) % UNROLL)
                    results(g, p)
            for p in range(UNROLL):
                evacuate(GSTEPS - 1, p)
                if p < UNROLL - 1:
                    silu(GSTEPS - 1, p + 1)
                results(GSTEPS - 1, p)

            with dve.Fori(0, STEPS) as i:
                for j in range(TPI):
                    t = bass.ds(i * TPI + j, 1)
                    dve.wait_ge(s_keep.sem, s_keep.end(run))
                    dve.wait_ge(s_wk.sem, s_wk.end(run))
                    dve.tensor_copy(SLOTS_NOW[:, j], SLOTS[:, t, :].rearrange("p a k -> p (a k)")).then_inc(g_idx.sem, 1)
                for j in range(TPI):
                    t = bass.ds(i * TPI + j, 1)
                    x = X[:, t, :].rearrange("p a d -> p (a d)")
                    dve.tensor_copy(W8[:, j], WEIGHTS[:, t, :].rearrange("p a k -> p (a k)")).then_inc(g_idx.sem, 1)
                    dve.wait_ge(g_idx.sem, g_idx.at(run, i, TPI + j + 1))
                    dve.wait_ge(g_rows[j].sem, g_rows[j].at(run, i))
                    for k in range(TOPK):
                        if k:
                            dve.wait_ge(g_sum.sem, g_sum.at(run, i, TOPK * j + k))
                        dve.scalar_tensor_tensor(x, GATHERED[:, j, k], W8[:, j, k:k + 1], x, ALU.mult, ALU.add).then_inc(g_sum.sem, 1)
            dve.wait_ge(g_sum.sem, g_sum.end(run))

        def moe_scalar(act, layer):
            r, run = front_run(layer), earlier(layer)
            with act.Fori(0, STEPS) as i:
                act.wait_ge(f_xt_ps.sem, f_xt_ps.at(r, i))
                act.wait_ge(e_h.sem, e_h.before(run, i))
                act.activation(XT[:], psum[:, 0, :], ACT.Copy).then_inc(f_xt.sem, 1)
                act.wait_ge(e_lg.sem, e_lg.at(run, i))
                act.wait_ge(e_comb.sem, e_comb.before(run, i))
                for k in range(2):
                    act.activation(PROB[:, 2 * k:2 * k + 2, :], psum[:, 6 + k, 0:2 * NE].rearrange("p (t c) -> p t c", t=2), ACT.Sigmoid).then_inc(e_prob.sem, 1)
                act.wait_ge(e_h.sem, e_h.at(run, i))
                act.wait_ge(e_he.sem, e_he.before(run, i))
                act.activation(SG, psum[:, 1, 0:TPI * INTER], ACT.Sigmoid).then_inc(e_sg.sem, 1)
                act.wait_ge(e_tr.sem, e_tr.at(run, i))
                act.wait_ge(e_y.sem, e_y.before(run, i))
                act.activation(HT, psum[0:INTER, 3, :], ACT.Copy).then_inc(e_ht.sem, 1)

            def transposed(g, p):
                act.wait_ge(c_tr.sem, c_tr.at(run, g, p + 1))
                act.wait_ge(c_h.sem, c_h.at(run, g, p - 1))
                act.activation(XSBT[:, p % 2], psum[:, p % 2, :], ACT.Copy).then_inc(c_xt.sem, 1)

            def sigmoid(g, p):
                act.wait_ge(c_h.sem, c_h.at(run, g, p + 1))
                act.wait_ge(c_he.sem, c_he.at(run, g, p - 1))
                act.activation(SGB[:, p % 2], psum[:, 2, 256 * (p % 2):256 * (p % 2) + 256], ACT.Sigmoid).then_inc(c_sg.sem, 1)

            def ahead(g, p):
                act.wait_ge(c_y.sem, c_y.at(run, g, p - 1))
                stand(act)
                expert_weights(act, g + (p + 2) // UNROLL, (p + 2) % UNROLL, (2, 3))

            act.wait_ge(o_expert.sem, o_expert.at(run, 0))
            for p in range(2):
                expert_weights(act, 0, p, (2, 3))
            with act.Fori(0, GSTEPS - 1) as g:
                for p in range(UNROLL):
                    transposed(g, p)
                    ahead(g, p)
                    sigmoid(g, p)
            for p in range(UNROLL):
                transposed(GSTEPS - 1, p)
                if p < UNROLL - 2:
                    ahead(GSTEPS - 1, p)
                sigmoid(GSTEPS - 1, p)

        def moe_gpsimd(pool, layer):
            r, run = front_run(layer), earlier(layer)
            with pool.Fori(0, STEPS) as i:
                inverse_deviations(pool, i, r, f_mv, f_rstd, rr=rstd_run(r))
            pool.wait_ge(cleared, 16)
            with pool.Fori(0, STEPS) as i:
                for j in range(TPI):
                    pool.wait_ge(s_idx.sem, s_idx.at(run, i, j + 1))
                    pool.wait_ge(s_xn[j].sem, s_xn[j].at(run, i))
                    stand(pool)
                    for k in range(TOPK):
                        pool.indirect_dma_start(out=slot_rows, out_offset=bass.IndirectOffsetOnAxis(ap=SLOTS_NOW[:, j, k:k + 1], axis=0),
                                                in_=XNS[:, j], in_offset=None).then_inc(s_scat[j].sem, 16)
            for j in range(TPI):
                pool.wait_ge(s_scat[j].sem, s_scat[j].end(run))

            def load(g, p):
                pool.dma_start(XSB[:, p], rows_of_group(slot_rows, g * UNROLL + p)).then_inc(c_ld[p].sem, 16)

            for p in range(UNROLL):
                load(0, p)
            with pool.Fori(0, GSTEPS - 1) as g:
                for p in range(UNROLL):
                    pool.wait_ge(c_tr.sem, c_tr.at(run, g, p + 1))
                    stand(pool)
                    load(g + 1, p)
            for p in range(UNROLL):
                pool.wait_ge(c_st[p].sem, c_st[p].end(run))
            with pool.Fori(0, STEPS) as i:
                for j in range(TPI):
                    pool.wait_ge(g_idx.sem, g_idx.at(run, i, j + 1))
                    pool.wait_ge(g_sum.sem, g_sum.at(run, i, TOPK * (j + 1 - TPI)))
                    stand(pool)
                    for k in range(TOPK):
                        pool.indirect_dma_start(out=GATHERED[:, j, k], out_offset=None, in_=slot_results,
                                                in_offset=bass.IndirectOffsetOnAxis(ap=SLOTS_NOW[:, j, k:k + 1], axis=0)).then_inc(g_rows[j].sem, 16)

        def rows_of_group(dram, g):
            return dram[bass.ds(g * (GROUP * P), GROUP * P), :].rearrange("(q s) d -> s q d", q=GROUP)

        def expert_weights(eng, g, p, tiles):
            for q in tiles:
                e = eng.value_load(EXPERT[0:1, q, bass.ds(g * UNROLL + p, 1)], min_val=0, max_val=NE - 1)
                eng.dma_start(EWB[:, p, q], a["expert_w"][bass.ds(e * P, P), :]).then_inc(c_ew[q // 2][p].sem, 16)

        def moe_sync(sp, layer):
            r, run = front_run(layer), earlier(layer)
            with sp.Fori(0, STEPS) as i:
                sp.wait_ge(f_xn.sem, f_xn.at(r, i))
                sp.dma_start(normalised[bass.ds(i * W, W), :].rearrange("(t p) d -> p t d", p=P), XN[:]).then_inc(e_saved.sem, 16)
            sp.wait_ge(e_saved.sem, e_saved.end(run))
            sp.wait_ge(o_row.sem, o_row.at(run, 0))
            for j in range(TPI):
                sp.dma_start(XNS[:, j], normalised[P * j:P * j + P, :]).then_inc(s_xn[j].sem, 16)
            with sp.Fori(1, STEPS) as i:
                for j in range(TPI):
                    sp.wait_ge(s_scat[j].sem, s_scat[j].before(run, i))
                    sp.dma_start(XNS[:, j], normalised[bass.ds(i * W + j * P, P), :]).then_inc(s_xn[j].sem, 16)
            sp.wait_ge(o_expert.sem, o_expert.at(run, 0))

            def store(g, p):
                sp.wait_ge(c_ysb.sem, c_ysb.at(run, g, p + 1))
                sp.dma_start(rows_of_group(slot_results, g * UNROLL + p), YSB[:, p]).then_inc(c_st[p].sem, 16)

            for p in range(UNROLL):
                expert_weights(sp, 0, p, (0, 1))
            with sp.Fori(0, GSTEPS - 1) as g:
                for p in range(UNROLL):
                    store(g, p)
                    expert_weights(sp, g + 1, p, (0, 1))
            for p in range(UNROLL):
                store(GSTEPS - 1, p)

        def moe_tensor(pe, layer):
            r, run = front_run(layer), earlier(layer)
            pe.wait_ge(e_ready, 3)
            pe.matmul(psum[:, 2, 0:NE], ones[0:1, :], zeros[0:1, 0:NE], start=True, stop=True, skip_group_check=True)
            with pe.Fori(0, STEPS) as i:
                front_tensor(pe, i, r)
                pe.wait_ge(f_xt.sem, f_xt.at(r, i))
                pe.wait_ge(e_prob.sem, e_prob.before(run, i))
                for j in range(TPI):
                    o = psum[:, 6 + j // 2, NE * (j % 2):NE * (j % 2) + NE]
                    pe.matmul(o, XT[:, P * j:P * j + P], router_t[:], start=True, stop=False, skip_group_check=True)
                    mm = pe.matmul(o, ones[0:1, :], e_bias[:], start=False, stop=True, skip_group_check=True)
                mm.then_inc(e_lg.sem, 1)
                pe.wait_ge(e_he.sem, e_he.before(run, i))
                for j in range(TPI):
                    mm = pe.matmul(psum[:, 1, INTER * j:INTER * j + INTER], XT[:, P * j:P * j + P], sh_gate[:], start=True, stop=True, skip_group_check=True)
                mm.then_inc(e_h.sem, 1)
                pe.wait_ge(e_he.sem, e_he.at(run, i))
                pe.wait_ge(e_ht.sem, e_ht.before(run, i))
                stand(pe)
                for j in range(TPI):
                    mm = pe.transpose(psum[0:INTER, 3, P * j:P * j + P], HE[:, INTER * j:INTER * j + INTER], ident[:])
                mm.then_inc(e_tr.sem, 1)
                pe.wait_ge(e_ht.sem, e_ht.at(run, i))
                pe.wait_ge(e_x.sem, e_x.before(run, i))
                for j in range(TPI):
                    mm = pe.matmul(psum[:, 5, P * j:P * j + P], HT[:, P * j:P * j + P], sh_down[:], start=True, stop=True, skip_group_check=True)
                mm.then_inc(e_y.sem, 1)
                pe.wait_ge(e_mask.sem, e_mask.at(run, i))
                for j in range(TPI):
                    mm = pe.matmul(psum[:, 2, 0:NE], onesb[:], MASK[:, bass.ds(i * TPI + j, 1), :].rearrange("p a e -> p (a e)"),
                                   start=False, stop=True, skip_group_check=True)
                mm.then_inc(e_cnt.sem, 1)

            pe.wait_ge(o_link.sem, o_link.at(run, 0))
            pe.matmul(psum[:, 2, 0:NE], ident[:], FIRST, start=True, stop=True, skip_group_check=True)
            pe.wait_ge(e_ready, 3)
            for q in range(GROUP):
                mm = pe.matmul(psum[0:1, 4, P * q:P * q + P], EXPERT_COL[:, q:q + 1], ident[:], start=True, stop=True, skip_group_check=True)
            mm.then_inc(o_row.sem, 1)
            with pe.Fori(0, STEPS) as i:
                for j in range(TPI):
                    m = MASK[:, bass.ds(i * TPI + j, 1), :].rearrange("p a e -> p (a e)")
                    pe.matmul(psum[:, 2, 0:NE], earlier_tokens[:], m, start=False, stop=True, skip_group_check=True).then_inc(s_a.sem, 1)
                    pe.wait_ge(s_slotm.sem, s_slotm.at(run, i, j + 1))
                    pe.matmul(psum[:, 2, 0:NE], other_tokens[:], m, start=False, stop=True, skip_group_check=True)

            def transposes(g, p):
                pe.wait_ge(c_ld[p].sem, c_ld[p].at(run, g))
                pe.wait_ge(c_xt.sem, c_xt.at(run, g, p - 1))
                for q in range(GROUP):
                    mm = pe.transpose(psum[:, p % 2, P * q:P * q + P], XSB[:, p, q], ident[:])
                mm.then_inc(c_tr.sem, 1)

            def hidden(g, p):
                for h in range(2):
                    pe.wait_ge(c_ew[h][p].sem, c_ew[h][p].at(run, g))
                pe.wait_ge(c_xt.sem, c_xt.at(run, g, p + 1))
                pe.wait_ge(c_he.sem, c_he.at(run, g, p - 1))
                for q in range(GROUP):
                    o = 256 * (p % 2) + INTER * q
                    mm = pe.matmul(psum[:, 2, o:o + INTER], XSBT[:, p % 2, P * q:P * q + P], EWB[:, p, q, 0:INTER], start=True, stop=True, skip_group_check=True)
                mm.then_inc(c_h.sem, 1)

            def hidden_transposes(g, p):
                pe.wait_ge(c_he.sem, c_he.at(run, g, p + 1))
                pe.wait_ge(c_ht.sem, c_ht.at(run, g, p - 1))
                stand(pe)
                for q in range(GROUP):
                    mm = pe.transpose(psum[0:INTER, 3 + p % 2, P * q:P * q + P], HEB[:, p % 2, INTER * q:INTER * q + INTER], ident[:])
                mm.then_inc(c_htr.sem, 1)

            def results(g, p):
                pe.wait_ge(c_ht.sem, c_ht.at(run, g, p + 1))
                pe.wait_ge(c_ysb.sem, c_ysb.at(run, g, p - 1))
                for q in range(GROUP):
                    mm = pe.matmul(psum[:, 5 + p % 2, P * q:P * q + P], HTB[:, p % 2, P * q:P * q + P],
                                   EWB[0:INTER, p, q, INTER:EW], start=True, stop=True, skip_group_check=True)
                mm.then_inc(c_y.sem, 1)

            transposes(0, 0)
            hidden(0, 0)
            with pe.Fori(0, GSTEPS - 1) as g:
                for p in range(UNROLL):
                    transposes(g + (p + 1) // UNROLL, (p + 1) % UNROLL)
                    hidden_transposes(g, p)
                    hidden(g + (p + 1) // UNROLL, (p + 1) % UNROLL)
                    results(g, p)
            for p in range(UNROLL):
                if p < UNROLL - 1:
                    transposes(GSTEPS - 1, p + 1)
                hidden_transposes(GSTEPS - 1, p)
                if p < UNROLL - 1:
                    hidden(GSTEPS - 1, p + 1)
                results(GSTEPS - 1, p)

        ENGINES = 4

        def begin(eng):
            eng.wait_ge(primed, 1)
            eng.wait_ge(loaded, 16 * (len(weights) + 1))

        def finish(eng, layer):
            eng.drain().then_inc(phase_done, 1)
            eng.wait_ge(phase_done, ENGINES * (layer + 1))

        block = ctx.enter_context(nc.Block())

        @block.sync
        def _(sp):
            for s in signals:
                if s.start:
                    sp.sem_inc(s.sem, s.start)
            sp.sem_inc(primed, 1)
            sp.dma_start(X[:], a["x"].rearrange("(t p) d -> p t d", p=P)).then_inc(loaded, 16)
            for t, src in weights:
                sp.dma_start(t[:], src).then_inc(loaded, 16)
            sp.wait_ge(e_ready, 3)
            sp.dma_start(slot_rows.rearrange("(p r) d -> p (r d)", p=P).rearrange("p (n z) -> p n z", z=512),
                         zeros[:].unsqueeze(1).broadcast_to([P, SLOT_TILES * D // 512, 512])).then_inc(cleared, 16)
            moe_sync(sp, 1)
            moe_sync(sp, 3)
            sp.wait_ge(phase_done, ENGINES * len(LAYERS))
            sp.dma_start(a["out"].rearrange("(t p) d -> p t d", p=P), X[:]).then_inc(stored, 16)
            sp.wait_ge(stored, 16)

        @block.vector
        def _(dve):
            begin(dve)
            cos_vector(dve, 0)
            finish(dve, 0)
            moe_vector(dve, 1)
            finish(dve, 1)
            glru_vector(dve, 2)
            finish(dve, 2)
            moe_vector(dve, 3)
            finish(dve, 3)
            mamba_vector(dve, 4)
            finish(dve, 4)
            ffn_vector(dve, 5)
            finish(dve, 5)
            rope_vector(dve, 6)
            finish(dve, 6)
            ffn_vector(dve, 7)
            finish(dve, 7)

        @block.scalar
        def _(act):
            begin(act)
            cos_scalar(act, 0)
            finish(act, 0)
            moe_scalar(act, 1)
            finish(act, 1)
            glru_scalar(act, 2)
            finish(act, 2)
            moe_scalar(act, 3)
            finish(act, 3)
            mamba_scalar(act, 4)
            finish(act, 4)
            ffn_scalar(act, 5)
            finish(act, 5)
            rope_scalar(act, 6)
            finish(act, 6)
            ffn_scalar(act, 7)
            finish(act, 7)

        @block.gpsimd
        def _(pool):
            pool.memset(ones4[:], 0.0).then_inc(constants, 1)
            pool.memset(tiny[:], 1e-12).then_inc(constants, 1)
            pool.wait_ge(constants, 1)
            for n in range(4):
                pool.memset(ones4[:, n, DH * n:DH * n + DH], 1.0).then_inc(constants, 1)
            pool.memset(minus_half[:], -0.5).then_inc(constants, 1)
            pool.memset(rms_eps[:], 1e-6).then_inc(constants, 1)
            pool.memset(ones[:], 1.0).then_inc(constants, 1)
            pool.memset(onesb[:], 1.0).then_inc(e_ready, 1)
            pool.memset(zeros[:], 0.0).then_inc(e_ready, 1)
            pool.memset(ones_row[:], 1.0).then_inc(e_ready, 1)
            begin(pool)
            cos_gpsimd(pool, 0)
            finish(pool, 0)
            moe_gpsimd(pool, 1)
            finish(pool, 1)
            glru_gpsimd(pool, 2)
            finish(pool, 2)
            moe_gpsimd(pool, 3)
            finish(pool, 3)
            mamba_gpsimd(pool, 4)
            finish(pool, 4)
            ffn_gpsimd(pool, 5)
            finish(pool, 5)
            rope_gpsimd(pool, 6)
            finish(pool, 6)
            ffn_gpsimd(pool, 7)
            finish(pool, 7)

        @block.tensor
        def _(pe):
            begin(pe)
            cos_tensor(pe, 0)
            finish(pe, 0)
            moe_tensor(pe, 1)
            finish(pe, 1)
            glru_tensor(pe, 2)
            finish(pe, 2)
            moe_tensor(pe, 3)
            finish(pe, 3)
            mamba_tensor(pe, 4)
            finish(pe, 4)
            ffn_tensor(pe, 5)
            finish(pe, 5)
            rope_tensor(pe, 6)
            finish(pe, 6)
            ffn_tensor(pe, 7)
            finish(pe, 7)


def layout(inputs):
    import numpy as np

    contiguous = np.ascontiguousarray

    def of(layer):
        return lambda name: np.asarray(inputs[layer + "_" + name])

    out = {}
    w = of("L0_attn_a")
    out["x"] = w("x").reshape(TOK, D)
    out["w_qkv"] = w("w_qkv")
    out["ln_w"], out["ln_b"] = w("ln_w").reshape(D, 1), w("ln_b").reshape(D, 1)
    inner = w("w_out").shape[0]
    w_out = np.zeros((P, 2, D), np.float32)
    w_out[:inner, 0] = w_out[inner:, 1] = w("w_out")
    out["w_out"] = w_out
    w = of("L0_attn_b")
    for name, source in (("wg_t", "Wg"), ("wc_t", "Wc"), ("w1_t", "w1"), ("w2_t", "w2"), ("w3_t", "w3")):
        out[name] = contiguous(w(source).T)
    out["rms_w"], out["ffn_w"] = w("ln_w").reshape(D, 1), w("ffn_w").reshape(D, 1)
    w = of("L0_ffn")
    experts, width = w("w_gate").shape[:2]
    out["router_t"] = contiguous(w("router_w").T)
    out["e_bias"] = w("expert_bias").reshape(1, experts)
    out["sh_gate"], out["sh_down"] = contiguous(w("w_gate_shared").T), contiguous(w("w_down_shared").T)
    expert_w = np.zeros((experts, D, width + D), np.float32)
    expert_w[:, :, :width] = w("w_gate").transpose(0, 2, 1)
    expert_w[:, :width, width:] = w("w_down").transpose(0, 2, 1)
    out["expert_w"] = expert_w.reshape(experts * D, width + D)
    earlier = (np.arange(P)[:, None] < np.arange(P)[None, :])
    out["earlier_tokens"] = earlier.astype(mybir.dt.np(BF16))
    out["other_tokens"] = (~earlier).astype(mybir.dt.np(BF16))
    out["slot_tile"] = np.arange(P * 4, dtype=np.float32).reshape(P, 4)
    w = of("L1_attn_a")
    out["w_in"] = w("W_in").reshape(D, 4, P)
    out["b_in"] = contiguous(w("b_in").reshape(4, P).T)
    out["conv_w"] = contiguous(w("conv_w").reshape(2, P, -1).transpose(1, 0, 2))
    out["conv_b"] = contiguous(w("conv_b").reshape(2, P).T)
    out["m_a"] = contiguous(w("A").reshape(2, P, -1).transpose(1, 0, 2))
    out["m_ct"] = contiguous(w("C").T.reshape(-1, 2, P))
    out["m_d"] = contiguous(w("Dp").reshape(2, P).T)
    out["m_wo"] = contiguous(w("W_out").reshape(2, P, D).transpose(1, 0, 2))
    out["m_bo"] = w("b_out").reshape(1, D)
    w = of("L1_ffn")
    for name, source in (("wr_t", "W_r"), ("wk_t", "W_k"), ("wv_t", "W_v")):
        out[name] = contiguous(w(source).T)
    out["mu"] = np.stack([w("mu_r"), w("mu_k")], 1)
    w = of("L1_attn_b")
    order = np.concatenate([np.arange(0, DH, 2), np.arange(1, DH, 2)])
    rows = (np.arange(D // DH)[:, None] * DH + order[None]).reshape(-1)
    out["w_qkvt"] = contiguous(np.concatenate([w("wq")[rows], w("wk")[rows], w("wv")], 0).T)
    out["w_ot"] = contiguous(w("wo").T)
    powers = np.arange(0, DH, 2, dtype=np.float32) / np.float32(DH)
    angles = np.outer(np.arange(SEQ, dtype=np.float32), 1.0 / np.float32(10000.0) ** powers).astype(np.float32)
    tiles = lambda t: np.concatenate([t.reshape(2, P, -1).transpose(1, 0, 2)] * (TPI // 2), 1)
    out["cos"] = contiguous(tiles(np.cos(angles)))
    out["sin"] = contiguous(np.stack([-tiles(np.sin(angles)), tiles(np.sin(angles))], 1))
    out["ident"] = np.eye(P, dtype=np.float32)
    out["identb"] = np.eye(P, dtype=mybir.dt.np(BF16))
    later = np.arange(P)[:, None] > np.arange(P)[None, :]
    out["mask_kq"] = np.where(later, NEG, 0.0).astype(mybir.dt.np(BF16))
    out["mask_qk"] = np.where(later.T, NEG, 0.0).astype(mybir.dt.np(BF16))
    return out


def kernel(**inputs):
    import numpy as np
    import concourse.bacc as bacc
    from concourse.bass_utils import run_bass_kernel_spmd

    nc = bacc.Bacc("TRN2", target_bir_lowering=False, num_devices=1)
    arrays, a = {}, {}
    for name, array in layout(inputs).items():
        arrays[f"in_{name}"] = array
        a[name] = nc.dram_tensor(f"in_{name}", array.shape, mybir.dt.from_np(array.dtype), kind="ExternalInput").ap()
    a["out"] = nc.dram_tensor("out", (TOK, D), F32, kind="ExternalOutput").ap()
    program(nc, a)
    r = run_bass_kernel_spmd(nc, [arrays], core_ids=[0])
    return np.asarray(r.results[0]["out"]).reshape(NSEQ, SEQ, D)
```

```python
from contextlib import ExitStack

import concourse.bass as bass
from concourse import mybir

F32 = mybir.dt.float32
BF16 = mybir.dt.bfloat16
I32 = mybir.dt.int32
ACT = mybir.ActivationFunctionType
ALU = mybir.AluOpType
AX = mybir.AxisListType

P = 128
D = 128
SEQ = 256
NSEQ = 16
TOK = NSEQ * SEQ
TILES = TOK // P
TPI = 4
STEPS = TILES // TPI
W = TPI * P
EPS = 1e-5
RMS_EPS = 1e-6
DH = 8
SPLIT = 6 * DH
HROWS = 64
NEG = -1.0e30


START = 2


class Signal:

    def __init__(self, nc, ctx, name, per=1, steps=STEPS, start=START):
        self.sem = ctx.enter_context(nc.semaphore(name))
        self.per, self.steps, self.start = per, steps, start

    def at(self, run, i, c=None):
        return i * self.per + (self.start + run * self.steps * self.per + (self.per if c is None else c))

    def before(self, run, i):
        return self.at(run, i, 0)

    def end(self, run):
        return self.start + (run + 1) * self.steps * self.per


LAYERS = ("cos", "moe", "glru", "moe", "mamba", "ffn", "rope", "ffn")


def program(nc, a):
    ctx = ExitStack()
    with ctx:
        def sb(name, shape, dt=F32):
            return ctx.enter_context(nc.sbuf_tensor(name, shape, dt))

        signals = []

        def signal(name, per=1, steps=STEPS, start=START):
            s = Signal(nc, ctx, name, per, steps, start)
            signals.append(s)
            return s

        def semaphore(name):
            return ctx.enter_context(nc.semaphore(name))

        psum = ctx.enter_context(nc.psum_tensor("psum", [P, 8, 512], F32))

        X = sb("X", [P, TILES, D])
        ident = sb("ident", [P, P])
        identb = sb("identb", [P, P], BF16)
        mask_kq = sb("mask_kq", [P, P], BF16)
        mask_qk = sb("mask_qk", [P, P], BF16)
        ones4 = sb("ones4", [P, 4, 32])
        tiny = sb("tiny", [P, 1])
        rms_eps = sb("rms_eps", [P, 1])
        ln_eps = sb("ln_eps", [P, 1])
        both_eps = sb("both_eps", [P, 1])
        ones = sb("ones", [P, P])
        ones_row = sb("ones_row", [P, 160])
        minus_half = sb("minus_half", [P, 64])
        ARENA = 40704
        GATHER_AT = ARENA - TPI * 8 * D
        arena = sb("arena", [P, ARENA])
        used = [0]

        def view(shape, dt=F32, at=None):
            n = 1
            for k in shape[1:]:
                n *= k
            words = n if dt in (F32, I32) else (n + 1) // 2
            o = used[0] if at is None else at
            used[0] = o + words
            assert used[0] <= ARENA, used[0]
            v = arena[0:shape[0], o:o + words]
            if dt != F32:
                v = v.bitcast(dt)
            if len(shape) > 2:
                names = [f"d{k}" for k in range(len(shape) - 1)]
                v = v.rearrange("p (" + " ".join(names) + ") -> p " + " ".join(names),
                                **{m: k for m, k in zip(names[1:], shape[2:])})
            return v

        stats = sb("stats", [P, TPI, 6])
        mv = sb("mv", [P, TPI, 2])
        rstd = sb("rstd", [P, TPI])
        XN = sb("XN", [P, TPI, D])
        XT = sb("XT", [P, W])

        loaded = semaphore("loaded")
        loaded_all = semaphore("loaded_all")
        stored = semaphore("stored")
        constants = semaphore("constants")
        primed = semaphore("primed")
        stood = semaphore("stood")
        phase_done = semaphore("phase_done")

        weights = []

        def weight(name, shape, dt=F32, src=None):
            t = sb("w_" + name, shape, dt)
            weights.append((t, a[name] if src is None else src))
            return t

        w_qkv = weight("w_qkv", [D, 192])
        ln_w = weight("ln_w", [D, 1])
        ln_b = weight("ln_b", [D, 1])
        w_out = weight("w_out", [P, 2, D])
        for t, n in ((ident, "ident"), (identb, "identb"), (mask_kq, "mask_kq"), (mask_qk, "mask_qk")):
            weights.append((t, a[n]))
        FIRST_WEIGHTS = len(weights)

        class Order:

            def __init__(self, sig, run, i):
                self.sem, self.sig, self.run, self.i, self.c = sig.sem, sig, run, i, 0

            def one(self):
                self.c += 1
                return 1

            def so_far(self):
                return self.sig.at(self.run, self.i, self.c)

            def close(self):
                assert self.c == self.sig.per, (self.c, self.sig.per)

        def stand(eng):
            eng.sem_inc(stood, 1)

        def inverse_deviations(pool, i, r, second=None):
            pool.wait_ge(f_mv.sem, f_mv.at(r, i))
            stand(pool)
            scale, offset = (1.0, EPS) if second is None else (1.0 + second, EPS * second)
            pool.tensor_scalar(rstd[:], mv[:, :, 1], scale, offset, ALU.mult, ALU.add).then_inc(f_rstd.sem, 1)
            pool.wait_ge(f_rstd.sem, f_rstd.at(r, i, 1))
            stand(pool)
            pool.tensor_tensor(rstd[:], rstd[:], minus_half[:, 0:TPI], ALU.pow).then_inc(f_rstd.sem, 1)

        def deviations(act, i, r, offset, second=0.0):
            act.wait_ge(f_mv.sem, f_mv.at(r, i))
            act.activation(rstd[:], mv[:, :, 1], ACT.Sqrt, scale=1.0 + second, bias=offset).then_inc(f_rstd.sem, 1)

        def invert(dve, i, r):
            dve.wait_ge(f_rstd.sem, f_rstd.at(r, i, 1))
            dve.reciprocal(rstd[:], rstd[:]).then_inc(f_rstd.sem, 1)

        used[0] = 0
        QKV = view([P, TPI, 192])
        SQ = view([P, TPI, 128])
        SS = view([P, TPI, 16])
        RN = view([P, TPI, 16])
        QN = view([P, 2, TPI, 8, DH])
        R1 = view([P, 64, DH])
        HML = view([P, 64, 3, DH], BF16)
        Qs = view([P, 32, HROWS], BF16)
        Ks = view([P, 32, HROWS], BF16)
        QT = view([P, 2, 2, 4, SEQ], BF16)
        KT = view([P, 2, 2, 4, SEQ], BF16)
        VP = view([P, 2, TPI, 8, 32])
        PR = view([P, 2, 4, 384])
        REC = view([P, SEQ])
        OT = view([P, SEQ])
        a_link = signal("a_link", 6)
        a_sq = signal("a_sq")
        a_ss = signal("a_ss")
        a_qkv_ps = signal("a_qkv_ps")
        a_qkv = signal("a_qkv", 2)
        a_split = signal("a_split")
        a_vp = signal("a_vp", 4)
        a_qrows = signal("a_qrows", 3)
        a_krows = signal("a_krows", 3)
        a_sqrt = signal("a_sqrt")
        a_tr = signal("a_tr", 4)
        a_qt = signal("a_qt", 2, start=START + 2)
        a_kt = signal("a_kt", 2, start=START + 2)
        a_sc = signal("a_sc", 4, start=START + 4)
        a_exp = signal("a_exp", 4)
        a_av = signal("a_av", 4, start=START + 4)
        a_rec = signal("a_rec")
        a_ot = signal("a_ot")
        a_y = signal("a_y")
        a_x = signal("a_x")

        def cos_vector(dve, layer):
            def front(s):
                front_stats(dve, s, layer)
                front_scale(dve, s, layer)

            def squares(s):
                dve.wait_ge(a_qkv.sem, a_qkv.at(0, s))
                dve.tensor_tensor(SQ, QKV[:, :, 0:128], QKV[:, :, 0:128], ALU.mult).then_inc(a_sq.sem, 1)
                dve.wait_ge(a_sq.sem, a_sq.at(0, s))
                dve.tensor_reduce(SS, SQ.rearrange("p t (h d) -> p t h d", d=DH), AX.X, ALU.add).then_inc(a_ss.sem, 1)

            def normal(s):
                link = Order(a_link, 0, s)
                dve.wait_ge(a_sqrt.sem, a_sqrt.at(0, s))
                dve.reciprocal(RN, RN).then_inc(link.sem, link.one())
                dve.wait_ge(link.sem, link.so_far())
                for k in range(2):
                    dve.tensor_tensor(
                        QN[:, k], QKV[:, :, 64 * k:64 * k + 64].rearrange("p t (h d) -> p t h d", d=DH),
                        RN[:, :, 8 * k:8 * k + 8].unsqueeze(3).broadcast_to([P, TPI, 8, DH]), ALU.mult).then_inc(link.sem, link.one())
                dve.wait_ge(link.sem, link.so_far())
                split3(dve, link, QN.rearrange("p s t h d -> p (s t h) d"), R1, HML, a_split, a_krows, 0, s)
                dve.wait_ge(a_split.sem, a_split.at(0, s))
                dve.wait_ge(a_tr.sem, a_tr.before(0, s))
                query_rows(dve, HML[:, 0:32], Qs, 32, a_qrows)
                link.close()

            def keys(s, u):
                for b in range(2):
                    dve.wait_ge(a_tr.sem, a_tr.at(0, s, 2 * b + 2))
                    dve.wait_ge(a_sc.sem, a_sc.before(0, s - 1))
                    dve.tensor_copy(KT[:, u, b], psum_b16(2)).then_inc(a_kt.sem, 1)

            def divide(i):
                dve.wait_ge(a_av.sem, a_av.at(0, i))
                dve.reciprocal(REC, psum[:, 3, 256:512]).then_inc(a_rec.sem, 1)
                dve.wait_ge(a_rec.sem, a_rec.at(0, i))
                dve.wait_ge(a_y.sem, a_y.before(0, i))
                dve.tensor_tensor(OT, psum[:, 3, 0:256], REC, ALU.mult).then_inc(a_ot.sem, 1)

            def add(i):
                dve.wait_ge(a_y.sem, a_y.at(0, i))
                xs = X[:, bass.ds(i * TPI, TPI), :].rearrange("p t d -> p (t d)")
                dve.tensor_tensor(xs, psum[:, 0, :], xs, ALU.add).then_inc(a_x.sem, 1)

            def step(i, u, first=False, left=STEPS):
                if left >= 1:
                    normal(i + 1)
                if not first:
                    add(i - 1)
                if left >= 3:
                    front(i + 3)
                if left >= 1:
                    keys(i + 1, 1 - u)
                if left >= 2:
                    squares(i + 2)
                divide(i)

            front(0)
            squares(0)
            normal(0)
            front(1)
            keys(0, 0)
            squares(1)
            front(2)
            step(0, 0, first=True)
            step(1, 1)
            with dve.Fori(1, STEPS // 2 - 2) as i2:
                for u in range(2):
                    step(i2 * 2 + u, u)
            for i in range(STEPS - 4, STEPS):
                step(i, i % 2, left=STEPS - 1 - i)
            add(STEPS - 1)
            dve.wait_ge(a_x.sem, a_x.end(0))

        def psum_b16(bank):
            return psum[:, bank, :].bitcast(BF16).rearrange("p (c q) -> p c q", q=SEQ)

        def split3(dve, link, src, rest, parts, done, copied, run, i):
            dve.wait_ge(copied.sem, copied.before(run, i))
            dve.tensor_copy(parts[:, :, 0, :], src).then_inc(link.sem, link.one())
            dve.wait_ge(link.sem, link.so_far())
            dve.tensor_tensor(rest, src, parts[:, :, 0, :], ALU.subtract).then_inc(link.sem, link.one())
            dve.wait_ge(link.sem, link.so_far())
            dve.tensor_copy(parts[:, :, 1, :], rest).then_inc(link.sem, link.one())
            dve.wait_ge(link.sem, link.so_far())
            dve.tensor_tensor(parts[:, :, 2, :], rest, parts[:, :, 1, :], ALU.subtract).then_inc(done.sem, 1)

        def cos_scalar(act, layer):
            def tokens(s):
                act.wait_ge(f_xt_ps.sem, f_xt_ps.at(layer, s))
                act.wait_ge(a_qkv_ps.sem, a_qkv_ps.before(0, s))
                act.activation(XT[:], psum[:, 0, :], ACT.Identity, scale=ln_w[:, 0:1], bias=ln_b[:, 0:1]).then_inc(f_xt.sem, 1)

            def projected(s):
                act.wait_ge(a_qkv_ps.sem, a_qkv_ps.at(0, s))
                act.wait_ge(a_split.sem, a_split.before(0, s))
                act.wait_ge(a_vp.sem, a_vp.before(0, s))
                for k in range(2):
                    act.activation(QKV[:, 2 * k:2 * k + 2, :], psum[:, 1 + k, 0:384].rearrange("p (t c) -> p t c", t=2),
                                   ACT.Copy).then_inc(a_qkv.sem, 1)

            def roots(s):
                act.wait_ge(a_ss.sem, a_ss.at(0, s))
                act.activation(RN, SS, ACT.Sqrt, bias=tiny[:, 0:1]).then_inc(a_sqrt.sem, 1)

            def rows(s):
                act.wait_ge(a_split.sem, a_split.at(0, s))
                act.wait_ge(a_tr.sem, a_tr.before(0, s))
                key_rows(act, HML[:, 32:64], Ks, a_krows)

            def queries(s, u):
                for b in range(2):
                    act.wait_ge(a_tr.sem, a_tr.at(0, s, 2 * b + 1))
                    act.wait_ge(a_sc.sem, a_sc.before(0, s - 1))
                    act.activation(QT[:, u, b], psum_b16(1), ACT.Copy).then_inc(a_qt.sem, 1)

            def weigh(i, n):
                act.wait_ge(a_sc.sem, a_sc.at(0, i, n + 1))
                act.wait_ge(a_av.sem, a_av.at(0, i, n - 1))
                act.activation(PR[:, n % 2], psum[:, 4:8, 0:384], ACT.Exp, scale=8.0).then_inc(a_exp.sem, 1)

            def step(i, u, left=STEPS):
                weigh(i, 0)
                weigh(i, 1)
                if left >= 2:
                    tokens(i + 2)
                weigh(i, 2)
                if left >= 2:
                    projected(i + 2)
                if left >= 1:
                    rows(i + 1)
                weigh(i, 3)
                if left >= 1:
                    queries(i + 1, 1 - u)
                if left >= 2:
                    roots(i + 2)

            tokens(0)
            projected(0)
            roots(0)
            rows(0)
            queries(0, 0)
            tokens(1)
            projected(1)
            roots(1)
            with act.Fori(0, STEPS // 2 - 2) as i2:
                for u in range(2):
                    step(i2 * 2 + u, u)
            for i in range(STEPS - 4, STEPS):
                step(i, i % 2, left=STEPS - 1 - i)

        def cos_gpsimd(pool, layer):
            pool.memset(VP, 0.0).then_inc(constants, 1)
            pool.memset(Qs, 0.0).then_inc(constants, 1)
            pool.memset(Ks, 0.0).then_inc(constants, 1)
            pool.wait_ge(constants, 17)

            def norm(s):
                inverse_deviations(pool, s, layer, second=EPS)

            def values(s, u):
                pool.wait_ge(a_qkv.sem, a_qkv.at(0, s))
                pool.wait_ge(a_av.sem, a_av.before(0, s - 1))
                stand(pool)
                for n in range(4):
                    pool.tensor_copy(VP[:, u, :, n:8:4, DH * n:DH * n + DH],
                                     QKV[:, :, 128:192].rearrange("p t (h d) -> p t h d", d=DH)[:, :, n:8:4, :]).then_inc(a_vp.sem, 1)

            norm(0)
            values(0, 0)
            norm(1)
            values(1, 1)
            norm(2)
            with pool.Fori(0, STEPS // 2 - 2) as i2:
                for u in range(2):
                    norm(i2 * 2 + u + 3)
                    values(i2 * 2 + u + 2, u)
            norm(STEPS - 1)
            values(STEPS - 2, 0)
            values(STEPS - 1, 1)

        def rows_of(x, u, k):
            return x[:, :, DH * u:DH * (u + k)].rearrange("p n (k d) -> p n k d", d=DH)

        def query_rows(dve, parts, rows, n, done):
            for part, u, k in ((0, 0, 3), (1, 3, 2), (2, 5, 1)):
                dve.tensor_copy(rows_of(rows, u, k), parts[:, :, part, :].unsqueeze(2).broadcast_to([P, n, k, DH])).then_inc(done.sem, 1)

        def key_rows(act, parts, rows, done):
            for u, k in ((0, 3), (3, 2), (5, 1)):
                act.activation(rows_of(rows, u, k), parts[:, :, 0:k, :], ACT.Copy).then_inc(done.sem, 1)

        def head_scores(pe, bank, kt, qt, k):
            pe.matmul(psum[:, bank, 0:256], kt[0:k, 0:128], qt[0:k, :], start=True, stop=False, skip_group_check=True)
            pe.matmul(psum[:, bank, 256:384], kt[0:k, 128:256], qt[0:k, 128:256], start=False, stop=False, skip_group_check=True)

        def mask_scores(pe, bank):
            v = psum[:, bank, :].rearrange("p (a q) -> p a q", q=256)[:, :, 0:128]
            return pe.matmul(v, identb[:], mask_kq[:].unsqueeze(1).broadcast_to([P, 2, P]), start=False, stop=True, skip_group_check=True)

        def weigh_values(pe, n, vp, pr, between=None):
            for half in range(2):
                for kt in range(2):
                    if between is not None and half + kt:
                        between()
                    for r in range(4):
                        lo, hi = (0, 256) if kt == 0 else (128, 256)
                        mm = pe.matmul(psum[32 * r:32 * r + 32, 3, 256 * half + lo:256 * half + hi],
                                       ones4[:, n, :] if half else vp(kt, 4 * r + n),
                                       pr[:, r, 0:256] if kt == 0 else pr[:, r, 256:384],
                                       start=(n == half == kt == 0), stop=(n == 3 and half == kt == 1),
                                       skip_group_check=True, tile_position=(0, 32 * r))
            return mm

        def cos_tensor(pe, layer):
            pe.wait_ge(constants, 17)

            def project(s):
                pe.wait_ge(f_xt.sem, f_xt.at(layer, s))
                pe.wait_ge(a_qt.sem, a_qt.before(0, s - 1))
                pe.wait_ge(a_kt.sem, a_kt.before(0, s - 1))
                for j in range(TPI):
                    mm = pe.matmul(psum[:, 1 + j // 2, 192 * (j % 2):192 * (j % 2) + 192], XT[:, P * j:P * j + P],
                                   w_qkv[:], start=True, stop=True, skip_group_check=True)
                mm.then_inc(a_qkv_ps.sem, 1)

            def transposes(s):
                pe.wait_ge(a_qrows.sem, a_qrows.at(0, s))
                pe.wait_ge(a_krows.sem, a_krows.at(0, s))
                for b in range(2):
                    for k, rows in ((0, Qs), (1, Ks)):
                        if b:
                            done = (a_qt, a_kt)[k]
                            pe.wait_ge(done.sem, done.at(0, s, 1))
                        for c in range(4):
                            for t in range(2):
                                h = (2 * b + t) * 8 + 2 * c
                                mm = pe.transpose(psum_b16(1 + k)[:, c, P * t:P * t + P],
                                                  rows[:, h:h + 2, :].rearrange("p h k -> p (h k)"), identb[:])
                        mm.then_inc(a_tr.sem, 1)

            def scores(i, u, n):
                if n == 0:
                    pe.wait_ge(a_qt.sem, a_qt.at(0, i))
                    pe.wait_ge(a_kt.sem, a_kt.at(0, i))
                pe.wait_ge(a_exp.sem, a_exp.at(0, i, n))
                for r in range(4):
                    b, h = r // 2, n + 4 * (r % 2)
                    c, lo = h // 2, HROWS * (h % 2)
                    head_scores(pe, 4 + r, KT[lo:lo + HROWS, u, b, c], QT[lo:lo + HROWS, u, b, c], SPLIT)
                for r in range(4):
                    mm = mask_scores(pe, 4 + r)
                mm.then_inc(a_sc.sem, 1)

            def values(i, u, n):
                pe.wait_ge(a_exp.sem, a_exp.at(0, i, n + 1))
                if n == 0:
                    pe.wait_ge(a_vp.sem, a_vp.at(0, i))
                    pe.wait_ge(a_ot.sem, a_ot.before(0, i))
                weigh_values(pe, n, lambda kt, h: VP[:, u, 2 * (h // 8) + kt, h % 8, :], PR[:, n % 2]).then_inc(a_av.sem, 1)

            def output(i):
                pe.wait_ge(a_ot.sem, a_ot.at(0, i))
                for b in range(2):
                    for t in range(2):
                        mm = pe.matmul(psum[:, 0, P * (2 * b + t):P * (2 * b + t) + P], OT[:, P * t:P * t + P],
                                       w_out[:, b, :], start=True, stop=True, skip_group_check=True)
                mm.then_inc(a_y.sem, 1)

            def step(i, u, first=False, left=STEPS):
                scores(i, u, 0)
                scores(i, u, 1)
                if not first:
                    output(i - 1)
                values(i, u, 0)
                scores(i, u, 2)
                if left >= 2:
                    pe.wait_ge(a_x.sem, a_x.before(0, i))
                    front_tensor(pe, i + 2, layer)
                values(i, u, 1)
                if left >= 2:
                    project(i + 2)
                scores(i, u, 3)
                values(i, u, 2)
                if left >= 1:
                    if left >= 2:
                        pe.wait_ge(a_qkv.sem, a_qkv.at(0, i + 2))
                    transposes(i + 1)
                values(i, u, 3)

            front_tensor(pe, 0, layer)
            project(0)
            pe.wait_ge(a_qkv.sem, a_qkv.at(0, 0))
            transposes(0)
            front_tensor(pe, 1, layer)
            pe.wait_ge(a_qt.sem, a_qt.at(0, 0))
            pe.wait_ge(a_kt.sem, a_kt.at(0, 0))
            project(1)
            step(0, 0, first=True)
            step(1, 1)
            with pe.Fori(1, STEPS // 2 - 2) as i2:
                for u in range(2):
                    step(i2 * 2 + u, u)
            for i in range(STEPS - 4, STEPS):
                step(i, i % 2, left=STEPS - 1 - i)
            output(STEPS - 1)

        def earlier(layer):
            return LAYERS[:layer].count(LAYERS[layer])

        def experts_before(layer):
            return LAYERS[:layer].count("moe") - 1

        def front_run(layer):
            return layer

        f_link = signal("f_link", 7)
        f_mv = signal("f_mv")
        f_rstd = signal("f_rstd", 2)
        f_xn = signal("f_xn", TPI)
        f_xt_ps = signal("f_xt_ps")
        f_xt = signal("f_xt")

        def front_stats(dve, i, r):
            link = Order(f_link, r, i)
            for j in range(TPI):
                dve.bn_stats(stats[:, j, :], X[:, bass.ds(i * TPI + j, 1), :].rearrange("p a d -> p (a d)")).then_inc(link.sem, link.one())
            dve.wait_ge(link.sem, link.so_far())
            stand(dve)
            for j in range(TPI):
                ins = dve.bn_aggr(mv[:, j, :], stats[:, j, :])
                if j < TPI - 1:
                    ins.then_inc(link.sem, link.one())
            ins.then_inc(f_mv.sem, 1)
            link.close()

        def front_scale(dve, i, r, saved=None, saved_run=0):
            dve.wait_ge(f_xt_ps.sem, f_xt_ps.before(r, i))
            if saved is not None:
                dve.wait_ge(saved.sem, saved.before(saved_run, i))
            dve.wait_ge(f_rstd.sem, f_rstd.at(r, i))
            for j in range(TPI):
                dve.tensor_scalar(XN[:, j, :], X[:, bass.ds(i * TPI + j, 1), :].rearrange("p a d -> p (a d)"),
                                  mv[:, j, 0:1], rstd[:, j:j + 1], ALU.subtract, ALU.mult).then_inc(f_xn.sem, 1)

        def front_vector(dve, i, r):
            front_stats(dve, i, r)
            front_scale(dve, i, r)

        def front_tensor(pe, i, r):
            pe.wait_ge(f_xn.sem, f_xn.at(r, i))
            pe.wait_ge(f_xt.sem, f_xt.before(r, i))
            for j in range(TPI):
                mm = pe.transpose(psum[:, 0, P * j:P * j + P], XN[:, j, :], ident[:])
            mm.then_inc(f_xt_ps.sem, 1)

        used[0] = 0
        wg_t = weight("wg_t", [D, D])
        wc_t = weight("wc_t", [D, D])
        w1_t = weight("w1_t", [D, D])
        w2_t = weight("w2_t", [D, D])
        w3_t = weight("w3_t", [D, D])
        rms_w = weight("rms_w", [D, 1])
        ffn_w = weight("ffn_w", [D, 1])
        BETA = view([P, W])
        KEEP = view([P, W])
        HX = view([P, W])
        HSQ = view([P, W])
        RMS = view([P, W])
        HN = view([P, W])
        GATE = view([P, W])
        g_proj = signal("g_proj")
        g_beta = signal("g_beta", 2)
        g_link = signal("g_link", 4)
        g_hx = signal("g_hx", 2)
        g_sq = signal("g_sq")
        g_ms = signal("g_ms")
        g_rms = signal("g_rms")
        g_hn = signal("g_hn")
        g_up = signal("g_up")
        g_sig = signal("g_sig")
        g_gate = signal("g_gate")
        g_y = signal("g_y")
        g_x = signal("g_x")

        def glru_vector(dve, layer):
            r = front_run(layer)
            run = experts_before(layer)

            def front(i):
                summed(dve, i, run)
                front_stats(dve, i, r)
                invert(dve, i, r)
                front_scale(dve, i, r)

            def step(i, left=STEPS):
                link = Order(g_link, 0, i)

                def sums(*tiles):
                    if left:
                        sum_rows(dve, i + 1, run, left == 1, tiles)

                dve.wait_ge(g_beta.sem, g_beta.at(0, i))
                dve.tensor_tensor(BETA, psum[:, 2, :], BETA, ALU.mult).then_inc(link.sem, link.one())
                dve.wait_ge(link.sem, link.so_far())
                dve.wait_ge(g_y.sem, g_y.before(0, i))
                stand(dve)
                for b in range(2):
                    s = slice(SEQ * b, SEQ * b + SEQ)
                    dve.tensor_tensor_scan(HX[:, s], KEEP[:, s], BETA[:, s], 0.0, ALU.mult, ALU.add).then_inc(g_hx.sem, 1)
                sums(0)
                dve.wait_ge(g_rms.sem, g_rms.at(0, i))
                dve.reciprocal(RMS, RMS).then_inc(link.sem, link.one())
                dve.wait_ge(link.sem, link.so_far())
                dve.scalar_tensor_tensor(HN, HX, ffn_w[:, 0:1], RMS, ALU.mult, ALU.mult).then_inc(g_hn.sem, 1)
                sums(1)
                dve.wait_ge(g_sig.sem, g_sig.at(0, i))
                dve.tensor_tensor(GATE, psum[:, 4, :], GATE, ALU.mult).then_inc(link.sem, link.one())
                dve.wait_ge(link.sem, link.so_far())
                dve.tensor_tensor(GATE, psum[:, 5, :], GATE, ALU.mult).then_inc(g_gate.sem, 1)
                sums(2, 3)
                if left:
                    front(i + 1)
                dve.wait_ge(g_y.sem, g_y.at(0, i))
                xs = X[:, bass.ds(i * TPI, TPI), :].rearrange("p t d -> p (t d)")
                dve.tensor_tensor(xs, psum[:, 6, :], xs, ALU.add).then_inc(link.sem, link.one())
                dve.wait_ge(link.sem, link.so_far())
                link.close()

            sum_rows(dve, 0, run, False, range(TPI))
            front(0)
            with dve.Fori(0, STEPS - 2) as i:
                step(i)
            step(STEPS - 2, left=1)
            step(STEPS - 1, left=0)

        def glru_scalar(act, layer):
            r = front_run(layer)
            with act.Fori(0, STEPS) as i:
                deviations(act, i, r, both_eps[:, 0:1], RMS_EPS)
                act.wait_ge(f_xt_ps.sem, f_xt_ps.at(r, i))
                act.wait_ge(g_proj.sem, g_proj.before(0, i))
                act.activation(XT[:], psum[:, 0, :], ACT.Copy, scale=rms_w[:, 0:1]).then_inc(f_xt.sem, 1)
                act.wait_ge(g_proj.sem, g_proj.at(0, i))
                act.wait_ge(g_hx.sem, g_hx.before(0, i))
                act.activation(BETA, psum[:, 1, :], ACT.Sigmoid).then_inc(g_beta.sem, 1)
                act.activation(KEEP, psum[:, 1, :], ACT.Sigmoid, scale=-1.0).then_inc(g_beta.sem, 1)
                act.wait_ge(g_hx.sem, g_hx.at(0, i))
                act.activation(HSQ, HX, ACT.Square).then_inc(g_sq.sem, 1)
                act.wait_ge(g_ms.sem, g_ms.at(0, i))
                act.wait_ge(g_hn.sem, g_hn.before(0, i))
                act.activation(RMS, psum[:, 3, :], ACT.Sqrt, bias=rms_eps[:, 0:1], scale=1.0 / D).then_inc(g_rms.sem, 1)
                act.wait_ge(g_up.sem, g_up.at(0, i))
                act.wait_ge(g_y.sem, g_y.before(0, i))
                act.activation(GATE, psum[:, 4, :], ACT.Sigmoid).then_inc(g_sig.sem, 1)

        def glru_gpsimd(pool, layer):
            r = front_run(layer)
            gather(pool, experts_before(layer))

        def glru_tensor(pe, layer):
            r = front_run(layer)
            with pe.Fori(0, STEPS) as i:
                front_tensor(pe, i, r)
                pe.wait_ge(f_xt.sem, f_xt.at(r, i))
                pe.wait_ge(g_hx.sem, g_hx.before(0, i))
                pe.matmul(psum[:, 1, :], wg_t[:], XT[:], start=True, stop=True)
                pe.matmul(psum[:, 2, :], wc_t[:], XT[:], start=True, stop=True).then_inc(g_proj.sem, 1)
                pe.wait_ge(g_sq.sem, g_sq.at(0, i))
                pe.matmul(psum[:, 3, :], ones[:], HSQ, start=True, stop=True).then_inc(g_ms.sem, 1)
                pe.wait_ge(g_hn.sem, g_hn.at(0, i))
                pe.matmul(psum[:, 4, :], w1_t[:], HN, start=True, stop=True)
                pe.matmul(psum[:, 5, :], w3_t[:], HN, start=True, stop=True).then_inc(g_up.sem, 1)
                pe.wait_ge(g_gate.sem, g_gate.at(0, i))
                for j in range(TPI):
                    s = slice(P * j, P * j + P)
                    pe.matmul(psum[:, 6, s], HX[:, s], ident[:], start=True, stop=False, skip_group_check=True)
                    mm = pe.matmul(psum[:, 6, s], GATE[:, s], w2_t[:], start=False, stop=True, skip_group_check=True)
                mm.then_inc(g_y.sem, 1)

        used[0] = 0
        wr_t = weight("wr_t", [D, D])
        wk_t = weight("wk_t", [D, D])
        wv_t = weight("wv_t", [D, D])
        mu = weight("mu", [D, 2])
        one_minus_mu = sb("one_minus_mu", [D, 2])
        XS = view([P, 2, SEQ + 1])
        MIX = view([P, 2, 2, SEQ])
        R_ = view([P, W])
        KK = view([P, W])
        h_zero = semaphore("h_zero")
        h_prev = signal("h_prev", 2)
        h_mix = signal("h_mix", 2)
        h_rk = signal("h_rk")
        h_r = signal("h_r")
        h_k = signal("h_k")
        h_v = signal("h_v")
        h_link = signal("h_link", 2)

        def ffn_vector(dve, layer):
            r, run = front_run(layer), earlier(layer)
            dve.memset(XS[:, :, 0:1], 0.0).then_inc(h_zero, 1)
            dve.tensor_scalar(one_minus_mu[:], mu[:], -1.0, 1.0, ALU.mult, ALU.add).then_inc(h_zero, 1)
            def step(i, left=STEPS):
                last = left == 0
                link = Order(h_link, run, i)
                for m in range(2):
                    dve.wait_ge(h_prev.sem, h_prev.at(run, i, m + 1))
                    dve.scalar_tensor_tensor(MIX[:, m], XS[:, :, 1:SEQ + 1], mu[:, m:m + 1], MIX[:, m],
                                             ALU.mult, ALU.add).then_inc(h_mix.sem, 1)
                if not last:
                    front_scale(dve, i + 1, r)
                if left >= 2:
                    front_stats(dve, i + 2, r)
                dve.wait_ge(h_rk.sem, h_rk.at(run, i))
                dve.tensor_scalar(KK, psum[:, 2, :], 0.0, None, ALU.max).then_inc(link.sem, link.one())
                dve.wait_ge(link.sem, link.so_far())
                dve.tensor_tensor(KK, KK, KK, ALU.mult).then_inc(h_k.sem, 1)
                dve.wait_ge(h_v.sem, h_v.at(run, i))
                dve.wait_ge(h_r.sem, h_r.at(run, i))
                dve.tensor_tensor(R_, psum[:, 3, :], R_, ALU.mult).then_inc(h_mul.sem, 1)
                dve.wait_ge(h_mul.sem, h_mul.at(run, i))
                xs = X[:, bass.ds(i * TPI, TPI), :].rearrange("p t d -> p (t d)")
                dve.tensor_tensor(xs, R_, xs, ALU.add).then_inc(link.sem, link.one())
                link.close()

            front_vector(dve, 0, r)
            front_stats(dve, 1, r)
            with dve.Fori(0, STEPS - 2) as i:
                step(i)
            step(STEPS - 2, left=1)
            step(STEPS - 1, left=0)
            dve.wait_ge(h_link.sem, h_link.end(run))

        h_mul = signal("h_mul")

        def ffn_scalar(act, layer):
            r, run = front_run(layer), earlier(layer)

            def tokens(i):
                act.wait_ge(f_xt_ps.sem, f_xt_ps.at(r, i))
                act.wait_ge(h_mix.sem, h_mix.before(run, i))
                act.activation(XS[:, :, 1:SEQ + 1], psum[:, 0, :].rearrange("p (b q) -> p b q", b=2), ACT.Copy).then_inc(f_xt.sem, 1)

            def previous(i):
                act.wait_ge(f_xt.sem, f_xt.at(r, i))
                act.wait_ge(h_rk.sem, h_rk.before(run, i))
                for m in range(2):
                    act.activation(MIX[:, m], XS[:, :, 0:SEQ], ACT.Copy, scale=one_minus_mu[:, m:m + 1]).then_inc(h_prev.sem, 1)

            def step(i, last):
                act.wait_ge(h_rk.sem, h_rk.at(run, i))
                act.wait_ge(h_mul.sem, h_mul.before(run, i))
                act.wait_ge(h_link.sem, h_link.before(run, i))
                act.activation(R_, psum[:, 1, :], ACT.Sigmoid).then_inc(h_r.sem, 1)
                if not last:
                    tokens(i + 1)
                    previous(i + 1)

            act.wait_ge(h_zero, 2 * run + 2)
            tokens(0)
            previous(0)
            with act.Fori(0, STEPS - 1) as i:
                step(i, False)
            step(STEPS - 1, True)

        def ffn_gpsimd(pool, layer):
            r, run = front_run(layer), earlier(layer)
            with pool.Fori(0, STEPS) as i:
                inverse_deviations(pool, i, r)

        def ffn_tensor(pe, layer):
            r, run = front_run(layer), earlier(layer)
            def step(i, last):
                pe.wait_ge(h_mix.sem, h_mix.at(run, i))
                pe.wait_ge(h_r.sem, h_r.before(run, i))
                pe.wait_ge(h_k.sem, h_k.before(run, i))
                for j in range(TPI):
                    s = slice(P * j % SEQ, P * j % SEQ + P)
                    pe.matmul(psum[:, 1, P * j:P * j + P], MIX[:, 0, j // 2, s], wr_t[:], start=True, stop=True)
                pe.matmul(psum[:, 2, :], wk_t[:], MIX[:, 1].rearrange("p b q -> p (b q)"), start=True, stop=True).then_inc(h_rk.sem, 1)
                if not last:
                    front_tensor(pe, i + 1, r)
                pe.wait_ge(h_k.sem, h_k.at(run, i))
                pe.wait_ge(h_mul.sem, h_mul.before(run, i))
                for j in range(TPI):
                    mm = pe.matmul(psum[:, 3, P * j:P * j + P], KK[:, P * j:P * j + P], wv_t[:], start=True, stop=True)
                mm.then_inc(h_v.sem, 1)

            front_tensor(pe, 0, r)
            with pe.Fori(0, STEPS - 1) as i:
                step(i, False)
            step(STEPS - 1, True)

        used[0] = 0
        E2 = 2
        STATE = 16
        TAPS = 4
        w_in = weight("w_in", [D, 2 * E2, P])
        b_in = weight("b_in", [P, 2 * E2])
        conv_w = weight("conv_w", [P, E2, TAPS])
        conv_b = weight("conv_b", [P, E2])
        m_a = weight("m_a", [P, E2, STATE])
        m_ct = weight("m_ct", [STATE, E2, P])
        m_d = weight("m_d", [P, E2])
        m_wo = weight("m_wo", [P, E2, D])
        m_bo = weight("m_bo", [P, D])
        XP = view([P, E2, 2, TAPS - 1 + SEQ])
        XCS = view([P, E2, 2, SEQ])
        XC = view([P, E2, TOK])
        Z = view([P, E2, TOK])
        U16 = view([STATE, NSEQ, SEQ])
        U = view([P, 2, SEQ])
        H = view([P, 2, SEQ])
        H16 = view([STATE, NSEQ, SEQ])
        YM = view([P, E2, W])
        HALF = NSEQ // 2
        m_zero = semaphore("m_zero")
        m_in = signal("m_in")
        m_xp = signal("m_xp", 4)
        m_conv = signal("m_conv", 8)
        m_u_ps = signal("m_u_ps")
        m_u = signal("m_u")
        m_spread = semaphore("m_spread")
        m_h = [semaphore(f"m_h{g}") for g in range(2)]
        m_gather = semaphore("m_gather")
        m_y_ps = signal("m_y_ps")
        m_ym = signal("m_ym", 4)
        m_out = signal("m_out")
        m_x = signal("m_x", 2)

        def mamba_vector(dve, layer):
            r = front_run(layer)
            dve.memset(XP[:, :, :, 0:TAPS - 1], 0.0).then_inc(m_zero, 1)
            run = experts_before(layer)

            def front(i):
                summed(dve, i, run)
                front_stats(dve, i, r)
                invert(dve, i, r)
                front_scale(dve, i, r)

            def step(i, left=STEPS):
                if left:
                    sum_rows(dve, i + 1, run, left == 1, range(0, 2))
                convolve(i)
                if left:
                    sum_rows(dve, i + 1, run, left == 1, range(2, TPI))
                    front(i + 1)

            def convolve(i):
                dve.wait_ge(m_u_ps.sem, m_u_ps.before(0, i))
                dve.wait_ge(m_xc.sem, m_xc.before(0, i))
                dve.wait_ge(m_xp.sem, m_xp.at(0, i, 2))
                for k in range(TAPS):
                    if k:
                        dve.wait_ge(m_conv.sem, m_conv.at(0, i, 2 * k))
                    for e in range(E2):
                        if k == 0:
                            ins = dve.tensor_scalar(XCS[:, e], XP[:, e, :, 0:SEQ], conv_w[:, e, 0:1], conv_b[:, e:e + 1], ALU.mult, ALU.add)
                        else:
                            ins = dve.scalar_tensor_tensor(XCS[:, e], XP[:, e, :, k:k + SEQ], conv_w[:, e, k:k + 1], XCS[:, e], ALU.mult, ALU.add)
                        ins.then_inc(m_conv.sem, 1)
            sum_rows(dve, 0, run, False, range(TPI))
            front(0)
            with dve.Fori(0, STEPS - 2) as i:
                step(i)
            step(STEPS - 2, left=1)
            step(STEPS - 1, left=0)
            with dve.Fori(0, STEPS) as i:
                dve.wait_ge(m_y_ps.sem, m_y_ps.at(0, i))
                dve.wait_ge(m_out.sem, m_out.before(0, i))
                ym = lambda e: YM[:, e, :]
                for e in range(E2):
                    dve.scalar_tensor_tensor(ym(e), XC[:, e, bass.ds(i * W, W)], m_d[:, e:e + 1], psum[:, 1 + e, :], ALU.mult, ALU.add).then_inc(m_ym.sem, 1)
                for e in range(E2):
                    dve.wait_ge(m_ym.sem, m_ym.at(0, i, e + 1))
                    dve.tensor_tensor(ym(e), ym(e), Z[:, e, bass.ds(i * W, W)], ALU.mult).then_inc(m_ym.sem, 1)
                xt = X[:, bass.ds(i * TPI, TPI), :]
                dve.tensor_tensor(xt, xt, m_bo[:].unsqueeze(1).broadcast_to([P, TPI, D]), ALU.add).then_inc(m_x.sem, 1)
                dve.wait_ge(m_x.sem, m_x.at(0, i, 1))
                dve.wait_ge(m_out.sem, m_out.at(0, i))
                xs = X[:, bass.ds(i * TPI, TPI), :].rearrange("p t d -> p (t d)")
                dve.tensor_tensor(xs, psum[:, 3, :], xs, ALU.add).then_inc(m_x.sem, 1)

        m_xc = signal("m_xc")

        def mamba_scalar(act, layer):
            r = front_run(layer)
            act.wait_ge(m_zero, 1)
            def step(i):
                deviations(act, i, r, ln_eps[:, 0:1])
                act.wait_ge(f_xt_ps.sem, f_xt_ps.at(r, i))
                act.wait_ge(m_in.sem, m_in.before(0, i))
                act.activation(XT[:], psum[:, 0, :], ACT.Copy).then_inc(f_xt.sem, 1)
                act.wait_ge(m_in.sem, m_in.at(0, i))
                act.wait_ge(m_conv.sem, m_conv.before(0, i))
                for e in range(E2):
                    act.activation(XP[:, e, :, TAPS - 1:], psum[:, 1 + e, :].rearrange("p (b q) -> p b q", b=2),
                                   ACT.Identity, bias=b_in[:, e:e + 1]).then_inc(m_xp.sem, 1)
                for e in range(E2):
                    act.activation(Z[:, e, bass.ds(i * W, W)], psum[:, 1 + E2 + e, :], ACT.Sigmoid, bias=b_in[:, E2 + e:E2 + e + 1]).then_inc(m_xp.sem, 1)
                act.wait_ge(m_conv.sem, m_conv.at(0, i))
                act.activation(XC[:, :, bass.ds(i * W, W)], XCS.rearrange("p e b q -> p e (b q)"), ACT.Copy).then_inc(m_xc.sem, 1)
                act.wait_ge(m_u_ps.sem, m_u_ps.at(0, i))
                act.activation(U16[:, bass.ds(i * 2, 2), :], psum[0:STATE, 5, :].rearrange("p (b q) -> p b q", b=2), ACT.Copy).then_inc(m_u.sem, 1)

            def recur(g, first, last):
                for t in range(first, last):
                    if t == 0:
                        act.wait_ge(m_spread, 16 * HALF * (g + 1))
                        act.activation(H[:, g, 0:1], U[:, g, 0:1], ACT.Tanh).then_inc(m_h[g], 1)
                    else:
                        act.wait_ge(m_h[g], t)
                        act.activation(H[:, g, t:t + 1], U[:, g, t:t + 1], ACT.Tanh, bias=H[:, g, t - 1:t]).then_inc(m_h[g], 1)

            with act.Fori(0, STEPS // 2) as i:
                step(i)
            part = SEQ // (STEPS // 2)
            for k in range(STEPS // 2):
                step(STEPS // 2 + k)
                recur(0, part * k, part * k + part)
            recur(1, 0, SEQ)

        def mamba_gpsimd(pool, layer):
            r = front_run(layer)
            gather(pool, experts_before(layer))

        def mamba_sync(sp, layer):
            def spread(g):
                sp.wait_ge(m_u.sem, m_u.at(0, (g + 1) * STEPS // 2 - 1))
                if g:
                    sp.wait_ge(m_spread, 16 * HALF)
                for s in range(HALF):
                    sp.dma_start(U[STATE * s:STATE * s + STATE, g, :], U16[:, HALF * g + s, :]).then_inc(m_spread, 16)

            def collect(g):
                sp.wait_ge(m_h[g], SEQ)
                for s in range(HALF):
                    sp.dma_start(H16[:, HALF * g + s, :], H[STATE * s:STATE * s + STATE, g, :]).then_inc(m_gather, 16)

            spread(0)
            spread(1)
            collect(0)
            sp.wait_ge(m_gather, 16 * HALF)
            collect(1)

        def mamba_tensor(pe, layer):
            r = front_run(layer)
            with pe.Fori(0, STEPS) as i:
                front_tensor(pe, i, r)
                pe.wait_ge(f_xt.sem, f_xt.at(r, i))
                pe.wait_ge(m_xp.sem, m_xp.before(0, i))
                for e in range(2 * E2):
                    mm = pe.matmul(psum[:, 1 + e, :], w_in[:, e, :], XT[:], start=True, stop=True)
                mm.then_inc(m_in.sem, 1)
                pe.wait_ge(m_conv.sem, m_conv.at(0, i))
                pe.wait_ge(m_u.sem, m_u.before(0, i))
                for e in range(E2):
                    mm = pe.matmul(psum[0:STATE, 5, :], m_a[:, e, :], XCS[:, e].rearrange("p b q -> p (b q)"), start=(e == 0), stop=(e == E2 - 1))
                mm.then_inc(m_u_ps.sem, 1)
            def output(i):
                pe.wait_ge(m_ym.sem, m_ym.before(0, i))
                for e in range(E2):
                    mm = pe.matmul(psum[:, 1 + e, :], m_ct[:, e, :], H16[:, bass.ds(i * 2, 2), :].rearrange("p b q -> p (b q)"), start=True, stop=True)
                mm.then_inc(m_y_ps.sem, 1)
                pe.wait_ge(m_ym.sem, m_ym.at(0, i))
                pe.wait_ge(m_x.sem, m_x.before(0, i))
                for j in range(TPI):
                    s = slice(P * j, P * j + P)
                    for e in range(E2):
                        mm = pe.matmul(psum[:, 3, s], YM[:, e, s], m_wo[:, e, :], start=(e == 0), stop=(e == E2 - 1), skip_group_check=True)
                mm.then_inc(m_out.sem, 1)

            for g in range(2):
                pe.wait_ge(m_gather, 16 * HALF * (g + 1))
                with pe.Fori(g * STEPS // 2, (g + 1) * STEPS // 2) as i:
                    output(i)

        used[0] = 0
        NH = 16
        w_qkvt = weight("w_qkvt", [D, 3 * D])
        w_ot = weight("w_ot", [D, D])
        cos = weight("cos", [P, TPI, DH // 2])
        sin = weight("sin", [P, 2, TPI, DH // 2])
        MROW = SPLIT
        SCORE_K = SPLIT + 3
        QKV3 = view([P, 3, TPI, D])
        RT = view([P, 2, TPI, NH, DH])
        RU = view([P, 2, TPI, NH, DH])
        RL = view([P, 2 * TPI * NH, DH])
        RH = view([P, 2 * TPI * NH, 3, DH], BF16)
        QS2 = view([P, TPI * NH, HROWS], BF16)
        KS2 = view([P, TPI * NH, HROWS], BF16)
        QT2 = view([P, 2, 2, NH // 2, SEQ], BF16)
        KT2 = view([P, 2, 2, NH // 2, SEQ], BF16)
        VP2 = view([P, 2, TPI, NH, 32])
        PR2 = view([P, 2, 4, 384])
        REC2 = view([P, SEQ])
        OT2 = view([P, 2, SEQ])
        MX = view([P, TPI, NH])
        ML = view([P, TPI * NH])
        r_zero = semaphore("r_zero")
        r_link = signal("r_link", 10)
        r_qkv_ps = signal("r_qkv_ps", TPI)
        r_qkv = signal("r_qkv", TPI)
        r_split = signal("r_split")
        r_vp = signal("r_vp", 4)
        r_qrows = signal("r_qrows", 3)
        r_krows = signal("r_krows", 3)
        r_tr = signal("r_tr", 12)
        r_qt = signal("r_qt", 8, start=START + 8)
        r_kt = signal("r_kt", 4, start=START + 4)
        r_s1 = signal("r_s1", 2 * NH)
        r_max = signal("r_max", 4 * NH)
        r_mrows = signal("r_mrows", 5)
        r_sc = signal("r_sc", 8, start=START + 8)
        r_exp = signal("r_exp", 8, start=START + 8)
        r_av = signal("r_av", 8, start=START + 8)
        r_rec = signal("r_rec", 2)
        r_ot = signal("r_ot", 2)
        r_y = signal("r_y")
        r_x = signal("r_x")

        TURN_BANKS = (1, 2, 4, 5, 6, 7, 1, 2, 1, 2, 1, 2)

        def rope_vector(dve, layer):
            r = front_run(layer)

            def front(s):
                front_vector(dve, s, r)

            def turn(s):
                link = Order(r_link, 0, s)
                dve.wait_ge(r_qkv.sem, r_qkv.at(0, s))
                for k in range(2):
                    x = QKV3[:, k].rearrange("p t (h d) -> p t h d", d=DH // 2)
                    xh = QKV3[:, k].rearrange("p t (h u d) -> p t h u d", u=2, d=DH // 2)
                    c = cos[:].unsqueeze(2).broadcast_to([P, TPI, 2 * NH, DH // 2])
                    dve.tensor_tensor(RT[:, k].rearrange("p t h (u d) -> p t (h u) d", u=2), x, c, ALU.mult).then_inc(link.sem, link.one())
                    for h in range(2):
                        sn = sin[:, h].unsqueeze(2).broadcast_to([P, TPI, NH, DH // 2])
                        dve.tensor_tensor(RU[:, k, :, :, 4 * h:4 * h + 4], xh[:, :, :, 1 - h, :], sn, ALU.mult).then_inc(link.sem, link.one())
                dve.wait_ge(link.sem, link.so_far())
                dve.tensor_tensor(RT, RT, RU, ALU.add).then_inc(link.sem, link.one())
                dve.wait_ge(link.sem, link.so_far())
                split3(dve, link, RT.rearrange("p s t h d -> p (s t h) d"), RL, RH, r_split, r_krows, 0, s)
                dve.wait_ge(r_split.sem, r_split.at(0, s))
                dve.wait_ge(r_tr.sem, r_tr.before(0, s))
                query_rows(dve, RH[:, 0:TPI * NH], QS2, TPI * NH, r_qrows)
                link.close()

            def largest(s, heads):
                for m in heads:
                    b, h, bank = m // NH, m % NH, 1 + m % 2
                    dve.wait_ge(r_s1.sem, r_s1.at(0, s, m + 1))
                    dve.tensor_reduce(MX[:, 2 * b, h:h + 1], psum[:, bank, 0:128], AX.X, ALU.max, negate=True).then_inc(r_max.sem, 1)
                    dve.tensor_reduce(MX[:, 2 * b + 1, h:h + 1], psum[:, bank, 128:384], AX.X, ALU.max, negate=True).then_inc(r_max.sem, 1)

            def largest_rows(s):
                dve.wait_ge(r_max.sem, r_max.at(0, s))
                m = MX.rearrange("p t h -> p (t h)")
                dve.wait_ge(r_tr.sem, r_tr.at(0, s, 8))
                dve.tensor_copy(QS2[:, :, MROW], m).then_inc(r_mrows.sem, 1)
                dve.wait_ge(r_mrows.sem, r_mrows.at(0, s, 1))
                dve.tensor_tensor(ML, m, QS2[:, :, MROW], ALU.subtract).then_inc(r_mrows.sem, 1)
                dve.wait_ge(r_mrows.sem, r_mrows.at(0, s, 2))
                dve.tensor_copy(QS2[:, :, MROW + 1], ML).then_inc(r_mrows.sem, 1)
                dve.wait_ge(r_mrows.sem, r_mrows.at(0, s, 3))
                dve.tensor_tensor(ML, ML, QS2[:, :, MROW + 1], ALU.subtract).then_inc(r_mrows.sem, 1)
                dve.wait_ge(r_mrows.sem, r_mrows.at(0, s, 4))
                dve.tensor_copy(QS2[:, :, MROW + 2], ML).then_inc(r_mrows.sem, 1)

            def divide(i, b):
                dve.wait_ge(r_av.sem, r_av.at(0, i, 4 * b + 4))
                dve.wait_ge(r_ot.sem, r_ot.at(0, i, b))
                dve.reciprocal(REC2, psum[:, 3, 256:512]).then_inc(r_rec.sem, 1)
                dve.wait_ge(r_rec.sem, r_rec.at(0, i, b + 1))
                dve.wait_ge(r_y.sem, r_y.before(0, i))
                dve.tensor_tensor(OT2[:, b], psum[:, 3, 0:256], REC2, ALU.mult).then_inc(r_ot.sem, 1)

            def keys(s, u):
                for k in range(4):
                    dve.wait_ge(r_tr.sem, r_tr.at(0, s, 2 * k + 2))
                    dve.wait_ge(r_sc.sem, r_sc.before(0, s - 1))
                    dve.tensor_copy(KT2[:, u, k // 2, 4 * (k % 2):4 * (k % 2) + 4], psum_b16(TURN_BANKS[2 * k + 1])).then_inc(r_kt.sem, 1)

            def add(i):
                dve.wait_ge(r_y.sem, r_y.at(0, i))
                xs = X[:, bass.ds(i * TPI, TPI), :].rearrange("p t d -> p (t d)")
                dve.tensor_tensor(xs, psum[:, 0, :], xs, ALU.add).then_inc(r_x.sem, 1)

            def step(i, u, first=False, left=STEPS):
                if left >= 1:
                    largest(i + 1, range(0, 8))
                if not first:
                    add(i - 1)
                if left >= 1:
                    largest(i + 1, range(8, 2 * NH))
                divide(i, 0)
                if left >= 1:
                    largest_rows(i + 1)
                if left >= 2:
                    turn(i + 2)
                divide(i, 1)
                if left >= 2:
                    keys(i + 2, u)
                if left >= 3:
                    front(i + 3)

            front(0)
            turn(0)
            front(1)
            keys(0, 0)
            largest(0, range(2 * NH))
            largest_rows(0)
            turn(1)
            front(2)
            keys(1, 1)
            step(0, 0, first=True)
            step(1, 1)
            with dve.Fori(1, STEPS // 2 - 2) as i2:
                for u in range(2):
                    step(i2 * 2 + u, u)
            for i in range(STEPS - 4, STEPS):
                step(i, i % 2, left=STEPS - 1 - i)
            add(STEPS - 1)
            dve.wait_ge(r_x.sem, r_x.end(0))

        def rope_scalar(act, layer):
            r = front_run(layer)

            def tokens(s):
                act.wait_ge(f_xt_ps.sem, f_xt_ps.at(r, s))
                act.wait_ge(r_qkv_ps.sem, r_qkv_ps.before(0, s))
                act.activation(XT[:], psum[:, 0, :], ACT.Copy).then_inc(f_xt.sem, 1)

            def projected(s, j):
                act.wait_ge(r_qkv_ps.sem, r_qkv_ps.at(0, s, j + 1))
                if j == 0:
                    act.wait_ge(r_split.sem, r_split.before(0, s))
                    act.wait_ge(r_vp.sem, r_vp.before(0, s))
                act.activation(QKV3[:, :, j, :], psum[:, max(0, j - 1), 0:384].rearrange("p (s c) -> p s c", s=3), ACT.Copy).then_inc(r_qkv.sem, 1)

            def rows(s):
                act.wait_ge(r_split.sem, r_split.at(0, s))
                act.wait_ge(r_tr.sem, r_tr.before(0, s))
                key_rows(act, RH[:, TPI * NH:], KS2, r_krows)

            def transposed(s, u, k):
                act.wait_ge(r_tr.sem, r_tr.at(0, s, k + 1))
                if k < 8:
                    b, hh = k // 4, k // 2 % 2
                    act.wait_ge(r_sc.sem, r_sc.before(0, s - 1))
                else:
                    b, hh = (k - 8) // 2, k % 2
                    act.wait_ge(r_s1.sem, r_s1.at(0, s))
                act.activation(QT2[:, u, b, 4 * hh:4 * hh + 4], psum_b16(TURN_BANKS[k]), ACT.Copy).then_inc(r_qt.sem, 1)

            def weigh(i, g):
                act.wait_ge(r_sc.sem, r_sc.at(0, i, g + 1))
                act.wait_ge(r_av.sem, r_av.at(0, i, g - 1))
                act.activation(PR2[:, g % 2], psum[:, 4:8, 0:384], ACT.Exp, scale=DH ** -0.5).then_inc(r_exp.sem, 1)

            def step(i, u, left=STEPS):
                weigh(i, 0)
                weigh(i, 1)
                if left >= 2:
                    tokens(i + 2)
                weigh(i, 2)
                if left >= 2:
                    projected(i + 2, 0)
                weigh(i, 3)
                if left >= 2:
                    projected(i + 2, 1)
                weigh(i, 4)
                if left >= 2:
                    projected(i + 2, 2)
                    projected(i + 2, 3)
                weigh(i, 5)
                weigh(i, 6)
                if left >= 1:
                    transposed(i + 1, 1 - u, 8)
                    transposed(i + 1, 1 - u, 9)
                weigh(i, 7)
                if left >= 1:
                    transposed(i + 1, 1 - u, 10)
                    transposed(i + 1, 1 - u, 11)
                if left >= 2:
                    rows(i + 2)
                    for k in range(0, 8, 2):
                        transposed(i + 2, u, k)

            tokens(0)
            for j in range(TPI):
                projected(0, j)
            rows(0)
            for k in range(0, 8, 2):
                transposed(0, 0, k)
            tokens(1)
            for j in range(TPI):
                projected(1, j)
            for k in range(8, 12):
                transposed(0, 0, k)
            rows(1)
            for k in range(0, 8, 2):
                transposed(1, 1, k)
            with act.Fori(0, STEPS // 2 - 2) as i2:
                for u in range(2):
                    step(i2 * 2 + u, u)
            for i in range(STEPS - 4, STEPS):
                step(i, i % 2, left=STEPS - 1 - i)

        def rope_gpsimd(pool, layer):
            r = front_run(layer)
            pool.memset(VP2, 0.0).then_inc(r_zero, 1)
            pool.memset(QS2, 0.0).then_inc(r_zero, 1)
            pool.memset(KS2, 0.0).then_inc(r_zero, 1)
            pool.wait_ge(r_zero, 3)
            pool.memset(KS2[:, :, MROW:MROW + 3], 1.0).then_inc(r_zero, 1)
            pool.wait_ge(r_zero, 4)

            def norm(s):
                inverse_deviations(pool, s, r)

            def values(s, u):
                pool.wait_ge(r_qkv.sem, r_qkv.at(0, s))
                pool.wait_ge(r_av.sem, r_av.before(0, s - 1))
                stand(pool)
                for n in range(4):
                    pool.tensor_copy(VP2[:, u, :, n:NH:4, DH * n:DH * n + DH],
                                     QKV3[:, 2].rearrange("p t (h d) -> p t h d", d=DH)[:, :, n:NH:4, :]).then_inc(r_vp.sem, 1)

            norm(0)
            values(0, 0)
            norm(1)
            values(1, 1)
            norm(2)
            with pool.Fori(0, STEPS // 2 - 2) as i2:
                for u in range(2):
                    norm(i2 * 2 + u + 3)
                    values(i2 * 2 + u + 2, u)
            norm(STEPS - 1)
            values(STEPS - 2, 0)
            values(STEPS - 1, 1)

        def rope_tensor(pe, layer):
            r = front_run(layer)
            pe.wait_ge(r_zero, 4)

            def project(s, j):
                if j == 0:
                    pe.wait_ge(f_xt.sem, f_xt.at(r, s))
                elif j == 1:
                    pe.wait_ge(r_qkv.sem, r_qkv.at(0, s, 1))
                else:
                    pe.wait_ge(r_max.sem, r_max.before(0, s))
                    pe.wait_ge(r_qt.sem, r_qt.at(0, s - 1, 4))
                    pe.wait_ge(r_kt.sem, r_kt.at(0, s - 1))
                pe.matmul(psum[:, max(0, j - 1), 0:384], XT[:, P * j:P * j + P], w_qkvt[:], start=True, stop=True, skip_group_check=True).then_inc(r_qkv_ps.sem, 1)

            def transposes(s, k):
                if k == 0:
                    pe.wait_ge(r_qrows.sem, r_qrows.at(0, s))
                    pe.wait_ge(r_krows.sem, r_krows.at(0, s))
                if k == 8:
                    pe.wait_ge(r_mrows.sem, r_mrows.at(0, s))
                if k == 2:
                    pe.wait_ge(r_exp.sem, r_exp.before(0, s - 1))
                elif k == 7:
                    pe.wait_ge(r_kt.sem, r_kt.at(0, s, 1))
                elif k in (0, 1) or k > 5:
                    pe.wait_ge(r_qt.sem, r_qt.at(0, s, {0: 0, 1: 0, 6: 1}.get(k, max(4, k - 5))))
                if k == 8:
                    pe.wait_ge(r_kt.sem, r_kt.at(0, s))
                b, hh, rows = (k // 4, k // 2 % 2, (QS2, KS2)[k % 2]) if k < 8 else ((k - 8) // 2, k % 2, QS2)
                for c in range(4):
                    for t in range(2):
                        h = (2 * b + t) * NH + 8 * hh + 2 * c
                        mm = pe.transpose(psum_b16(TURN_BANKS[k])[:, c, P * t:P * t + P],
                                          rows[:, h:h + 2, :].rearrange("p h k -> p (h k)"), identb[:])
                mm.then_inc(r_tr.sem, 1)

            def head(t, u, b, h):
                return t[HROWS * (h % 2):HROWS * (h % 2) + HROWS, u, b, h // 2]

            def largest(s, u, heads):
                for m in heads:
                    b, h, bank = m // NH, m % NH, 1 + m % 2
                    if m == 0:
                        pe.wait_ge(r_qt.sem, r_qt.at(0, s, 4))
                        pe.wait_ge(r_kt.sem, r_kt.at(0, s))
                    pe.wait_ge(r_max.sem, r_max.at(0, s, 2 * (m - 1)))
                    q, kk = head(QT2, u, b, h), head(KT2, u, b, h)
                    pe.matmul(psum[:, bank, 0:128], q[0:SPLIT, 0:128], kk[0:SPLIT, 0:128], start=True, stop=False, skip_group_check=True)
                    pe.matmul(psum[:, bank, 128:384], q[0:SPLIT, 128:256], kk[0:SPLIT, :], start=False, stop=False, skip_group_check=True)
                    v = psum[:, bank, 0:384].rearrange("p (a q) -> p a q", q=P)[:, 0:3:2, :]
                    pe.matmul(v, identb[:], mask_qk[:].unsqueeze(1).broadcast_to([P, 2, P]), start=False, stop=True, skip_group_check=True).then_inc(r_s1.sem, 1)

            def scores(i, u, g, between=None):
                b, n = g // 4, g % 4
                if g == 0:
                    pe.wait_ge(r_qt.sem, r_qt.at(0, i))
                    pe.wait_ge(r_kt.sem, r_kt.at(0, i))
                pe.wait_ge(r_exp.sem, r_exp.at(0, i, g))
                for rr in range(4):
                    head_scores(pe, 4 + rr, head(KT2, u, b, n + 4 * rr), head(QT2, u, b, n + 4 * rr), SCORE_K)
                    if between is not None:
                        between()
                for rr in range(4):
                    mm = mask_scores(pe, 4 + rr)
                mm.then_inc(r_sc.sem, 1)

            def values(i, u, g, between=None):
                b, n = g // 4, g % 4
                pe.wait_ge(r_exp.sem, r_exp.at(0, i, g + 1))
                if g == 0:
                    pe.wait_ge(r_vp.sem, r_vp.at(0, i))
                if n == 0:
                    pe.wait_ge(r_ot.sem, r_ot.at(0, i, b))
                weigh_values(pe, n, lambda kt, h: VP2[:, u, 2 * b + kt, h, :], PR2[:, g % 2], between).then_inc(r_av.sem, 1)

            def output(i):
                pe.wait_ge(r_ot.sem, r_ot.at(0, i))
                for j in range(TPI):
                    mm = pe.matmul(psum[:, 0, P * j:P * j + P], OT2[:, j // 2, P * (j % 2):P * (j % 2) + P], w_ot[:],
                                   start=True, stop=True, skip_group_check=True)
                mm.then_inc(r_y.sem, 1)

            def step(i, u, first=False, left=STEPS):
                heads = iter(range(2 * NH))

                def one():
                    largest(i + 1, 1 - u, [next(heads)])

                if left >= 1:
                    pe.wait_ge(r_qt.sem, r_qt.at(0, i + 1, 3))
                    pe.wait_ge(r_kt.sem, r_kt.at(0, i + 1, 3))
                scores(i, u, 0)
                for g in range(8):
                    between = one if g < 4 and left >= 1 else None
                    if g < 7:
                        scores(i, u, g + 1, between)
                    if g == 0 and not first:
                        output(i - 1)
                    if g == 1 and left >= 2:
                        pe.wait_ge(r_x.sem, r_x.before(0, i))
                        pe.wait_ge(r_qkv.sem, r_qkv.before(0, i + 2))
                        front_tensor(pe, i + 2, r)
                    if g in (2, 3) and left >= 2:
                        project(i + 2, g - 2)
                    if g == 4 and left >= 2:
                        project(i + 2, 2)
                        project(i + 2, 3)
                    if g in (6, 7) and left >= 1:
                        for k in range(2):
                            transposes(i + 1, 8 + 2 * (g - 6) + k)
                    if between is not None:
                        one()
                    values(i, u, g, between)
                if left >= 2:
                    for k in range(8):
                        transposes(i + 2, k)

            front_tensor(pe, 0, r)
            for j in range(TPI):
                project(0, j)
            pe.wait_ge(r_qkv.sem, r_qkv.at(0, 0))
            for k in range(8):
                transposes(0, k)
            front_tensor(pe, 1, r)
            project(1, 0)
            project(1, 1)
            largest(0, 0, range(2 * NH))
            project(1, 2)
            project(1, 3)
            pe.wait_ge(r_qkv.sem, r_qkv.at(0, 1))
            for k in range(8, 12):
                transposes(0, k)
            for k in range(8):
                transposes(1, k)
            step(0, 0, first=True)
            step(1, 1)
            with pe.Fori(1, STEPS // 2 - 2) as i2:
                for u in range(2):
                    step(i2 * 2 + u, u)
            for i in range(STEPS - 4, STEPS):
                step(i, i % 2, left=STEPS - 1 - i)
            output(STEPS - 1)

        NE = 160
        TOPK = 8
        INTER = 64
        ROUTED_SCALE = 2.5
        SLOT_TILES = -(-(TOK * TOPK // P + NE) // 8) * 8
        GROUP = 4
        GROUPS = SLOT_TILES // GROUP
        UNROLL = 4
        GSTEPS = GROUPS // UNROLL
        assert GROUPS % UNROLL == 0 and GROUPS <= P
        EW = INTER + D
        router_t = weight("router_t", [D, NE])
        e_bias = weight("e_bias", [P, NE])
        sh_gate = weight("sh_gate", [D, INTER])
        sh_down = weight("sh_down", [INTER, D])
        earlier_tokens = weight("earlier_tokens", [P, P], BF16)
        other_tokens = weight("other_tokens", [P, P], BF16)
        slot_tile = weight("slot_tile", [P, GROUP])
        onesb = sb("onesb", [P, P], BF16)
        zeros = sb("zeros", [P, 512])
        slot_rows = nc.dram_tensor("slot_rows", (SLOT_TILES * P, D), F32).ap()
        slot_results = nc.dram_tensor("slot_results", (SLOT_TILES * P, D), F32).ap()
        normalised = nc.dram_tensor("normalised", (TOK, D), F32).ap()
        M8 = sb("M8", [P, TPI, TOPK])
        SUM = sb("SUM", [P, TPI])
        S8 = sb("S8", [P, TPI, TOPK])
        W8 = sb("W8", [P, TPI, TOPK])
        SLOTS = sb("SLOTS", [P, TILES, TOPK], I32)
        WEIGHTS = sb("WEIGHTS", [P, TILES, TOPK])
        SLOTS_NOW = sb("SLOTS_NOW", [P, TPI, TOPK], I32)
        EXPERT_COL = sb("EXPERT_COL", [P, GROUP])
        EXPERT = sb("EXPERT", [1, GROUP, P], I32)
        used[0] = 0
        MASK = view([P, TILES, NE], BF16)
        COMB = view([P, TILES, NE])
        step_part = used[0]
        PROB = view([P, TPI, NE])
        REST = view([P, TPI, NE])
        SG = view([P, TPI * INTER])
        HE = view([P, TPI * INTER])
        HT = view([INTER, W])
        used[0] = step_part
        XNS = view([P, TPI, D])
        SLOTM = view([P, TPI, NE])
        JUNK = view([P, TOPK, NE], BF16)
        used[0] = step_part
        COUNT = view([P, NE], I32)
        NTILES = view([P, NE])
        INCL = view([P, NE])
        FIRST = view([P, NE])
        JUNK2 = view([P, GROUP, NE], BF16)
        used[0] = max(used[0], step_part + 2 * TPI * NE + 2 * TPI * INTER + W)
        XSB = view([P, UNROLL, GROUP, D])
        EWB = view([P, UNROLL, GROUP, EW])
        XSBT = view([P, UNROLL, GROUP * P])
        SGB = view([P, 2, GROUP * INTER])
        HEB = view([P, 2, GROUP * INTER])
        HTB = view([INTER, 2, GROUP * P])
        YSB = view([P, UNROLL, GROUP, D])
        assert used[0] <= GATHER_AT
        used[0] = GATHER_AT
        GATHERED = view([P, TPI, TOPK, D])
        cleared = semaphore("cleared")
        e_saved = signal("e_saved", 16)
        e_lg = signal("e_lg")
        e_logit = signal("e_logit", 2)
        e_prob = signal("e_prob")
        e_link = signal("e_link", 2 * TPI + 5)
        e_comb = signal("e_comb")
        e_mask = signal("e_mask")
        e_x = signal("e_x")
        e_h = signal("e_h")
        e_sg = signal("e_sg")
        e_he = signal("e_he")
        e_tr = signal("e_tr")
        e_ht = signal("e_ht")
        e_y = signal("e_y")
        e_cnt = signal("e_cnt")
        o_link = signal("o_link", 9, 1)
        o_row = signal("o_row", 1, 1)
        o_expert = signal("o_expert", 1, 1)
        s_xn = [signal(f"s_xn{j}", 16) for j in range(TPI)]
        s_a = signal("s_a", TPI)
        s_slotm = signal("s_slotm", TPI)
        s_s8 = signal("s_s8", TPI)
        s_idx = signal("s_idx", TPI)
        s_w = signal("s_w", TPI * TOPK)
        s_wk = signal("s_wk", TPI)
        s_rows = [signal(f"s_rows{j}", 16 * TOPK, start=0) for j in range(TPI)]
        c_ld = [signal(f"c_ld{p}", 16, GSTEPS, start=0) for p in range(UNROLL)]
        c_ew = [[signal(f"c_ew{h}{p}", (32, 16, 16)[h], GSTEPS, start=(START, START, 0)[h]) for p in range(UNROLL)] for h in range(3)]
        c_st = [signal(f"c_st{p}", 16, GSTEPS) for p in range(UNROLL)]
        c_tr = signal("c_tr", UNROLL, GSTEPS)
        c_xt = signal("c_xt", UNROLL, GSTEPS)
        c_h = signal("c_h", UNROLL, GSTEPS)
        c_sg = signal("c_sg", UNROLL, GSTEPS)
        c_he = signal("c_he", UNROLL, GSTEPS)
        c_htr = signal("c_htr", UNROLL, GSTEPS)
        c_ht = signal("c_ht", UNROLL, GSTEPS)
        c_y = signal("c_y", UNROLL, GSTEPS)
        c_ysb = signal("c_ysb", UNROLL, GSTEPS)
        g_idx = signal("g_idx", TPI)
        g_w = signal("g_w", TPI)
        g_sum = signal("g_sum", TPI * TOPK, start=START + TPI * TOPK)

        def moe_vector(dve, layer):
            r, run = front_run(layer), earlier(layer)

            def route(i, last):
                if not last:
                    front_stats(dve, i + 1, r)
                dve.wait_ge(e_lg.sem, e_lg.at(run, i))
                dve.wait_ge(e_comb.sem, e_comb.before(run, i))
                for k in range(2):
                    dve.tensor_tensor(PROB[:, 2 * k:2 * k + 2, :], psum[:, 6 + k, 0:2 * NE].rearrange("p (t c) -> p t c", t=2),
                                      e_bias[:].unsqueeze(1).broadcast_to([P, 2, NE]), ALU.add).then_inc(e_logit.sem, 1)
                if not last:
                    front_scale(dve, i + 1, r, e_saved, run)
                dve.wait_ge(e_sg.sem, e_sg.at(run, i))
                dve.wait_ge(e_tr.sem, e_tr.before(run, i))
                dve.tensor_tensor(HE, psum[:, 1, 0:TPI * INTER], SG, ALU.mult).then_inc(e_he.sem, 1)
                link = Order(e_link, run, i)
                dve.wait_ge(e_prob.sem, e_prob.at(run, i))
                stand(dve)
                for j in range(TPI):
                    dve.max(M8[:, j], PROB[:, j]).then_inc(link.sem, link.one())
                dve.wait_ge(link.sem, link.so_far())
                stand(dve)
                dve.tensor_reduce(SUM[:], M8[:], AX.X, ALU.add).then_inc(link.sem, link.one())
                for j in range(TPI):
                    dve.match_replace(REST[:, j], M8[:, j], PROB[:, j], -1.0).then_inc(link.sem, link.one())
                dve.wait_ge(link.sem, link.so_far())
                dve.tensor_scalar(SUM[:], SUM[:], 1e-9, None, ALU.add).then_inc(link.sem, link.one())
                dve.tensor_scalar(MASK[:, bass.ds(i * TPI, TPI), :], REST, 0.0, None, ALU.is_lt).then_inc(e_mask.sem, 1)
                dve.wait_ge(link.sem, link.so_far())
                dve.reciprocal(SUM[:], SUM[:]).then_inc(link.sem, link.one())
                dve.wait_ge(e_mask.sem, e_mask.at(run, i))
                dve.scalar_tensor_tensor(REST, REST, 0.0, PROB, ALU.is_lt, ALU.mult).then_inc(link.sem, link.one())
                dve.wait_ge(link.sem, link.so_far())
                dve.tensor_scalar(SUM[:], SUM[:], ROUTED_SCALE, None, ALU.mult).then_inc(link.sem, link.one())
                dve.wait_ge(link.sem, link.so_far())
                dve.tensor_tensor(COMB[:, bass.ds(i * TPI, TPI), :], REST, SUM[:].unsqueeze(2).broadcast_to([P, TPI, NE]), ALU.mult).then_inc(e_comb.sem, 1)
                dve.wait_ge(e_y.sem, e_y.at(run, i))
                xs = X[:, bass.ds(i * TPI, TPI), :].rearrange("p t d -> p (t d)")
                dve.tensor_tensor(xs, psum[:, 5, :], xs, ALU.add).then_inc(e_x.sem, 1)
                link.close()

            front_stats(dve, 0, r)
            front_scale(dve, 0, r, e_saved, run)
            with dve.Fori(0, STEPS - 1) as i:
                route(i, False)
            route(STEPS - 1, True)

            link = Order(o_link, run, 0)
            dve.wait_ge(e_cnt.sem, e_cnt.end(run))
            dve.wait_ge(e_comb.sem, e_comb.end(run))
            dve.tensor_copy(COUNT, psum[:, 2, 0:NE]).then_inc(link.sem, link.one())
            dve.wait_ge(link.sem, link.so_far())
            dve.tensor_scalar(COUNT, COUNT, P - 1, None, ALU.add).then_inc(link.sem, link.one())
            dve.wait_ge(link.sem, link.so_far())
            dve.tensor_scalar(COUNT, COUNT, 7, None, ALU.arith_shift_right).then_inc(link.sem, link.one())
            dve.wait_ge(link.sem, link.so_far())
            dve.tensor_copy(NTILES, COUNT).then_inc(link.sem, link.one())
            dve.wait_ge(link.sem, link.so_far())
            dve.tensor_tensor_scan(INCL, ones_row[:], NTILES, 0.0, ALU.mult, ALU.add).then_inc(link.sem, link.one())
            dve.wait_ge(link.sem, link.so_far())
            dve.tensor_tensor(FIRST, INCL, NTILES, ALU.subtract).then_inc(link.sem, link.one())
            for q in range(GROUP):
                ins = dve.scalar_tensor_tensor(JUNK2[:, q], INCL, slot_tile[:, q:q + 1], ones_row[:], ALU.is_le, ALU.mult, accum_out=EXPERT_COL[:, q:q + 1])
            ins.then_inc(link.sem, link.one())
            dve.drain()
            dve.wait_ge(link.sem, link.so_far())
            dve.tensor_scalar(FIRST, FIRST, float(P), None, ALU.mult).then_inc(link.sem, link.one())
            dve.tensor_scalar(EXPERT_COL[:], EXPERT_COL[:], NE - 1.0, None, ALU.min).then_inc(link.sem, link.one())
            dve.wait_ge(o_row.sem, o_row.at(run, 0))
            dve.tensor_copy(EXPERT[:], psum[0:1, 4, :].rearrange("p (q g) -> p q g", q=GROUP)).then_inc(o_expert.sem, 1)
            link.close()

            def place(i, first):
                for j in range(TPI):
                    t = bass.ds(i * TPI + j, 1)
                    dve.wait_ge(s_a.sem, s_a.at(run, i, j + 1))
                    dve.scalar_tensor_tensor(SLOTM[:, j], psum[:, 2, 0:NE], 1.0, MASK[:, t, :].rearrange("p a e -> p (a e)"),
                                             ALU.add, ALU.mult).then_inc(s_slotm.sem, 1)
                    dve.wait_ge(s_slotm.sem, s_slotm.at(run, i, j + 1))
                    stand(dve)
                    dve.max(S8[:, j], SLOTM[:, j]).then_inc(s_s8.sem, 1)
                    dve.wait_ge(s_s8.sem, s_s8.at(run, i, j + 1))
                    if not first:
                        dve.wait_ge(s_rows[j].sem, s_rows[j].before(2 * run, i))
                    dve.tensor_scalar(SLOTS_NOW[:, j], S8[:, j], -1.0, None, ALU.add).then_inc(s_idx.sem, 1)
                    dve.tensor_scalar(SLOTS[:, t, :].rearrange("p a k -> p (a k)"), S8[:, j], -1.0, None, ALU.add)
                    dve.wait_ge(s_w.sem, s_w.at(run, i, TOPK * j))
                    for k in range(TOPK):
                        dve.scalar_tensor_tensor(JUNK[:, k], SLOTM[:, j], S8[:, j, k:k + 1], COMB[:, t, :].rearrange("p a e -> p (a e)"),
                                                 ALU.is_equal, ALU.mult, accum_out=W8[:, j, k:k + 1]).then_inc(s_w.sem, 1)
                    dve.wait_ge(s_w.sem, s_w.at(run, i, TOPK * j + TOPK))
                    dve.tensor_copy(WEIGHTS[:, t, :].rearrange("p a k -> p (a k)"), W8[:, j]).then_inc(s_wk.sem, 1)

            place(0, True)
            with dve.Fori(1, STEPS) as i:
                place(i, False)

            def silu(g, p):
                dve.wait_ge(c_sg.sem, c_sg.at(run, g, p + 1))
                dve.wait_ge(c_htr.sem, c_htr.at(run, g, p - 1))
                dve.tensor_tensor(HEB[:, p % 2], psum[:, 2, 256 * (p % 2):256 * (p % 2) + 256], SGB[:, p % 2], ALU.mult).then_inc(c_he.sem, 1)

            def evacuate(g, p):
                dve.wait_ge(c_htr.sem, c_htr.at(run, g, p + 1))
                dve.wait_ge(c_y.sem, c_y.at(run, g, p - 1))
                dve.tensor_copy(HTB[:, p % 2], psum[0:INTER, 3 + p % 2, :]).then_inc(c_ht.sem, 1)

            def results(g, p):
                dve.wait_ge(c_y.sem, c_y.at(run, g, p + 1))
                dve.wait_ge(c_st[p].sem, c_st[p].before(run, g))
                dve.tensor_copy(YSB[:, p], psum[:, 5 + p % 2, :].rearrange("p (q d) -> p q d", q=GROUP)).then_inc(c_ysb.sem, 1)

            silu(0, 0)
            with dve.Fori(0, GSTEPS - 1) as g:
                for p in range(UNROLL):
                    evacuate(g, p)
                    silu(g + (p + 1) // UNROLL, (p + 1) % UNROLL)
                    results(g, p)
            for p in range(UNROLL):
                evacuate(GSTEPS - 1, p)
                if p < UNROLL - 1:
                    silu(GSTEPS - 1, p + 1)
                results(GSTEPS - 1, p)

            dve.wait_ge(s_wk.sem, s_wk.end(run))
            for j in range(TPI):
                dve.tensor_copy(SLOTS_NOW[:, j], SLOTS[:, j]).then_inc(g_idx.sem, 1)

        def sum_rows(dve, i, run, last, tiles):
            for j in tiles:
                x = X[:, bass.ds(i * TPI + j, 1), :].rearrange("p a d -> p (a d)")
                if j == 0:
                    for t in range(TPI):
                        dve.tensor_copy(W8[:, t], WEIGHTS[:, bass.ds(i * TPI + t, 1), :].rearrange("p a k -> p (a k)")).then_inc(g_w.sem, 1)
                    dve.wait_ge(g_w.sem, g_w.at(run, i))
                dve.wait_ge(s_rows[j].sem, s_rows[j].at(2 * run + 1, i))
                if not last:
                    dve.tensor_copy(SLOTS_NOW[:, j], SLOTS[:, bass.ds((i + 1) * TPI + j, 1), :].rearrange("p a k -> p (a k)")).then_inc(g_idx.sem, 1)
                for k in range(TOPK):
                    if k:
                        dve.wait_ge(g_sum.sem, g_sum.at(run, i, TOPK * j + k))
                    dve.scalar_tensor_tensor(x, GATHERED[:, j, k], W8[:, j, k:k + 1], x, ALU.mult, ALU.add).then_inc(g_sum.sem, 1)

        def summed(dve, i, run):
            dve.wait_ge(g_sum.sem, g_sum.at(run, i))
            stand(dve)

        def gather(pool, run):
            with pool.Fori(0, STEPS) as i:
                for j in range(TPI):
                    pool.wait_ge(g_idx.sem, g_idx.at(run, i, j + 1))
                    pool.wait_ge(g_sum.sem, g_sum.at(run, i, TOPK * (j + 1 - TPI)))
                    stand(pool)
                    for k in range(TOPK):
                        pool.indirect_dma_start(out=GATHERED[:, j, k], out_offset=None, in_=slot_results,
                                                in_offset=bass.IndirectOffsetOnAxis(ap=SLOTS_NOW[:, j, k:k + 1], axis=0)).then_inc(s_rows[j].sem, 16)

        def moe_scalar(act, layer):
            r, run = front_run(layer), earlier(layer)

            def tokens(i):
                act.wait_ge(f_xt_ps.sem, f_xt_ps.at(r, i))
                act.wait_ge(e_h.sem, e_h.before(run, i))
                act.activation(XT[:], psum[:, 0, :], ACT.Copy).then_inc(f_xt.sem, 1)

            def route(i, last):
                act.wait_ge(e_h.sem, e_h.at(run, i))
                act.wait_ge(e_he.sem, e_he.before(run, i))
                act.activation(SG, psum[:, 1, 0:TPI * INTER], ACT.Sigmoid).then_inc(e_sg.sem, 1)
                act.wait_ge(e_logit.sem, e_logit.at(run, i))
                act.activation(PROB, PROB, ACT.Sigmoid).then_inc(e_prob.sem, 1)
                if not last:
                    tokens(i + 1)
                act.wait_ge(e_tr.sem, e_tr.at(run, i))
                act.wait_ge(e_y.sem, e_y.before(run, i))
                act.activation(HT, psum[0:INTER, 3, :], ACT.Copy).then_inc(e_ht.sem, 1)

            tokens(0)
            with act.Fori(0, STEPS - 1) as i:
                route(i, False)
            route(STEPS - 1, True)

            def transposed(g, p):
                act.wait_ge(c_tr.sem, c_tr.at(run, g, p + 1))
                act.wait_ge(c_h.sem, c_h.at(run, g, p - 1))
                act.activation(XSBT[:, p], psum[:, p % 2, :], ACT.Copy).then_inc(c_xt.sem, 1)

            def sigmoid(g, p):
                act.wait_ge(c_h.sem, c_h.at(run, g, p + 1))
                act.wait_ge(c_he.sem, c_he.at(run, g, p - 1))
                act.activation(SGB[:, p % 2], psum[:, 2, 256 * (p % 2):256 * (p % 2) + 256], ACT.Sigmoid).then_inc(c_sg.sem, 1)

            def store(g, p):
                act.wait_ge(c_ysb.sem, c_ysb.at(run, g, p))
                act.dma_start(rows_of_group(slot_results, g * UNROLL + p - 1), YSB[:, (p - 1) % UNROLL]).then_inc(c_st[(p - 1) % UNROLL].sem, 16)

            act.wait_ge(o_expert.sem, o_expert.at(run, 0))
            for p in range(3):
                expert_weights(act, 0, p, (2,))
            transposed(0, 0)
            transposed(0, 1)
            sigmoid(0, 0)

            def group(g, p, first=False, left=UNROLL):
                if left >= 2:
                    transposed(g + (p + 2) // UNROLL, (p + 2) % UNROLL)
                if left >= 3:
                    weights_ahead(act, run, g, p, 2)
                if left >= 1:
                    sigmoid(g + (p + 1) // UNROLL, (p + 1) % UNROLL)
                if not first:
                    store(g, p)

            for p in range(UNROLL):
                group(0, p, first=(p == 0))
            with act.Fori(1, GSTEPS - 1) as g:
                for p in range(UNROLL):
                    group(g, p)
            for p in range(UNROLL):
                group(GSTEPS - 1, p, left=UNROLL - 1 - p)
            store(GSTEPS - 1, UNROLL)

        def moe_gpsimd(pool, layer):
            r, run = front_run(layer), earlier(layer)
            with pool.Fori(0, STEPS) as i:
                inverse_deviations(pool, i, r)
            pool.wait_ge(cleared, 16)
            with pool.Fori(0, STEPS) as i:
                for j in range(TPI):
                    pool.wait_ge(s_idx.sem, s_idx.at(run, i, j + 1))
                    pool.wait_ge(s_xn[j].sem, s_xn[j].at(run, i))
                    stand(pool)
                    for k in range(TOPK):
                        pool.indirect_dma_start(out=slot_rows, out_offset=bass.IndirectOffsetOnAxis(ap=SLOTS_NOW[:, j, k:k + 1], axis=0),
                                                in_=XNS[:, j], in_offset=None).then_inc(s_rows[j].sem, 16)
            for j in range(TPI):
                pool.wait_ge(s_rows[j].sem, s_rows[j].end(2 * run))

            def load(g, p):
                pool.dma_start(XSB[:, p], rows_of_group(slot_rows, g * UNROLL + p)).then_inc(c_ld[p].sem, 16)

            for p in range(UNROLL):
                load(0, p)
            pool.wait_ge(o_expert.sem, o_expert.at(run, 0))
            for p in range(3):
                expert_weights(pool, 0, p, (3,))
            with pool.Fori(0, GSTEPS - 1) as g:
                for p in range(UNROLL):
                    pool.wait_ge(c_tr.sem, c_tr.at(run, g, p + 1))
                    stand(pool)
                    load(g + 1, p)
                    weights_ahead(pool, run, g, p, 3)
            for p in range(UNROLL - 3):
                weights_ahead(pool, run, GSTEPS - 1, p, 3)
            for p in range(UNROLL):
                pool.wait_ge(c_st[p].sem, c_st[p].end(run))

        def rows_of_group(dram, g):
            return dram[bass.ds(g * (GROUP * P), GROUP * P), :].rearrange("(q s) d -> s q d", q=GROUP)

        def expert_weights(eng, g, p, tiles):
            for q in tiles:
                e = eng.value_load(EXPERT[0:1, q, bass.ds(g * UNROLL + p, 1)], min_val=0, max_val=NE - 1)
                eng.dma_start(EWB[:, p, q], a["expert_w"][bass.ds(e * P, P), :]).then_inc(c_ew[max(q - 1, 0)][p].sem, 16)

        def weights_ahead(eng, run, g, p, q):
            eng.wait_ge(c_y.sem, c_y.at(run, g, p))
            stand(eng)
            expert_weights(eng, g + (p + 3) // UNROLL, (p + 3) % UNROLL, (q,))

        def moe_sync(sp, layer):
            r, run = front_run(layer), earlier(layer)
            with sp.Fori(0, STEPS) as i:
                sp.wait_ge(f_xn.sem, f_xn.at(r, i))
                sp.dma_start(normalised[bass.ds(i * W, W), :].rearrange("(t p) d -> p t d", p=P), XN[:]).then_inc(e_saved.sem, 16)
            sp.wait_ge(e_saved.sem, e_saved.end(run))
            sp.wait_ge(o_row.sem, o_row.at(run, 0))
            for j in range(TPI):
                sp.dma_start(XNS[:, j], normalised[P * j:P * j + P, :]).then_inc(s_xn[j].sem, 16)
            with sp.Fori(1, STEPS) as i:
                for j in range(TPI):
                    sp.wait_ge(s_rows[j].sem, s_rows[j].before(2 * run, i))
                    sp.dma_start(XNS[:, j], normalised[bass.ds(i * W + j * P, P), :]).then_inc(s_xn[j].sem, 16)
            sp.wait_ge(o_expert.sem, o_expert.at(run, 0))

            for p in range(UNROLL):
                expert_weights(sp, 0, p, (0, 1))
            with sp.Fori(0, GSTEPS - 1) as g:
                for p in range(UNROLL):
                    sp.wait_ge(c_y.sem, c_y.at(run, g, p + 1))
                    stand(sp)
                    expert_weights(sp, g + 1, p, (0, 1))

        def moe_tensor(pe, layer):
            r, run = front_run(layer), earlier(layer)
            pe.wait_ge(constants, 14)
            pe.matmul(psum[:, 2, 0:NE], ones[0:1, :], zeros[0:1, 0:NE], start=True, stop=True, skip_group_check=True)
            def count(i):
                pe.wait_ge(e_mask.sem, e_mask.at(run, i))
                for j in range(TPI):
                    mm = pe.matmul(psum[:, 2, 0:NE], onesb[:], MASK[:, bass.ds(i * TPI + j, 1), :].rearrange("p a e -> p (a e)"),
                                   start=False, stop=True, skip_group_check=True)
                mm.then_inc(e_cnt.sem, 1)

            def route(i, first, last):
                pe.wait_ge(f_xt.sem, f_xt.at(r, i))
                pe.wait_ge(e_logit.sem, e_logit.before(run, i))
                for j in range(TPI):
                    o = psum[:, 6 + j // 2, NE * (j % 2):NE * (j % 2) + NE]
                    mm = pe.matmul(o, XT[:, P * j:P * j + P], router_t[:], start=True, stop=True, skip_group_check=True)
                mm.then_inc(e_lg.sem, 1)
                pe.wait_ge(e_he.sem, e_he.before(run, i))
                for j in range(TPI):
                    mm = pe.matmul(psum[:, 1, INTER * j:INTER * j + INTER], XT[:, P * j:P * j + P], sh_gate[:], start=True, stop=True, skip_group_check=True)
                mm.then_inc(e_h.sem, 1)
                if not first:
                    count(i - 1)
                if not last:
                    front_tensor(pe, i + 1, r)
                pe.wait_ge(e_he.sem, e_he.at(run, i))
                pe.wait_ge(e_ht.sem, e_ht.before(run, i))
                stand(pe)
                for j in range(TPI):
                    mm = pe.transpose(psum[0:INTER, 3, P * j:P * j + P], HE[:, INTER * j:INTER * j + INTER], ident[:])
                mm.then_inc(e_tr.sem, 1)
                pe.wait_ge(e_ht.sem, e_ht.at(run, i))
                pe.wait_ge(e_x.sem, e_x.before(run, i))
                for j in range(TPI):
                    mm = pe.matmul(psum[:, 5, P * j:P * j + P], HT[:, P * j:P * j + P], sh_down[:], start=True, stop=True, skip_group_check=True)
                mm.then_inc(e_y.sem, 1)

            front_tensor(pe, 0, r)
            route(0, True, False)
            with pe.Fori(1, STEPS - 1) as i:
                route(i, False, False)
            route(STEPS - 1, False, True)
            count(STEPS - 1)

            pe.wait_ge(o_link.sem, o_link.at(run, 0))
            pe.matmul(psum[:, 2, 0:NE], ident[:], FIRST, start=True, stop=True, skip_group_check=True)
            pe.wait_ge(constants, 14)
            for q in range(GROUP):
                mm = pe.matmul(psum[0:1, 4, P * q:P * q + P], EXPERT_COL[:, q:q + 1], ident[:], start=True, stop=True, skip_group_check=True)
            mm.then_inc(o_row.sem, 1)
            with pe.Fori(0, STEPS) as i:
                for j in range(TPI):
                    m = MASK[:, bass.ds(i * TPI + j, 1), :].rearrange("p a e -> p (a e)")
                    pe.matmul(psum[:, 2, 0:NE], earlier_tokens[:], m, start=False, stop=True, skip_group_check=True).then_inc(s_a.sem, 1)
                    pe.wait_ge(s_slotm.sem, s_slotm.at(run, i, j + 1))
                    pe.matmul(psum[:, 2, 0:NE], other_tokens[:], m, start=False, stop=True, skip_group_check=True)

            def transposes(g, p):
                pe.wait_ge(c_ld[p].sem, c_ld[p].at(run, g))
                pe.wait_ge(c_xt.sem, c_xt.at(run, g, p - 1))
                for q in range(GROUP):
                    mm = pe.transpose(psum[:, p % 2, P * q:P * q + P], XSB[:, p, q], ident[:])
                mm.then_inc(c_tr.sem, 1)

            def hidden(g, p):
                for h in range(3):
                    pe.wait_ge(c_ew[h][p].sem, c_ew[h][p].at(run, g))
                pe.wait_ge(c_xt.sem, c_xt.at(run, g, p + 1))
                pe.wait_ge(c_he.sem, c_he.at(run, g, p - 1))
                for q in range(GROUP):
                    o = 256 * (p % 2) + INTER * q
                    mm = pe.matmul(psum[:, 2, o:o + INTER], XSBT[:, p, P * q:P * q + P], EWB[:, p, q, 0:INTER], start=True, stop=True, skip_group_check=True)
                mm.then_inc(c_h.sem, 1)

            def hidden_transposes(g, p):
                pe.wait_ge(c_he.sem, c_he.at(run, g, p + 1))
                pe.wait_ge(c_ht.sem, c_ht.at(run, g, p - 1))
                stand(pe)
                for q in range(GROUP):
                    mm = pe.transpose(psum[0:INTER, 3 + p % 2, P * q:P * q + P], HEB[:, p % 2, INTER * q:INTER * q + INTER], ident[:])
                mm.then_inc(c_htr.sem, 1)

            def results(g, p):
                pe.wait_ge(c_ht.sem, c_ht.at(run, g, p + 1))
                pe.wait_ge(c_ysb.sem, c_ysb.at(run, g, p - 1))
                for q in range(GROUP):
                    mm = pe.matmul(psum[:, 5 + p % 2, P * q:P * q + P], HTB[:, p % 2, P * q:P * q + P],
                                   EWB[0:INTER, p, q, INTER:EW], start=True, stop=True, skip_group_check=True)
                mm.then_inc(c_y.sem, 1)

            transposes(0, 0)
            transposes(0, 1)
            hidden(0, 0)
            with pe.Fori(0, GSTEPS - 1) as g:
                for p in range(UNROLL):
                    transposes(g + (p + 2) // UNROLL, (p + 2) % UNROLL)
                    hidden_transposes(g, p)
                    hidden(g + (p + 1) // UNROLL, (p + 1) % UNROLL)
                    results(g, p)
            for p in range(UNROLL):
                if p < UNROLL - 2:
                    transposes(GSTEPS - 1, p + 2)
                hidden_transposes(GSTEPS - 1, p)
                if p < UNROLL - 1:
                    hidden(GSTEPS - 1, p + 1)
                results(GSTEPS - 1, p)

        ENGINES = 4

        def begin(eng):
            eng.wait_ge(primed, 1)
            eng.wait_ge(loaded, 16 * (FIRST_WEIGHTS + 1))

        def barriers(layers):
            return sum(k != "moe" for k in LAYERS[:layers])

        def finish(eng, layer):
            eng.drain().then_inc(phase_done, 1)
            if layer == 0:
                eng.wait_ge(loaded_all, 16 * (len(weights) - FIRST_WEIGHTS))
            eng.wait_ge(phase_done, ENGINES * barriers(layer + 1))

        block = ctx.enter_context(nc.Block())

        @block.sync
        def _(sp):
            for s in signals:
                if s.start:
                    sp.sem_inc(s.sem, s.start)
            sp.sem_inc(primed, 1)
            for t, src in weights[:FIRST_WEIGHTS]:
                sp.dma_start(t[:], src).then_inc(loaded, 16)
            for t, src in weights[FIRST_WEIGHTS:]:
                sp.dma_start(t[:], src).then_inc(loaded_all, 16)
            sp.wait_ge(constants, 14)
            sp.dma_start(slot_rows.rearrange("(p r) d -> p (r d)", p=P).rearrange("p (n z) -> p n z", z=512),
                         zeros[:].unsqueeze(1).broadcast_to([P, SLOT_TILES * D // 512, 512])).then_inc(cleared, 16)
            moe_sync(sp, 1)
            moe_sync(sp, 3)
            mamba_sync(sp, 4)
            sp.wait_ge(phase_done, ENGINES * barriers(len(LAYERS)))
            sp.dma_start(a["out"].rearrange("(t p) d -> p t d", p=P), X[:]).then_inc(stored, 16)
            sp.wait_ge(stored, 16)

        @block.vector
        def _(dve):
            begin(dve)
            cos_vector(dve, 0)
            finish(dve, 0)
            moe_vector(dve, 1)
            glru_vector(dve, 2)
            finish(dve, 2)
            moe_vector(dve, 3)
            mamba_vector(dve, 4)
            finish(dve, 4)
            ffn_vector(dve, 5)
            finish(dve, 5)
            rope_vector(dve, 6)
            finish(dve, 6)
            ffn_vector(dve, 7)
            finish(dve, 7)

        @block.scalar
        def _(act):
            act.dma_start(X[:], a["x"].rearrange("(t p) d -> p t d", p=P)).then_inc(loaded, 16)
            begin(act)
            cos_scalar(act, 0)
            finish(act, 0)
            moe_scalar(act, 1)
            glru_scalar(act, 2)
            finish(act, 2)
            moe_scalar(act, 3)
            mamba_scalar(act, 4)
            finish(act, 4)
            ffn_scalar(act, 5)
            finish(act, 5)
            rope_scalar(act, 6)
            finish(act, 6)
            ffn_scalar(act, 7)
            finish(act, 7)

        @block.gpsimd
        def _(pool):
            pool.memset(ones4[:], 0.0).then_inc(constants, 1)
            pool.memset(tiny[:], 1e-12).then_inc(constants, 1)
            pool.wait_ge(constants, 1)
            for n in range(4):
                pool.memset(ones4[:, n, DH * n:DH * n + DH], 1.0).then_inc(constants, 1)
            pool.memset(minus_half[:], -0.5).then_inc(constants, 1)
            pool.memset(rms_eps[:], RMS_EPS).then_inc(constants, 1)
            pool.memset(ln_eps[:], EPS).then_inc(constants, 1)
            pool.memset(both_eps[:], EPS * RMS_EPS).then_inc(constants, 1)
            pool.memset(ones[:], 1.0).then_inc(constants, 1)
            pool.memset(onesb[:], 1.0).then_inc(constants, 1)
            pool.memset(zeros[:], 0.0).then_inc(constants, 1)
            pool.memset(ones_row[:], 1.0).then_inc(constants, 1)
            begin(pool)
            cos_gpsimd(pool, 0)
            finish(pool, 0)
            moe_gpsimd(pool, 1)
            glru_gpsimd(pool, 2)
            finish(pool, 2)
            moe_gpsimd(pool, 3)
            mamba_gpsimd(pool, 4)
            finish(pool, 4)
            ffn_gpsimd(pool, 5)
            finish(pool, 5)
            rope_gpsimd(pool, 6)
            finish(pool, 6)
            ffn_gpsimd(pool, 7)
            finish(pool, 7)

        @block.tensor
        def _(pe):
            begin(pe)
            cos_tensor(pe, 0)
            finish(pe, 0)
            moe_tensor(pe, 1)
            glru_tensor(pe, 2)
            finish(pe, 2)
            moe_tensor(pe, 3)
            mamba_tensor(pe, 4)
            finish(pe, 4)
            ffn_tensor(pe, 5)
            finish(pe, 5)
            rope_tensor(pe, 6)
            finish(pe, 6)
            ffn_tensor(pe, 7)
            finish(pe, 7)


def layout(inputs):
    import numpy as np

    contiguous = np.ascontiguousarray

    def of(layer):
        return lambda name: np.asarray(inputs[layer + "_" + name])

    out = {}
    w = of("L0_attn_a")
    out["x"] = w("x").reshape(TOK, D)
    out["w_qkv"] = w("w_qkv")
    out["ln_w"], out["ln_b"] = w("ln_w").reshape(D, 1), w("ln_b").reshape(D, 1)
    inner = w("w_out").shape[0]
    w_out = np.zeros((P, 2, D), np.float32)
    w_out[:inner, 0] = w_out[inner:, 1] = w("w_out")
    out["w_out"] = w_out
    w = of("L0_attn_b")
    for name, source in (("wg_t", "Wg"), ("wc_t", "Wc"), ("w1_t", "w1"), ("w2_t", "w2"), ("w3_t", "w3")):
        out[name] = contiguous(w(source).T)
    out["rms_w"], out["ffn_w"] = w("ln_w").reshape(D, 1), w("ffn_w").reshape(D, 1)
    w = of("L0_ffn")
    experts, width = w("w_gate").shape[:2]
    out["router_t"] = contiguous(w("router_w").T)
    out["e_bias"] = contiguous(np.broadcast_to(w("expert_bias").reshape(1, experts), (P, experts)))
    out["sh_gate"], out["sh_down"] = contiguous(w("w_gate_shared").T), contiguous(w("w_down_shared").T)
    expert_w = np.zeros((experts, D, width + D), np.float32)
    expert_w[:, :, :width] = w("w_gate").transpose(0, 2, 1)
    expert_w[:, :width, width:] = w("w_down").transpose(0, 2, 1)
    out["expert_w"] = expert_w.reshape(experts * D, width + D)
    earlier = (np.arange(P)[:, None] < np.arange(P)[None, :])
    out["earlier_tokens"] = earlier.astype(mybir.dt.np(BF16))
    out["other_tokens"] = (~earlier).astype(mybir.dt.np(BF16))
    out["slot_tile"] = np.arange(P * 4, dtype=np.float32).reshape(P, 4)
    w = of("L1_attn_a")
    out["w_in"] = w("W_in").reshape(D, 4, P)
    out["b_in"] = contiguous(w("b_in").reshape(4, P).T)
    out["conv_w"] = contiguous(w("conv_w").reshape(2, P, -1).transpose(1, 0, 2))
    out["conv_b"] = contiguous(w("conv_b").reshape(2, P).T)
    out["m_a"] = contiguous(w("A").reshape(2, P, -1).transpose(1, 0, 2))
    out["m_ct"] = contiguous(w("C").T.reshape(-1, 2, P))
    out["m_d"] = contiguous(w("Dp").reshape(2, P).T)
    out["m_wo"] = contiguous(w("W_out").reshape(2, P, D).transpose(1, 0, 2))
    out["m_bo"] = contiguous(np.broadcast_to(w("b_out").reshape(1, D), (P, D)))
    w = of("L1_ffn")
    for name, source in (("wr_t", "W_r"), ("wk_t", "W_k"), ("wv_t", "W_v")):
        out[name] = contiguous(w(source).T)
    out["mu"] = np.stack([w("mu_r"), w("mu_k")], 1)
    w = of("L1_attn_b")
    order = np.concatenate([np.arange(0, DH, 2), np.arange(1, DH, 2)])
    rows = (np.arange(D // DH)[:, None] * DH + order[None]).reshape(-1)
    out["w_qkvt"] = contiguous(np.concatenate([w("wq")[rows], w("wk")[rows], w("wv")], 0).T)
    out["w_ot"] = contiguous(w("wo").T)
    powers = np.arange(0, DH, 2, dtype=np.float32) / np.float32(DH)
    angles = np.outer(np.arange(SEQ, dtype=np.float32), 1.0 / np.float32(10000.0) ** powers).astype(np.float32)
    tiles = lambda t: np.concatenate([t.reshape(2, P, -1).transpose(1, 0, 2)] * (TPI // 2), 1)
    out["cos"] = contiguous(tiles(np.cos(angles)))
    out["sin"] = contiguous(np.stack([-tiles(np.sin(angles)), tiles(np.sin(angles))], 1))
    out["ident"] = np.eye(P, dtype=np.float32)
    out["identb"] = np.eye(P, dtype=mybir.dt.np(BF16))
    later = np.arange(P)[:, None] > np.arange(P)[None, :]
    out["mask_kq"] = np.where(later, NEG, 0.0).astype(mybir.dt.np(BF16))
    out["mask_qk"] = np.where(later.T, NEG, 0.0).astype(mybir.dt.np(BF16))
    return out


def kernel(**inputs):
    import numpy as np
    import concourse.bacc as bacc
    from concourse.bass_utils import run_bass_kernel_spmd

    nc = bacc.Bacc("TRN2", target_bir_lowering=False, num_devices=1)
    arrays, a = {}, {}
    for name, array in layout(inputs).items():
        arrays[f"in_{name}"] = array
        a[name] = nc.dram_tensor(f"in_{name}", array.shape, mybir.dt.from_np(array.dtype), kind="ExternalInput").ap()
    a["out"] = nc.dram_tensor("out", (TOK, D), F32, kind="ExternalOutput").ap()
    program(nc, a)
    r = run_bass_kernel_spmd(nc, [arrays], core_ids=[0])
    return np.asarray(r.results[0]["out"]).reshape(NSEQ, SEQ, D)
```
